# Optimizing a Trainium2 kernel written in Bass

```python
import numpy as np
import jax
import jax.numpy as jnp

def _softmax(x, axis=-1):
    return jax.nn.softmax(x, axis=axis)
def _gelu(x):
    return jax.nn.gelu(x, approximate=True)
def _silu(x):
    return jax.nn.silu(x)
def _sigmoid(x):
    return jax.nn.sigmoid(x)
def _layernorm(x, axis=-1, eps=1e-5):
    m = jnp.mean(x, axis=axis, keepdims=True)
    v = jnp.var(x, axis=axis, keepdims=True)
    return (x - m) / jnp.sqrt(v + eps)
def _scatter_add(tgt, idx, src, axis=0):
    return tgt.at[idx].add(src)
def _segment_sum(src, seg, n):
    return jax.ops.segment_sum(src, seg, n)

kernel_name = 'mk_conv_preact_d2_conv_nhwc128_4fff38'

def setup_inputs(seed: int = 0):
    np.random.seed(seed)
    _w = jnp.asarray
    def _rec_inputs():
        import jax
        import jax.numpy as jnp
        _gk = jax.random.key(seed)
        x = -0.0002928 + 1 * jax.random.normal(jax.random.fold_in(_gk, 1), (2, 128, 128, 128), jnp.float32)
        return x
    x = _rec_inputs()
    def _L0_conv_setup():
        import jax, jax.numpy as jnp
        import numpy as np
        N_HEAD = 8
        TOKEN_CODIM = 4
        TEMP = 1.0
        EPS = 1e-05

        def instance_norm(x, w=None, b=None):
            mu = jnp.mean(x, axis=(-2, -1), keepdims=True)
            var = jnp.var(x, axis=(-2, -1), keepdims=True)
            y = (x - mu) * jax.lax.rsqrt(var + EPS)
            if w is not None:
                y = y * w[:, None, None] + b[:, None, None]
            return y

        def spectral_conv(x, wr, wi, bias, out_hw):
            B, Cin, H, W = x.shape
            Ho, Wo = out_hw
            w = wr + 1j * wi
            m1, m2 = (wr.shape[2], wr.shape[3])
            h = m1 // 2
            xf = jnp.fft.rfft2(x, norm='forward')
            top = jnp.einsum('bixy,ioxy->boxy', xf[:, :, :h, :m2], w[:, :, :h])
            bot = jnp.einsum('bixy,ioxy->boxy', xf[:, :, H - h:, :m2], w[:, :, h:])
            of = jnp.zeros((B, wr.shape[1], Ho, Wo // 2 + 1), dtype=xf.dtype)
            of = of.at[:, :, :h, :m2].set(top)
            of = of.at[:, :, Ho - h:, :m2].set(bot)
            return jnp.fft.irfft2(of, s=(Ho, Wo), norm='forward') + bias[:, None, None]

        def fft_resample(x, Ho, Wo):
            B, C, H, W = x.shape
            xf = jnp.fft.rfft2(x, norm='forward')
            h, wc = (Ho // 2, Wo // 2 + 1)
            of = jnp.zeros((B, C, Ho, wc), dtype=xf.dtype)
            of = of.at[:, :, :h].set(xf[:, :, :h, :wc])
            of = of.at[:, :, Ho - h:].set(xf[:, :, H - h:, :wc])
            return jnp.fft.irfft2(of, s=(Ho, Wo), norm='forward')

        def fno_layer(x, wr, wi, bias, sw, sb, out_hw, norm=False, act=False):
            skip = jnp.einsum('bihw,oi->bohw', x, sw) + sb[:, None, None]
            if out_hw != tuple(x.shape[-2:]):
                skip = fft_resample(skip, *out_hw)
            xf = spectral_conv(x, wr, wi, bias, out_hw)
            if norm:
                xf = instance_norm(xf)
            y = xf + skip
            return jax.nn.gelu(y, approximate=False) if act else y

        def to_heads(z, b):
            bt, ad, h, w = z.shape
            t = bt // b
            z = z.reshape(b, t, N_HEAD, ad // N_HEAD, h, w)
            return jnp.transpose(z, (0, 2, 1, 3, 4, 5)).reshape(b, N_HEAD, t, -1)
        key = jax.random.key(seed)
        ks = jax.random.split(key, 12)
        b, C, H, W = (2, 128, 128, 128)
        f = jax.random.normal
        return dict(x=f(ks[0], (b, C, H, W), jnp.float32), norm1_w=jnp.ones((1,)), norm1_b=jnp.zeros((1,)), kqv_wr=f(ks[1], (3, 1, N_HEAD, 16, 8)) * 0.02, kqv_wi=f(ks[2], (3, 1, N_HEAD, 16, 8)) * 0.02, kqv_bias=f(ks[3], (3, N_HEAD)) * 0.02, kqv_sw=f(ks[4], (3, N_HEAD, 1)) * 0.5, kqv_sb=jnp.zeros((3, N_HEAD)), p_wr=f(ks[5], (N_HEAD, 1, 32, 16)) * 0.02, p_wi=f(ks[6], (N_HEAD, 1, 32, 16)) * 0.02, p_bias=jnp.zeros((1,)), p_sw=f(ks[7], (1, N_HEAD)) * (1.0 / np.sqrt(N_HEAD)), p_sb=jnp.zeros((1,)), attn_norm_w=jnp.ones((1,)), attn_norm_b=jnp.zeros((1,)), norm2_w=jnp.ones((TOKEN_CODIM,)), norm2_b=jnp.zeros((TOKEN_CODIM,)), mix_wr=f(ks[8], (2, TOKEN_CODIM, TOKEN_CODIM, 32, 16)) * 0.02, mix_wi=f(ks[9], (2, TOKEN_CODIM, TOKEN_CODIM, 32, 16)) * 0.02, mix_bias=jnp.zeros((2, TOKEN_CODIM)), mix_sw=f(ks[10], (2, TOKEN_CODIM, TOKEN_CODIM)) * 0.5, mix_sb=jnp.zeros((2, TOKEN_CODIM)), mon_w=jnp.ones((TOKEN_CODIM,)), mon_b=jnp.zeros((TOKEN_CODIM,)))
    _L0_conv_all = _L0_conv_setup()
    _L0_conv_in = {k: v for k, v in _L0_conv_all.items() if k in ('norm1_w', 'norm1_b', 'kqv_wr', 'kqv_wi', 'kqv_bias', 'kqv_sw', 'kqv_sb', 'p_wr', 'p_wi', 'p_bias', 'p_sw', 'p_sb', 'attn_norm_w', 'attn_norm_b', 'norm2_w', 'norm2_b', 'mix_wr', 'mix_wi', 'mix_bias', 'mix_sw', 'mix_sb', 'mon_w', 'mon_b', )}
    del _L0_conv_all

    def _L1_conv_setup():
        import jax, jax.numpy as jnp
        import numpy as np
        EPS = 1e-05

        def _ln(x, g, b):
            m = jnp.mean(x, axis=-1, keepdims=True)
            v = jnp.var(x, axis=-1, keepdims=True)
            return (x - m) / jnp.sqrt(v + EPS) * g + b
        key = jax.random.key(seed)
        ks = jax.random.split(key, 16)
        B, N, CZ, C = (1, 512, 128, 16)
        s_cz = 1.0 / np.sqrt(CZ)
        s_c = 1.0 / np.sqrt(C)

        def lin(k, fan_in, shape):
            return jax.random.uniform(k, shape, jnp.float32, -1.0, 1.0) / np.sqrt(fan_in)
        return {'x': jax.random.normal(ks[0], (B, N, N, CZ), jnp.float32), 'Wa1': lin(ks[1], CZ, (CZ, C)), 'ba1': lin(ks[2], CZ, (C,)), 'Wa2': lin(ks[3], CZ, (CZ, C)), 'ba2': lin(ks[4], CZ, (C,)), 'Wb1': lin(ks[5], CZ, (CZ, C)), 'bb1': lin(ks[6], CZ, (C,)), 'Wb2': lin(ks[7], CZ, (CZ, C)), 'bb2': lin(ks[8], CZ, (C,)), 'ln2_g': jnp.ones((C,), jnp.float32), 'ln2_b': jnp.zeros((C,), jnp.float32), 'Wg': lin(ks[9], CZ, (CZ, CZ)), 'bg': lin(ks[10], CZ, (CZ,)), 'Wz': lin(ks[11], C, (C, CZ)), 'bz': lin(ks[12], C, (CZ,))}
    _L1_conv_all = _L1_conv_setup()
    _L1_conv_in = {k: v for k, v in _L1_conv_all.items() if k in ('Wa1', 'ba1', 'Wa2', 'ba2', 'Wb1', 'bb1', 'Wb2', 'bb2', 'ln2_g', 'ln2_b', 'Wg', 'bg', 'Wz', 'bz', )}
    del _L1_conv_all

    return {
        "x": x,
        "L0_conv_norm1_w": _L0_conv_in["norm1_w"],
        "L0_conv_norm1_b": _L0_conv_in["norm1_b"],
        "L0_conv_kqv_wr": _L0_conv_in["kqv_wr"],
        "L0_conv_kqv_wi": _L0_conv_in["kqv_wi"],
        "L0_conv_kqv_bias": _L0_conv_in["kqv_bias"],
        "L0_conv_kqv_sw": _L0_conv_in["kqv_sw"],
        "L0_conv_kqv_sb": _L0_conv_in["kqv_sb"],
        "L0_conv_p_wr": _L0_conv_in["p_wr"],
        "L0_conv_p_wi": _L0_conv_in["p_wi"],
        "L0_conv_p_bias": _L0_conv_in["p_bias"],
        "L0_conv_p_sw": _L0_conv_in["p_sw"],
        "L0_conv_p_sb": _L0_conv_in["p_sb"],
        "L0_conv_attn_norm_w": _L0_conv_in["attn_norm_w"],
        "L0_conv_attn_norm_b": _L0_conv_in["attn_norm_b"],
        "L0_conv_norm2_w": _L0_conv_in["norm2_w"],
        "L0_conv_norm2_b": _L0_conv_in["norm2_b"],
        "L0_conv_mix_wr": _L0_conv_in["mix_wr"],
        "L0_conv_mix_wi": _L0_conv_in["mix_wi"],
        "L0_conv_mix_bias": _L0_conv_in["mix_bias"],
        "L0_conv_mix_sw": _L0_conv_in["mix_sw"],
        "L0_conv_mix_sb": _L0_conv_in["mix_sb"],
        "L0_conv_mon_w": _L0_conv_in["mon_w"],
        "L0_conv_mon_b": _L0_conv_in["mon_b"],
        "L1_conv_Wa1": _L1_conv_in["Wa1"],
        "L1_conv_ba1": _L1_conv_in["ba1"],
        "L1_conv_Wa2": _L1_conv_in["Wa2"],
        "L1_conv_ba2": _L1_conv_in["ba2"],
        "L1_conv_Wb1": _L1_conv_in["Wb1"],
        "L1_conv_bb1": _L1_conv_in["bb1"],
        "L1_conv_Wb2": _L1_conv_in["Wb2"],
        "L1_conv_bb2": _L1_conv_in["bb2"],
        "L1_conv_ln2_g": _L1_conv_in["ln2_g"],
        "L1_conv_ln2_b": _L1_conv_in["ln2_b"],
        "L1_conv_Wg": _L1_conv_in["Wg"],
        "L1_conv_bg": _L1_conv_in["bg"],
        "L1_conv_Wz": _L1_conv_in["Wz"],
        "L1_conv_bz": _L1_conv_in["bz"],
    }

def reference(x, L0_conv_norm1_w, L0_conv_norm1_b, L0_conv_kqv_wr, L0_conv_kqv_wi, L0_conv_kqv_bias, L0_conv_kqv_sw, L0_conv_kqv_sb, L0_conv_p_wr, L0_conv_p_wi, L0_conv_p_bias, L0_conv_p_sw, L0_conv_p_sb, L0_conv_attn_norm_w, L0_conv_attn_norm_b, L0_conv_norm2_w, L0_conv_norm2_b, L0_conv_mix_wr, L0_conv_mix_wi, L0_conv_mix_bias, L0_conv_mix_sw, L0_conv_mix_sb, L0_conv_mon_w, L0_conv_mon_b, L1_conv_Wa1, L1_conv_ba1, L1_conv_Wa2, L1_conv_ba2, L1_conv_Wb1, L1_conv_bb1, L1_conv_Wb2, L1_conv_bb2, L1_conv_ln2_g, L1_conv_ln2_b, L1_conv_Wg, L1_conv_bg, L1_conv_Wz, L1_conv_bz):
    import jax
    import jax.numpy as jnp
    def _L0_conv_ref(x, norm1_w, norm1_b, kqv_wr, kqv_wi, kqv_bias, kqv_sw, kqv_sb, p_wr, p_wi, p_bias, p_sw, p_sb, attn_norm_w, attn_norm_b, norm2_w, norm2_b, mix_wr, mix_wi, mix_bias, mix_sw, mix_sb, mon_w, mon_b):
        import jax, jax.numpy as jnp
        import numpy as np
        N_HEAD = 8
        TOKEN_CODIM = 4
        TEMP = 1.0
        EPS = 1e-05

        def instance_norm(x, w=None, b=None):
            mu = jnp.mean(x, axis=(-2, -1), keepdims=True)
            var = jnp.var(x, axis=(-2, -1), keepdims=True)
            y = (x - mu) * jax.lax.rsqrt(var + EPS)
            if w is not None:
                y = y * w[:, None, None] + b[:, None, None]
            return y

        def spectral_conv(x, wr, wi, bias, out_hw):
            B, Cin, H, W = x.shape
            Ho, Wo = out_hw
            w = wr + 1j * wi
            m1, m2 = (wr.shape[2], wr.shape[3])
            h = m1 // 2
            xf = jnp.fft.rfft2(x, norm='forward')
            top = jnp.einsum('bixy,ioxy->boxy', xf[:, :, :h, :m2], w[:, :, :h])
            bot = jnp.einsum('bixy,ioxy->boxy', xf[:, :, H - h:, :m2], w[:, :, h:])
            of = jnp.zeros((B, wr.shape[1], Ho, Wo // 2 + 1), dtype=xf.dtype)
            of = of.at[:, :, :h, :m2].set(top)
            of = of.at[:, :, Ho - h:, :m2].set(bot)
            return jnp.fft.irfft2(of, s=(Ho, Wo), norm='forward') + bias[:, None, None]

        def fft_resample(x, Ho, Wo):
            B, C, H, W = x.shape
            xf = jnp.fft.rfft2(x, norm='forward')
            h, wc = (Ho // 2, Wo // 2 + 1)
            of = jnp.zeros((B, C, Ho, wc), dtype=xf.dtype)
            of = of.at[:, :, :h].set(xf[:, :, :h, :wc])
            of = of.at[:, :, Ho - h:].set(xf[:, :, H - h:, :wc])
            return jnp.fft.irfft2(of, s=(Ho, Wo), norm='forward')

        def fno_layer(x, wr, wi, bias, sw, sb, out_hw, norm=False, act=False):
            skip = jnp.einsum('bihw,oi->bohw', x, sw) + sb[:, None, None]
            if out_hw != tuple(x.shape[-2:]):
                skip = fft_resample(skip, *out_hw)
            xf = spectral_conv(x, wr, wi, bias, out_hw)
            if norm:
                xf = instance_norm(xf)
            y = xf + skip
            return jax.nn.gelu(y, approximate=False) if act else y

        def to_heads(z, b):
            bt, ad, h, w = z.shape
            t = bt // b
            z = z.reshape(b, t, N_HEAD, ad // N_HEAD, h, w)
            return jnp.transpose(z, (0, 2, 1, 3, 4, 5)).reshape(b, N_HEAD, t, -1)
        b, C, H, W = x.shape
        tokens = x.reshape(b * C, 1, H, W)
        tok_n = instance_norm(tokens, norm1_w, norm1_b)
        k = fno_layer(tok_n, kqv_wr[0], kqv_wi[0], kqv_bias[0], kqv_sw[0], kqv_sb[0], (H // 2, W // 2))
        q = fno_layer(tok_n, kqv_wr[1], kqv_wi[1], kqv_bias[1], kqv_sw[1], kqv_sb[1], (H // 2, W // 2))
        v = fno_layer(tok_n, kqv_wr[2], kqv_wi[2], kqv_bias[2], kqv_sw[2], kqv_sb[2], (H, W))
        kh, qh, vh = (to_heads(k, b), to_heads(q, b), to_heads(v, b))
        scores = jnp.einsum('bati,basi->bats', qh, kh) / (np.float32(np.sqrt(kh.shape[-1])) * TEMP)
        probs = jax.nn.softmax(scores, axis=-1)
        attn = jnp.einsum('bats,basi->bati', probs, vh)
        attn = attn.reshape(b, N_HEAD, C, 1, H, W).transpose(0, 2, 1, 3, 4, 5).reshape(b * C, N_HEAD, H, W)
        attn = fno_layer(attn, p_wr, p_wi, p_bias, p_sw, p_sb, (H, W))
        attn = instance_norm(attn + tokens, attn_norm_w, attn_norm_b)
        attn = attn.reshape(b * (C // TOKEN_CODIM), TOKEN_CODIM, H, W)
        h0 = instance_norm(attn, norm2_w, norm2_b)
        h1 = fno_layer(h0, mix_wr[0], mix_wi[0], mix_bias[0], mix_sw[0], mix_sb[0], (H, W), norm=True, act=True)
        h2 = fno_layer(h1, mix_wr[1], mix_wi[1], mix_bias[1], mix_sw[1], mix_sb[1], (H, W), norm=True)
        out = instance_norm(h2, mon_w, mon_b) + attn
        return out.reshape(b, C, H, W)

    def _L1_conv_ref(x, Wa1, ba1, Wa2, ba2, Wb1, bb1, Wb2, bb2, ln2_g, ln2_b, Wg, bg, Wz, bz):
        import jax, jax.numpy as jnp
        import numpy as np
        EPS = 1e-05

        def _ln(x, g, b):
            m = jnp.mean(x, axis=-1, keepdims=True)
            v = jnp.var(x, axis=-1, keepdims=True)
            return (x - m) / jnp.sqrt(v + EPS) * g + b
        direction = 'outgoing'
        a = jax.nn.sigmoid((x @ Wa1 + ba1) * (x @ Wa2 + ba2))
        b = jax.nn.sigmoid((x @ Wb1 + bb1) * (x @ Wb2 + bb2))
        if direction == 'incoming':
            a = jnp.swapaxes(a, 1, 2)
            b = jnp.swapaxes(b, 1, 2)
        g = jax.nn.sigmoid(x @ Wg + bg)
        z = jnp.einsum('bikc,bkjc->bijc', a, b)
        return g * (_ln(z, ln2_g, ln2_b) @ Wz + bz)

    def _gn(v, G=32, eps=1e-5):
        B_, H_, W_, C_ = v.shape
        g = v.reshape(B_, H_, W_, G, C_ // G)
        m = jnp.mean(g, axis=(1, 2, 4), keepdims=True)
        s = jnp.var(g, axis=(1, 2, 4), keepdims=True)
        return ((g - m) / jnp.sqrt(s + eps)).reshape(v.shape)

    def _ln_c(v, eps=1e-6):
        m = jnp.mean(v, axis=-1, keepdims=True)
        s = jnp.var(v, axis=-1, keepdims=True)
        return (v - m) / jnp.sqrt(s + eps)

    def _ln_t(v, eps=1e-5):
        m = jnp.mean(v, axis=-1, keepdims=True)
        s = jnp.var(v, axis=-1, keepdims=True)
        return (v - m) / jnp.sqrt(s + eps)

    def _to_tokens(v):
        B_, H_, W_, C_ = v.shape
        return v.reshape(B_, H_ * W_, C_)
    def _from_tokens(t, like):
        return t.reshape(like.shape)

    x = x + _L0_conv_ref(_gn(x), L0_conv_norm1_w, L0_conv_norm1_b, L0_conv_kqv_wr, L0_conv_kqv_wi, L0_conv_kqv_bias, L0_conv_kqv_sw, L0_conv_kqv_sb, L0_conv_p_wr, L0_conv_p_wi, L0_conv_p_bias, L0_conv_p_sw, L0_conv_p_sb, L0_conv_attn_norm_w, L0_conv_attn_norm_b, L0_conv_norm2_w, L0_conv_norm2_b, L0_conv_mix_wr, L0_conv_mix_wi, L0_conv_mix_bias, L0_conv_mix_sw, L0_conv_mix_sb, L0_conv_mon_w, L0_conv_mon_b)
    x = x + _L1_conv_ref(_gn(x), L1_conv_Wa1, L1_conv_ba1, L1_conv_Wa2, L1_conv_ba2, L1_conv_Wb1, L1_conv_bb1, L1_conv_Wb2, L1_conv_bb2, L1_conv_ln2_g, L1_conv_ln2_b, L1_conv_Wg, L1_conv_bg, L1_conv_Wz, L1_conv_bz)
    return x


_drawn_inputs = setup_inputs


def setup_inputs(seed=0):
    import zlib

    import numpy as np

    out = dict(_drawn_inputs(seed))
    spreads = {'L0_conv_kqv_sb': (0.0, 0.8),
     'L0_conv_norm2_w': (1.0, 0.2),
     'L0_conv_norm2_b': (0.0, 0.364),
     'L0_conv_mix_bias': (0.0, 0.8),
     'L0_conv_mix_sb': (0.0, 0.285),
     'L0_conv_mon_w': (1.0, 0.2),
     'L0_conv_mon_b': (0.0, 0.301),
     'L1_conv_ln2_g': (1.0, 0.6),
     'L1_conv_ln2_b': (0.0, 0.588)}
    factors = {'L0_conv_kqv_wr': 8.0,
     'L0_conv_kqv_wi': 8.0,
     'L0_conv_kqv_bias': 8.0,
     'L0_conv_kqv_sw': 6.365,
     'L0_conv_p_wr': 8.0,
     'L0_conv_p_wi': 8.0,
     'L0_conv_p_sw': 3.251,
     'L1_conv_ba1': 4.774,
     'L1_conv_ba2': 5.481,
     'L1_conv_bb1': 5.801,
     'L1_conv_bb2': 7.492,
     'L1_conv_bg': 8.0}
    for name, (base, spread) in spreads.items():
        noise = np.random.default_rng([zlib.crc32(name.encode()), seed]).standard_normal(out[name].shape)
        drawn = base * np.exp(spread * noise) if base else spread * noise
        out[name] = jnp.asarray(drawn.astype(out[name].dtype))
    for name, factor in factors.items():
        out[name] = (out[name] * factor).astype(out[name].dtype)
    return out
```

```python
from contextlib import ExitStack

import numpy as np

import concourse.bass as bass
from concourse import mybir

F32 = mybir.dt.float32
ALU = mybir.AluOpType
ACT = mybir.ActivationFunctionType
AX = mybir.AxisListType

BATCH = 2
N = 128
HW = N * N
HEADS = 8
KX, KY = 32, 16
CH = 8
TILE = 512
TILES = HW // TILE
C = 16
EPS = 1e-5
L0, L1 = 8.0, float(np.sqrt(128.0))
DC = L0 * L0
KX_ORDER = np.concatenate([np.arange(0, 16), -np.arange(1, 17)])

CONST_PARTS = [("fh", 65), ("fw", 128), ("inv1", 1024), ("inv2", 512), ("f2w", 32), ("f2h", 512),
               ("swap", 128), ("varw", 256), ("ident", 128), ("ones", 128), ("quad", 128), ("rho", 1)]
COL_PARTS = [("n2w", 1), ("n2b", 1), ("monw", 1), ("monb", 1), ("bz", 1), ("bg", 1), ("lng", 1),
             ("lnb", 1), ("kq", 256), ("mix", 512), ("mixrev", 64), ("skip", 256),
             ("wz", 1024), ("wg", 128), ("wab", 256), ("bab", 2)]
VEC_PARTS = [("sw", 24), ("sb", 24), ("bias", 24), ("psw", 8), ("n1w", 1), ("n1b", 1), ("pbias", 1),
             ("psb", 1), ("anw", 1), ("anb", 1), ("pdc", 8), ("mixsb", 256)]


def spans(parts):
    at, out = 0, {}
    for name, n in parts:
        out[name] = slice(at, at + n)
        at += n
    return out, at


CONST, CONST_N = spans(CONST_PARTS)
COL, COL_N = spans(COL_PARTS)
VEC, VEC_N = spans(VEC_PARTS)


def inverse_rows(za, c):
    return za[:, :].rearrange("p (h r k) -> p k r h", r=2, k=KY)[:, 2 * c:2 * c + 2]


class Units:

    def __init__(self, parts):
        self.at, self.n = {}, 0
        for name, n in parts:
            self.at[name] = self.n
            self.n += n
        assert self.n % 4 == 0, self.n

    def __call__(self, name, k=0):
        return self.at[name] + k


AU = Units([("st1", 32), ("st2", 8), ("xft", 8), ("xct", 2), ("pt", 2), ("inv0", 8), ("y", 32),
            ("swap0", 2), ("inv1", 8), ("p1", 40), ("zh", 4), ("swap1", 2), ("inv2", 8), ("p2", 32),
            ("x2t", 32), ("abx", 8), ("af", 4), ("znt", 4), ("g", 32)])
VU = Units([("sum", 1), ("sbc", 1), ("gram", 1), ("sc", 2), ("u", 2), ("fy", 2), ("inv0", 8),
            ("rows", 1), ("var0", 1), ("inv1", 8), ("h1t", 32), ("zh", 4), ("hc", 2), ("var1", 1),
            ("inv2", 8), ("gn2", 1), ("bias", 1), ("ab", 16), ("z", 4), ("fin", 64)])


def gelu_unit(g):
    return AU("p1", g + max(0, (g - 2) // 4))


def zf_unit(k):
    return AU("p1", min(4 * k + 6, 32) + k)


def aby_unit(k):
    return VU("ab", k + max(0, k - 2))


def abt_unit(k):
    return VU("ab", min(k + 2, 7) + k + 1)


def zz_unit(g):
    return VU("fin", 0 if g == 0 else 2 * g - 1)


def back_unit(g):
    return VU("fin", min(2 * g + 2, 63))


class Signal:

    def __init__(self, nc, ctx, name, per):
        self.sem, self.per = ctx.enter_context(nc.semaphore(name)), per

    def at(self, b, n):
        return b * self.per + n

    def full(self, b, unit):
        return b * self.per + unit + 1

    def free(self, b, unit):
        return b * self.per + unit + 1

    def emptied(self, b, unit):
        return b * self.per + unit + 5


def bc(ap, axis, n):
    v = ap.unsqueeze(axis)
    shape = list(v.shape)
    shape[axis] = n
    return v.to_broadcast(shape)


DVE_STEPS = 121
POOL_STEPS = 20


def build(nc, x, const, cols, vec, proj, kernels_dram, out):
    ctx = ExitStack()
    with ctx:
        def sb(name, n, parts=N):
            return ctx.enter_context(nc.sbuf_tensor(name, [parts, n], F32))

        def sig(name, per):
            return Signal(nc, ctx, name, per)

        big1, big2 = sb("big1", HW), sb("big2", HW)
        za, zb = sb("za", 4096), sb("zb", 4096)
        cst, col, vc = sb("cst", CONST_N), sb("col", COL_N), sb("vc", VEC_N)

        def K(name):
            return cst[:, CONST[name]]

        def W(name):
            return col[:, COL[name]]

        def B(name):
            return vc[:, VEC[name]]

        ident, ones = K("ident"), K("ones")
        inv1, f2h = K("inv1"), K("f2h")

        yw = big2[:, 0:8320].rearrange("p (a t) -> p a t", t=N)
        xh = [big2[:, 8320 + 1024 * s:9344 + 1024 * s].rearrange("p (t w) -> p t w", w=N) for s in range(4)]
        sq = [za[:, 0:2048], za[:, 2048:4096]]
        s1p = zb[:, 0:1024].rearrange("p (j w) -> p j w", w=N)
        s2p = zb[:, 1024:2048].rearrange("p (j w) -> p j w", w=N)

        def part(n, size=1024):
            return big2[:, 1024 * n:1024 * n + size]

        xcg, xc, xs = part(0), part(1), part(2)
        xct, xst = part(3, 512), part(4, 512)
        rh = [part(5, 512), big2[:, 5632:6144]]
        t2 = [part(6), part(7)]
        sc, prob, pt = part(8), part(9), part(10)
        wh = [part(11), part(12)]
        ul, fy = part(13), part(14)
        cri = [part(15), part(3)]
        hc, hs, acc, tmp = (za[:, 1024 * i:1024 * i + 1024] for i in range(4))
        accp, tmpp, oc, osq = (zb[:, 1024 * i:1024 * i + 1024] for i in range(4))
        abt = za[:, :].rearrange("p (n h) -> p n h", h=N)
        bf, af = za[:, 2048:4096], zb[:, 0:2048]
        firsts = [zb[:, 2048 + 512 * i:2560 + 512 * i] for i in range(2)]
        prods = [zb[:, 3072 + 512 * i:3584 + 512 * i] for i in range(2)]
        z = za[:, 0:2048].rearrange("p (c n) -> p c n", n=N)
        z2 = zb[:, 2048:4096]
        znt = za[:, 0:2048].rearrange("p (j i) -> p j i", i=N)
        ow = [za[:, 2048 + 512 * i:2560 + 512 * i] for i in range(2)]
        gt = [za[:, 3072 + 512 * i:3584 + 512 * i] for i in range(2)]
        xr = [za[:, 0:2048], za[:, 2048:4096]]

        h1w = sb("h1w", 4 * TILE)
        s12, mr_bc, root = sb("s12", 256), sb("mr_bc", 256), sb("root", 128)
        fws, gram, sbc, tq, tu = (sb(n, m) for n, m in (("fws", 128), ("gram", 128), ("sbc", 128), ("tq", 128), ("tu", 128)))
        at_, bt, dmat, m1s = (sb(n, 128) for n in ("at", "bt", "dmat", "m1s"))
        diag, crow = sb("diag", 384), sb("crow", 128)
        gs, sm = sb("gs", 128), sb("sm", 64)
        bn = sb("bn", TILES * 6)
        wabs, wgs, wzs = sb("wabs", 256), sb("wgs", 128), sb("wzs", 1024)
        mrt, mit, ccol, wsum = sb("mrt", 32), sb("mit", 32), sb("ccol", 8), sb("wsum", 8)
        pj, crt = big1[0:HEADS, 1024:3202], big1[0:HEADS, 4096:5120]

        banks_a = [ctx.enter_context(nc.psum_tensor(f"bank_a{i}", [N, TILE], F32)) for i in range(4)]
        banks_v = [ctx.enter_context(nc.psum_tensor(f"bank_v{i}", [N, TILE], F32)) for i in range(4)]

        def A(n):
            return banks_a[n % 4]

        def V(n):
            return banks_v[n % 4]

        loaded = sig("loaded", 0)
        set_dve, set_pe, set_crt, set_step = (sig(n, 0) for n in ("set_dve", "set_pe", "set_crt", "set_step"))
        act_full, act_done = sig("act_full", AU.n), sig("act_done", AU.n)
        vec_full, vec_done = sig("vec_full", VU.n), sig("vec_done", VU.n)
        dve_step, pool_step = sig("dve_step", DVE_STEPS), sig("pool_step", POOL_STEPS)
        root_ask, root_got = sig("root_ask", 7), sig("root_got", 9)
        x_in = [sig(f"x_in{j}", 16) for j in range(8)]
        xh_in = [sig(f"xh_in{s}", 64) for s in range(4)]
        squared, square_used = sig("squared", 8), sig("square_used", 8)
        sums_ready, gn_ready, fw_ready, diag_ready = (sig(n, 1) for n in ("sums_ready", "gn_ready", "fw_ready", "diag_ready"))
        gx_ready = sig("gx_ready", 8)
        xf_ready, xc_ready, low_ready = (sig(n, 1) for n in ("xf_ready", "xc_ready", "low_ready"))
        rh_t2, rh_ready, rh_used = sig("rh_t2", 8), sig("rh_ready", 8), sig("rh_used", 6)
        score_ready, exp_ready, prob_ready, bt_ready = (sig(n, 1) for n in ("score_ready", "exp_ready", "prob_ready", "bt_ready"))
        cri_in = [sig(f"cri_in{s}", 64) for s in range(2)]
        wh_t2, wh_ready, wh_used = sig("wh_t2", 8), sig("wh_ready", 8), sig("wh_used", 7)
        rows_ready, poolmix, osq_ready, oc_ready = sig("rows_ready", 1), sig("poolmix", 2), sig("osq_ready", 2), sig("oc_ready", 2)
        coef2_ready, x2_half, scaled, x2_ready, stored = sig("coef2_ready", 1), sig("x2_half", TILES), sig("scaled", TILES), sig("x2_ready", TILES), sig("stored", 128)
        xr_in = [sig(f"xr_in{s}", 64) for s in range(2)]
        gn2_ready, w2_ready, ab_ready = sig("gn2_ready", 1), sig("w2_ready", 1), sig("ab_ready", 8)
        zn_ready = sig("zn_ready", 1)

        block = ctx.enter_context(nc.Block())

        @block.sync
        def _(sync):
            sync.dma_start(cst[:, :], const).then_inc(loaded.sem, 16)
            sync.dma_start(col[:, :], cols).then_inc(loaded.sem, 16)
            sync.dma_start(vc[:, :], vec.to_broadcast([N, VEC_N])).then_inc(loaded.sem, 16)
            sync.dma_start(pj, proj).then_inc(loaded.sem, 16)
            sync.wait_ge(set_crt.sem, 1)
            sync.dma_start(kernels_dram, crt).then_inc(stored.sem, 16)
            with sync.Fori(0, BATCH) as b:
                first = sync.snap(b * N)
                xb = x.rearrange("b t h w -> (b t) h w")[bass.ds(first, N)]
                ob = out.rearrange("b t h w -> (b t) h w")[bass.ds(first, N)]
                sync.wait_ge(stored.sem, stored.at(b, 16))
                for j in range(16):
                    if j >= 4:
                        sync.wait_ge(act_done.sem, act_done.emptied(b, AU("st1", 2 * j - 7)))
                    sync.dma_start(xh[j % 4], xb[8 * j:8 * j + 8].rearrange("t h w -> h t w"))\
                        .then_inc(xh_in[j % 4].sem, 16)
                    if j % 2 == 1:
                        k = j // 2
                        sync.dma_start(big1[:, 2048 * k:2048 * k + 2048],
                                       xb[:, 16 * k:16 * k + 16].rearrange("t h w -> t (h w)"))\
                            .then_inc(x_in[k].sem, 16)
                for h in range(HEADS):
                    if h >= 2:
                        sync.wait_ge(wh_ready.sem, wh_ready.at(b, h - 1))
                        sync.wait_ge(wh_t2.sem, wh_t2.at(b, h - 1))
                    else:
                        sync.wait_ge(vec_done.sem, vec_done.emptied(b, VU("sc", 1)))
                    sync.dma_start(cri[h % 2], kernels_dram[h:h + 1, :].to_broadcast([N, 1024]))\
                        .then_inc(cri_in[h % 2].sem, 16)
                for j in range(8):
                    if j < 2:
                        sync.wait_ge(vec_full.sem, vec_full.full(b, VU("inv2", 7)))
                    else:
                        sync.wait_ge(x2_half.sem, x2_half.at(b, 4 * (j - 1)))
                    sync.dma_start(xr[j % 2], xb[:, 16 * j:16 * j + 16].rearrange("t h w -> t (h w)"))\
                        .then_inc(xr_in[j % 2].sem, 16)
                for j in range(8):
                    sync.wait_ge(vec_done.sem, vec_done.emptied(b, back_unit(4 * j + 3)))
                    sync.dma_start(ob[:, 16 * j:16 * j + 16].rearrange("t h w -> t (h w)"),
                                   big2[:, 2048 * j:2048 * j + 2048]).then_inc(stored.sem, 16)
            sync.wait_ge(stored.sem, stored.at(BATCH, 16))

        @block.tensor
        def _(pe):
            mm, tr = nc.tensor.matmul, nc.tensor.transpose

            pe.wait_ge(loaded.sem, 64)
            mm(banks_v[0][:, 0:1], W("wz")[:, 0:N], W("lnb"), start=True, stop=True).then_inc(set_pe.sem, 1)
            pe.wait_ge(set_dve.sem, 1)

            with pe.Fori(0, BATCH) as b:
                def inverse(k, coef):
                    for c in range(CH):
                        u = c // 2
                        bank = V(VU(f"inv{k}", u)) if c % 2 else A(AU(f"inv{k}", u))
                        if c % 2:
                            pe.wait_ge(vec_done.sem, vec_done.free(b, VU(f"inv{k}", u)))
                        else:
                            pe.wait_ge(act_done.sem, act_done.free(b, AU(f"inv{k}", u)))
                        mm(bank[:, :], coef[:, N * c:N * c + N], inv1[:, 512 * (c > 0):512 * (c > 0) + 512],
                           start=True, stop=True).then_inc(vec_full.sem if c % 2 else act_full.sem, 1)
                    pe.wait_ge(act_done.sem, act_done.emptied(b, AU(f"inv{k}", 3)))
                    pe.wait_ge(vec_done.sem, vec_done.emptied(b, VU(f"inv{k}", 3)))
                    for q in range(8):
                        u = 4 + q // 2
                        bank = V(VU(f"inv{k}", u)) if q % 2 else A(AU(f"inv{k}", u))
                        if q % 2:
                            pe.wait_ge(vec_done.sem, vec_done.free(b, VU(f"inv{k}", u)))
                        else:
                            pe.wait_ge(act_done.sem, act_done.free(b, AU(f"inv{k}", u)))
                        for j in range(4):
                            g = 4 * q + j
                            last = tr(bank[:, N * j:N * j + N], za[:, N * g:N * g + N], ident)
                        last.then_inc(vec_full.sem if q % 2 else act_full.sem, 1)
                    pe.wait_ge(act_done.sem, act_done.emptied(b, AU(f"inv{k}", 7)))
                    pe.wait_ge(vec_done.sem, vec_done.emptied(b, VU(f"inv{k}", 7)))

                def tile(unit, weights, image, g):
                    pe.wait_ge(act_done.sem, act_done.free(b, unit))
                    mm(A(unit)[:, :], weights, image[:, TILE * g:TILE * g + TILE], start=True, stop=False)
                    mm(A(unit)[:, :], zb[:, N * g:N * g + N], K("inv2"), start=False, stop=True)\
                        .then_inc(act_full.sem, 1)

                for q in range(16):
                    pe.wait_ge(xh_in[q % 4].sem, xh_in[q % 4].at(b, 16 * (q // 4 + 1)))
                    for r in range(2):
                        n = AU("st1", 2 * q + r)
                        pe.wait_ge(act_done.sem, act_done.free(b, n))
                        for j in range(4):
                            last = mm(A(n)[:, N * j:N * j + 65], xh[q % 4][:, 4 * r + j, :], K("fh"),
                                      start=True, stop=True)
                        last.then_inc(act_full.sem, 1)

                n = VU("sum")
                pe.wait_ge(sums_ready.sem, sums_ready.at(b, 1))
                pe.wait_ge(vec_done.sem, vec_done.free(b, n))
                mm(V(n)[:, 0:256], ones, s12[:, :], start=True, stop=True).then_inc(vec_full.sem, 1)

                pe.wait_ge(fw_ready.sem, fw_ready.at(b, 1))
                for u in range(8):
                    n = AU("st2", u)
                    pe.wait_ge(act_done.sem, act_done.free(b, n))
                    for j in range(8):
                        a = 8 * u + j
                        o = A(n)[:, 64 * j:64 * j + 64]
                        last = mm(o, yw[:, a, :], fws[:, 0:64], start=True, stop=a < 63)
                        if a == 63:
                            last = mm(o, yw[:, 64, :], fws[:, 64:128], start=False, stop=True)
                    last.then_inc(act_full.sem, 1)

                n = VU("sbc")
                pe.wait_ge(diag_ready.sem, diag_ready.at(b, 1))
                pe.wait_ge(vec_done.sem, vec_done.free(b, n))
                mm(V(n)[:, 0:N], ones, diag[:, 0:N], start=True, stop=True).then_inc(vec_full.sem, 1)

                pe.wait_ge(xf_ready.sem, xf_ready.at(b, 1))
                for u in range(8):
                    n = AU("xft", u)
                    pe.wait_ge(act_done.sem, act_done.free(b, n))
                    for j in range(4):
                        c = 4 * u + j
                        last = tr(A(n)[:, N * j:N * j + N], za[:, N * c:N * c + N], ident)
                    last.then_inc(act_full.sem, 1)
                n = VU("gram")
                pe.wait_ge(vec_done.sem, vec_done.free(b, n))
                for c in range(32):
                    if c % 4 == 0:
                        pe.wait_ge(act_done.sem, act_done.emptied(b, AU("xft", c // 4)))
                    last = mm(V(n)[:, 0:N], zb[:, N * c:N * c + N], zb[:, N * c:N * c + N], start=c == 0, stop=c == 31)
                last.then_inc(vec_full.sem, 1)

                pe.wait_ge(xc_ready.sem, xc_ready.at(b, 1))
                for u, src in enumerate((xc, xs)):
                    n = AU("xct", u)
                    pe.wait_ge(act_done.sem, act_done.free(b, n))
                    for c in range(4):
                        last = tr(A(n)[:, N * c:N * c + N], src[:, N * c:N * c + N], ident)
                    last.then_inc(act_full.sem, 1)

                pe.wait_ge(low_ready.sem, low_ready.at(b, 1))
                for h in range(HEADS):
                    n = VU("sc", h // 4)
                    if h % 4 == 0:
                        pe.wait_ge(vec_done.sem, vec_done.free(b, n))
                    pe.wait_ge(rh_ready.sem, rh_ready.at(b, h + 1))
                    for c in range(4):
                        last = mm(V(n)[:, N * (h % 4):N * (h % 4) + N], xct[:, N * c:N * c + N],
                                  rh[h % 2][:, N * c:N * c + N], start=c == 0, stop=c == 3)
                    last.then_inc(vec_full.sem if h % 4 == 3 else rh_used.sem, 1)

                pe.wait_ge(prob_ready.sem, prob_ready.at(b, 1))
                for u in range(2):
                    n = AU("pt", u)
                    pe.wait_ge(act_done.sem, act_done.free(b, n))
                    for j in range(4):
                        h = 4 * u + j
                        last = tr(A(n)[:, N * j:N * j + N], prob[:, N * h:N * h + N], ident)
                    last.then_inc(act_full.sem, 1)

                pe.wait_ge(vec_done.sem, vec_done.free(b, VU("u", 0)))
                pe.wait_ge(vec_done.sem, vec_done.free(b, VU("u", 1)))
                for h in range(HEADS):
                    if h % 4 == 0:
                        pe.wait_ge(act_done.sem, act_done.emptied(b, AU("pt", h // 4)))
                    pe.wait_ge(wh_ready.sem, wh_ready.at(b, h + 1))
                    for c in range(CH):
                        last = mm(V(VU("u", 1 - c // 4))[:, N * (c % 4):N * (c % 4) + N], wh[h % 2][:, N * c:N * c + N],
                                  pt[:, N * h:N * h + N], start=h == 0 and c % 4 == 0,
                                  stop=h == HEADS - 1 and c > 0, skip_group_check=True)
                    last.then_inc(wh_used.sem if h < HEADS - 1 else vec_full.sem, 1)
                pe.wait_ge(bt_ready.sem, bt_ready.at(b, 1))
                mm(V(VU("u", 1))[:, 0:N], dmat[:, :], at_[:, :], start=False, stop=True,
                   skip_group_check=True).then_inc(vec_full.sem, 1)
                for u in range(2):
                    n = VU("fy", u)
                    pe.wait_ge(vec_done.sem, vec_done.free(b, n))
                    for j in range(4):
                        c = 4 * u + j
                        last = mm(V(n)[:, N * j:N * j + N], xcg[:, N * c:N * c + N], bt[:, :], start=True, stop=True)
                    last.then_inc(vec_full.sem, 1)

                pe.wait_ge(vec_done.sem, vec_done.emptied(b, VU("u", 1)))
                inverse(0, ul)

                for g in range(TILES):
                    if g % 4 == 0:
                        pe.wait_ge(gx_ready.sem, gx_ready.at(b, g // 4 + 1))
                    tile(AU("y", g), bt[:, :], big1, g)

                n = VU("rows")
                pe.wait_ge(rows_ready.sem, rows_ready.at(b, 1))
                pe.wait_ge(vec_done.sem, vec_done.free(b, n))
                mm(V(n)[:, 0:384], ones, diag[:, :], start=True, stop=True).then_inc(vec_full.sem, 1)

                def mix(layer):
                    pe.wait_ge(vec_done.sem, vec_done.emptied(b, VU("hc", 1) if layer else VU("rows")))
                    for u in range(2):
                        n = AU(f"swap{layer}", u)
                        pe.wait_ge(act_done.sem, act_done.free(b, n))
                        mm(A(n)[:, :], K("swap"), hc[:, 512 * u:512 * u + 512], start=True, stop=True)\
                            .then_inc(act_full.sem, 1)
                    n = VU(f"var{layer}")
                    pe.wait_ge(osq_ready.sem, osq_ready.at(b, layer + 1))
                    pe.wait_ge(vec_done.sem, vec_done.free(b, n))
                    for c in range(CH):
                        last = mm(V(n)[:, 0:N], varw[:, N * (c > 0):N * (c > 0) + N], osq[:, N * c:N * c + N],
                                  start=c == 0, stop=c == CH - 1)
                    last.then_inc(vec_full.sem, 1)
                    pe.wait_ge(oc_ready.sem, oc_ready.at(b, layer + 1))
                    inverse(layer + 1, oc)

                varw = K("varw")
                mix(0)

                def turn(g):
                    n = VU("h1t", g)
                    pe.wait_ge(act_done.sem, act_done.emptied(b, gelu_unit(g)))
                    pe.wait_ge(vec_done.sem, vec_done.free(b, n))
                    for j in range(4):
                        at = TILE * g + N * j
                        last = tr(V(n)[:, N * j:N * j + N], big2[:, at:at + N], ident)
                    last.then_inc(vec_full.sem, 1)

                def rows(g):
                    n = zf_unit(g // 4)
                    pe.wait_ge(vec_done.sem, vec_done.emptied(b, VU("h1t", g)))
                    if g % 4 == 0:
                        pe.wait_ge(act_done.sem, act_done.free(b, n))
                    for j in range(4):
                        row = 4 * (g % 4) + j
                        last = mm(A(n)[:, 32 * row:32 * row + 32], h1w[:, TILE * (g % 4) + N * j:TILE * (g % 4) + N * j + N],
                                  K("f2w"), start=True, stop=True)
                    if g % 4 == 3:
                        last.then_inc(act_full.sem, 1)

                for g in range(TILES + 2):
                    if g < TILES:
                        tile(gelu_unit(g), m1s[:, :], big1, g)
                    if 1 <= g <= TILES:
                        turn(g - 1)
                    if g >= 2:
                        rows(g - 2)

                for q in range(8):
                    u = q // 2
                    n = VU("zh", u) if q % 2 else AU("zh", u)
                    if q == 0:
                        pe.wait_ge(act_done.sem, act_done.emptied(b, zf_unit(7)))
                    if q % 2:
                        pe.wait_ge(vec_done.sem, vec_done.free(b, n))
                    else:
                        pe.wait_ge(act_done.sem, act_done.free(b, n))
                    bank = V(n) if q % 2 else A(n)
                    for j in range(4):
                        c = 4 * q + j
                        last = tr(bank[:, N * j:N * j + N], za[:, N * c:N * c + N], ident)
                    last.then_inc(vec_full.sem if q % 2 else act_full.sem, 1)
                pe.wait_ge(act_done.sem, act_done.emptied(b, AU("zh", 3)))
                pe.wait_ge(vec_done.sem, vec_done.emptied(b, VU("zh", 3)))
                for u in range(2):
                    n = VU("hc", u)
                    pe.wait_ge(vec_done.sem, vec_done.free(b, n))
                    for j in range(4):
                        c = 4 * u + j
                        for v in range(4):
                            r = 4 * c + v
                            last = mm(V(n)[:, N * j:N * j + N], f2h[:, N * v:N * v + N], zb[:, N * r:N * r + N],
                                      start=v == 0, stop=v == 3)
                    last.then_inc(vec_full.sem, 1)
                mix(1)

                for g in range(TILES):
                    tile(AU("p2", g), W("skip")[:, N:2 * N], big2, g)

                for g in range(TILES):
                    n = AU("x2t", g)
                    pe.wait_ge(x2_ready.sem, x2_ready.at(b, g + 1))
                    pe.wait_ge(act_done.sem, act_done.free(b, n))
                    for j in range(4):
                        at = TILE * g + N * j
                        last = tr(A(n)[:, N * j:N * j + N], big2[:, at:at + N], ident)
                    last.then_inc(act_full.sem, 1)

                n = VU("gn2")
                pe.wait_ge(gn2_ready.sem, gn2_ready.at(b, 1))
                pe.wait_ge(vec_done.sem, vec_done.free(b, n))
                mm(V(n)[:, 0:2], K("quad"), sm[:, 40:42], start=True, stop=True).then_inc(vec_full.sem, 1)
                n = VU("bias")
                pe.wait_ge(w2_ready.sem, w2_ready.at(b, 1))
                pe.wait_ge(vec_done.sem, vec_done.free(b, n))
                for k, weights in enumerate((wabs[:, 0:N], wabs[:, N:2 * N], wgs[:, :])):
                    last = mm(V(n)[:, k:k + 1], weights, sm[:, 48:49], start=True, stop=True)
                last.then_inc(vec_full.sem, 1)

                for k in range(8 + 2):
                    if k < 8:
                        n, m = AU("abx", k), aby_unit(k)
                        pe.wait_ge(act_done.sem, act_done.free(b, n))
                        for j in range(4):
                            at = TILE * (4 * k + j)
                            last = mm(A(n)[32 * j:32 * j + 32, :], wabs[:, 0:32], big1[:, at:at + TILE], start=True,
                                      stop=True)
                        last.then_inc(act_full.sem, 1)
                        pe.wait_ge(vec_done.sem, vec_done.free(b, m))
                        for j in range(4):
                            at = TILE * (4 * k + j)
                            last = mm(V(m)[32 * j:32 * j + 32, :], wabs[:, N:N + 32], big1[:, at:at + TILE], start=True,
                                      stop=True)
                        last.then_inc(vec_full.sem, 1)
                    if k >= 2:
                        m = abt_unit(k - 2)
                        pe.wait_ge(ab_ready.sem, ab_ready.at(b, k - 1))
                        pe.wait_ge(vec_done.sem, vec_done.free(b, m))
                        for j in range(4):
                            last = tr(V(m)[:, N * j:N * j + N], prods[k % 2][:, N * j:N * j + N], ident)
                        last.then_inc(vec_full.sem, 1)
                pe.wait_ge(vec_done.sem, vec_done.emptied(b, abt_unit(7)))
                for u in range(4):
                    n = AU("af", u)
                    pe.wait_ge(act_done.sem, act_done.free(b, n))
                    for j in range(4):
                        c = 4 * u + j
                        last = tr(A(n)[:, N * j:N * j + N], abt[:, c, :], ident)
                    last.then_inc(act_full.sem, 1)
                for u in range(4):
                    n = VU("z", u)
                    if u == 0:
                        pe.wait_ge(act_done.sem, act_done.emptied(b, AU("af", 3)))
                    pe.wait_ge(vec_done.sem, vec_done.free(b, n))
                    for j in range(4):
                        c = 4 * u + j
                        last = mm(V(n)[:, N * j:N * j + N], af[:, N * c:N * c + N], bf[:, N * c:N * c + N], start=True,
                                  stop=True)
                    last.then_inc(vec_full.sem, 1)
                pe.wait_ge(zn_ready.sem, zn_ready.at(b, 1))
                for u in range(4):
                    n = AU("znt", u)
                    pe.wait_ge(act_done.sem, act_done.free(b, n))
                    for j in range(4):
                        c = 4 * u + j
                        last = tr(A(n)[:, N * j:N * j + N], z2[:, N * c:N * c + N], ident)
                    last.then_inc(act_full.sem, 1)
                pe.wait_ge(act_done.sem, act_done.emptied(b, AU("znt", 3)))

                def turn_back(g):
                    n = back_unit(g)
                    pe.wait_ge(vec_done.sem, vec_done.emptied(b, zz_unit(g)))
                    pe.wait_ge(vec_done.sem, vec_done.free(b, n))
                    for j in range(4):
                        last = tr(V(n)[:, N * j:N * j + N], ow[g % 2][:, N * j:N * j + N], ident)
                    last.then_inc(vec_full.sem, 1)

                for g in range(TILES + 1):
                    if g < TILES:
                        n = AU("g", g)
                        pe.wait_ge(act_done.sem, act_done.free(b, n))
                        mm(A(n)[:, :], wgs[:, :], big1[:, TILE * g:TILE * g + TILE], start=True, stop=True)\
                            .then_inc(act_full.sem, 1)
                        n = zz_unit(g)
                        pe.wait_ge(vec_done.sem, vec_done.free(b, n))
                        for j in range(4):
                            h = 4 * g + j
                            last = mm(V(n)[:, N * j:N * j + N], wzs[:, N * (h % 8):N * (h % 8) + N], znt[:, h // 8, :],
                                      start=True, stop=True)
                        last.then_inc(vec_full.sem, 1)
                    if g >= 1:
                        turn_back(g - 1)

        @block.scalar
        def _(act):
            act.wait_ge(loaded.sem, 64)
            act.wait_ge(set_dve.sem, 1)
            with act.Fori(0, BATCH) as b:
                roots = [0]

                def square_root(n, unit=None):
                    if unit is None:
                        roots[0] += 1
                        act.wait_ge(root_ask.sem, root_ask.at(b, roots[0]))
                    else:
                        act.wait_ge(vec_done.sem, vec_done.emptied(b, unit))
                    nc.scalar.activation(root[:, 0:n], root[:, 0:n], ACT.Sqrt, bias=sm[:, 63:64])\
                        .then_inc(root_got.sem, 1)

                def inverse(k):
                    for u in range(4):
                        act.wait_ge(act_full.sem, act_full.full(b, AU(f"inv{k}", u)))
                        nc.scalar.activation(inverse_rows(za, 2 * u), A(AU(f"inv{k}", u))[:, :].rearrange("p (y r h) -> p y r h", y=2, r=2), ACT.Copy).then_inc(act_done.sem, 1)
                    for u in range(4, 8):
                        act.wait_ge(act_full.sem, act_full.full(b, AU(f"inv{k}", u)))
                        q = 2 * (u - 4)
                        nc.scalar.activation(zb[:, TILE * q:TILE * q + TILE], A(AU(f"inv{k}", u))[:, :], ACT.Copy).then_inc(act_done.sem, 1)

                for j in range(8):
                    act.wait_ge(x_in[j].sem, x_in[j].at(b, 16))
                    if j >= 2:
                        act.wait_ge(square_used.sem, square_used.at(b, j - 1))
                    nc.scalar.activation(sq[j % 2], big1[:, 2048 * j:2048 * j + 2048], ACT.Square)\
                        .then_inc(squared.sem, 1)
                    for u in range(4 * j, 4 * j + 4):
                        n = AU("st1", u)
                        act.wait_ge(act_full.sem, act_full.full(b, n))
                        nc.scalar.activation(yw[:, :, 4 * u:4 * u + 4].rearrange("p a t -> p t a"),
                             A(n)[:, :].rearrange("p (t a) -> p t a", t=4)[:, :, 0:65], ACT.Copy).then_inc(act_done.sem, 1)
                square_root(32)
                square_root(1)
                for u in range(8):
                    act.wait_ge(act_full.sem, act_full.full(b, AU("st2", u)))
                    if u == 0:
                        act.wait_ge(square_used.sem, square_used.at(b, 8))
                    nc.scalar.activation(za[:, TILE * u:TILE * u + TILE], A(AU("st2", u))[:, :], ACT.Copy).then_inc(act_done.sem, 1)
                for u in range(8):
                    act.wait_ge(act_full.sem, act_full.full(b, AU("xft", u)))
                    nc.scalar.activation(zb[:, TILE * u:TILE * u + TILE], A(AU("xft", u))[:, :], ACT.Copy).then_inc(act_done.sem, 1)
                for u, dst in enumerate((xct, xst)):
                    act.wait_ge(act_full.sem, act_full.full(b, AU("xct", u)))
                    nc.scalar.activation(dst, A(AU("xct", u))[:, :], ACT.Copy).then_inc(act_done.sem, 1)
                act.wait_ge(score_ready.sem, score_ready.at(b, 1))
                nc.scalar.activation(sc, sc, ACT.Exp, scale=1.0 / 64).then_inc(exp_ready.sem, 1)
                for u in range(2):
                    act.wait_ge(act_full.sem, act_full.full(b, AU("pt", u)))
                    nc.scalar.activation(pt[:, TILE * u:TILE * u + TILE], A(AU("pt", u))[:, :], ACT.Copy).then_inc(act_done.sem, 1)
                inverse(0)
                for g in range(TILES):
                    act.wait_ge(act_full.sem, act_full.full(b, AU("y", g)))
                    nc.scalar.activation(big1[:, TILE * g:TILE * g + TILE], A(AU("y", g))[:, :], ACT.Copy).then_inc(act_done.sem, 1)
                square_root(1)
                square_root(1)

                def mix(layer):
                    for u in range(2):
                        act.wait_ge(act_full.sem, act_full.full(b, AU(f"swap{layer}", u)))
                        nc.scalar.activation(hs[:, TILE * u:TILE * u + TILE], A(AU(f"swap{layer}", u))[:, :], ACT.Copy).then_inc(act_done.sem, 1)
                    square_root(N, VU(f"var{layer}"))
                    inverse(layer + 1)

                mix(0)

                def row_transforms(k):
                    act.wait_ge(act_full.sem, act_full.full(b, zf_unit(k)))
                    nc.scalar.activation(za[:, :].rearrange("p (k h) -> p h k", h=N)[:, 16 * k:16 * k + 16, :],
                         A(zf_unit(k))[:, :].rearrange("p (h k) -> p h k", k=32), ACT.Copy).then_inc(act_done.sem, 1)

                for g in range(TILES):
                    act.wait_ge(act_full.sem, act_full.full(b, gelu_unit(g)))
                    nc.scalar.activation(big2[:, TILE * g:TILE * g + TILE], A(gelu_unit(g))[:, :], ACT.Gelu)\
                        .then_inc(act_done.sem, 1)
                    if g >= 5 and (g - 5) % 4 == 0:
                        row_transforms((g - 5) // 4)
                row_transforms(7)
                for u in range(4):
                    act.wait_ge(act_full.sem, act_full.full(b, AU("zh", u)))
                    nc.scalar.activation(zb[:, 2 * TILE * u:2 * TILE * u + TILE], A(AU("zh", u))[:, :], ACT.Copy).then_inc(act_done.sem, 1)
                mix(1)
                for g in range(TILES):
                    act.wait_ge(act_full.sem, act_full.full(b, AU("p2", g)))
                    nc.scalar.activation(big2[:, TILE * g:TILE * g + TILE], A(AU("p2", g))[:, :], ACT.Copy).then_inc(act_done.sem, 1)
                square_root(1)

                act.wait_ge(coef2_ready.sem, coef2_ready.at(b, 1))
                for g in range(TILES + 2):
                    if g < TILES:
                        at = slice(TILE * g, TILE * g + TILE)
                        nc.scalar.activation(big2[:, at], big2[:, at], ACT.Identity, bias=sm[:, 31:32],
                                             scale=sm[:, 30:31]).then_inc(scaled.sem, 1)
                    if g >= 2:
                        n = AU("x2t", g - 2)
                        act.wait_ge(act_full.sem, act_full.full(b, n))
                        nc.scalar.activation(big1[:, TILE * (g - 2):TILE * (g - 2) + TILE], A(n)[:, :], ACT.Copy).then_inc(act_done.sem, 1)
                square_root(1)
                for k in range(8 + 1):
                    if k < 8:
                        n = AU("abx", k)
                        act.wait_ge(act_full.sem, act_full.full(b, n))
                        if k == 0:
                            act.wait_ge(vec_done.sem, vec_done.emptied(b, VU("bias")))
                        elif k >= 2:
                            act.wait_ge(vec_done.sem, vec_done.emptied(b, aby_unit(k - 2)))
                        nc.scalar.activation(firsts[k % 2], A(n)[:, :], ACT.Identity, bias=sm[:, 51:52])\
                            .then_inc(act_done.sem, 1)
                    if k >= 1:
                        act.wait_ge(vec_done.sem, vec_done.emptied(b, aby_unit(k - 1)))
                        nc.scalar.activation(prods[(k - 1) % 2], prods[(k - 1) % 2], ACT.Sigmoid).then_inc(ab_ready.sem, 1)
                for u in range(4):
                    act.wait_ge(act_full.sem, act_full.full(b, AU("af", u)))
                    nc.scalar.activation(af[:, TILE * u:TILE * u + TILE], A(AU("af", u))[:, :], ACT.Copy).then_inc(act_done.sem, 1)
                square_root(N)
                for u in range(4):
                    act.wait_ge(act_full.sem, act_full.full(b, AU("znt", u)))
                    nc.scalar.activation(znt[:, 4 * u:4 * u + 4, :], A(AU("znt", u))[:, :].rearrange("p (j i) -> p j i", i=N), ACT.Copy).then_inc(act_done.sem, 1)
                for g in range(TILES):
                    act.wait_ge(act_full.sem, act_full.full(b, AU("g", g)))
                    if g >= 2:
                        act.wait_ge(vec_done.sem, vec_done.emptied(b, zz_unit(g - 2)))
                    nc.scalar.activation(gt[g % 2], A(AU("g", g))[:, :], ACT.Sigmoid, bias=sm[:, 50:51])\
                        .then_inc(act_done.sem, 1)

        @block.gpsimd
        def _(pool):
            pool.wait_ge(loaded.sem, 64)
            pool.wait_ge(set_dve.sem, 1)
            tt = nc.gpsimd.tensor_tensor
            with pool.Fori(0, BATCH) as b:
                steps = [0]

                def link(ins):
                    steps[0] += 1
                    ins.then_inc(pool_step.sem, 1)
                    pool.wait_ge(pool_step.sem, pool_step.at(b, steps[0]))

                def gx(j):
                    v = big1[:, 2048 * j:2048 * j + 2048].rearrange("p (h w) -> p h w", w=N)
                    link(tt(v, v, bc(mr_bc[:, 0:N], 1, 16), ALU.subtract))
                    tt(v, v, bc(mr_bc[:, N:2 * N], 1, 16), ALU.mult).then_inc(gx_ready.sem, 1)

                pool.wait_ge(gn_ready.sem, gn_ready.at(b, 1))
                pool.wait_ge(act_done.sem, act_done.emptied(b, AU("st1", 31)))
                for j in range(3):
                    gx(j)
                pool.wait_ge(low_ready.sem, low_ready.at(b, 1))
                for h in range(HEADS):
                    if h >= 2:
                        pool.wait_ge(rh_ready.sem, rh_ready.at(b, h - 1))
                    tt(t2[h % 2][:, 0:512].rearrange("p (c t) -> p c t", t=N), xst.rearrange("p (c t) -> p c t", t=N),
                       bc(mit[:, :].rearrange("p (c h) -> p c h", h=HEADS)[:, :, h], 2, N), ALU.mult)\
                        .then_inc(rh_t2.sem, 1)
                for h in range(HEADS):
                    pool.wait_ge(cri_in[h % 2].sem, cri_in[h % 2].at(b, 16 * (h // 2 + 1)))
                    if h >= 2:
                        pool.wait_ge(wh_ready.sem, wh_ready.at(b, h - 1))
                    elif h == 0:
                        pool.wait_ge(rh_ready.sem, rh_ready.at(b, HEADS))
                    tt(t2[h % 2].rearrange("p (y r k) -> p y r k", r=2, k=KX), xs.rearrange("p (y r k) -> p y r k", r=2, k=KX),
                       bc(cri[h % 2][:, 512:1024].rearrange("p (y k) -> p y k", k=KX), 2, 2), ALU.mult)\
                        .then_inc(wh_t2.sem, 1)
                for j in range(3, 8):
                    gx(j)

                def mix(layer):
                    w = W("mix")[:, 256 * layer + 128:256 * layer + 256].rearrange("p (c i o) -> p c i o", c=CH, i=4)
                    src = hs.rearrange("p (c g i) -> p c g i", c=CH, i=4)
                    pool.wait_ge(act_done.sem, act_done.emptied(b, AU(f"swap{layer}", 1)))
                    for i in range(4):
                        dst = (tmpp if i else accp).rearrange("p (c g o) -> p c g o", c=CH, o=4)
                        link(tt(dst, bc(src[:, :, :, i], 3, 4), bc(w[:, :, i, :], 2, 32), ALU.mult))
                        if 0 < i < 3:
                            link(tt(accp, accp, tmpp, ALU.add))
                    tt(accp, accp, tmpp, ALU.add).then_inc(poolmix.sem, 1)

                mix(0)
                mix(1)
                for g in range(TILES):
                    at = slice(TILE * g, TILE * g + TILE)
                    pool.wait_ge(x2_half.sem, x2_half.at(b, g + 1))
                    pool.wait_ge(scaled.sem, scaled.at(b, g + 1))
                    tt(big2[:, at], big2[:, at], big1[:, at], ALU.add).then_inc(x2_ready.sem, 1)
                assert steps[0] == POOL_STEPS, ("POOL_STEPS", steps[0])

        @block.vector
        def _(dve):
            v = nc.vector
            tt, ts, stt, red = v.tensor_tensor, v.tensor_scalar, v.scalar_tensor_tensor, v.tensor_reduce
            count = [0]

            def step(ins):
                count[0] += 1
                ins.then_inc(set_step.sem, 1)
                dve.wait_ge(set_step.sem, count[0])

            v.memset(sm[:, 63:64], EPS)
            v.memset(dmat[:, :], 0.0)
            dve.wait_ge(loaded.sem, 64)
            kq = W("kq").rearrange("p (f g n) -> p f g n", f=4, g=2)
            for f, op in ((0, ALU.add), (2, ALU.subtract)):
                for g in range(2):
                    step(tt(kq[0:64, f, g, 0:8], kq[0:64, f, g, 0:8], kq[0:64, f + 1, g, 0:8], op))
                    step(ts(kq[0:64, f, g, 0:8], kq[0:64, f, g, 0:8], 0.5, None, ALU.mult))
            for layer in range(2):
                for f, op in ((0, ALU.add), (1, ALU.subtract)):
                    at = COL["mix"].start + 256 * layer + 128 * f
                    rv = COL["mixrev"].start + 32 * layer + 16 * f
                    step(tt(col[0:64, at:at + 16], col[0:64, at:at + 16], col[0:64, rv:rv + 16], op))
                    step(ts(col[0:64, at:at + 16], col[0:64, at:at + 16], 0.5, None, ALU.mult))
            swk, swq, swv = (B("sw")[:, 8 * i:8 * i + 8] for i in range(3))
            step(tt(B("sb"), B("sb"), B("bias"), ALU.add))
            cbk, cbq, cbv = (B("sb")[:, 8 * i:8 * i + 8] for i in range(3))
            kr, qr, ki, qi = kq[:, 0, 0, :], kq[:, 0, 1, :], kq[:, 2, 0, :], kq[:, 2, 1, :]
            chunks = lambda ap: ap.rearrange("p (c h) -> p c h", h=HEADS)
            step(tt(chunks(kr), chunks(kr), bc(swk, 1, 4), ALU.add))
            step(tt(chunks(qr), chunks(qr), bc(swq, 1, 4), ALU.add))
            step(tt(mrt[:, :], qr, kr, ALU.mult))
            step(tt(mit[:, :], qi, ki, ALU.mult))
            step(tt(mrt[:, :], mrt[:, :], mit[:, :], ALU.add))
            step(tt(wsum[:, :], swq, swk, ALU.mult))
            step(tt(chunks(mrt[:, :]), chunks(mrt[:, :]), bc(wsum[:, :], 1, 4), ALU.subtract))
            step(tt(mit[:, :], qr, ki, ALU.mult))
            step(tt(gs[:, 0:32], qi, kr, ALU.mult))
            step(tt(mit[:, :], mit[:, :], gs[:, 0:32], ALU.subtract))
            step(ts(mrt[:, :], mrt[:, :], K("rho"), None, ALU.mult))
            step(ts(mit[:, :], mit[:, :], K("rho"), None, ALU.mult))
            step(tt(mrt[0:1, 0:8], mrt[0:1, 0:8], wsum[0:1, :], ALU.add))
            step(tt(gs[0:1, 32:40], cbk[0:1, :], qr[0:1, 0:8], ALU.mult))
            step(ts(mit[0:1, 0:8], gs[0:1, 32:40], -1.0, None, ALU.mult))
            step(tt(mrt[32:33, 0:8], cbk[32:33, :], cbq[32:33, :], ALU.mult))
            step(tt(mit[32:33, 0:8], cbq[32:33, :], kr[32:33, 0:8], ALU.mult))
            step(tt(ccol[:, :], B("pdc"), B("psw"), ALU.add))
            step(tt(ccol[:, :], ccol[:, :], cbv, ALU.mult))
            step(tt(gs[:, 40:41], B("pbias"), B("psb"), ALU.add))
            step(tt(ccol[:, 0:1], ccol[:, 0:1], gs[:, 40:41], ALU.add))
            step(ts(ccol[:, :], ccol[:, :], DC, None, ALU.mult))
            vsum = sm[:, 0:8]
            step(tt(vsum, B("psw"), swv, ALU.mult))
            step(ts(sm[:, 8:9], B("n1b"), DC, None, ALU.mult))
            step(ts(B("mixsb"), B("mixsb"), DC, None, ALU.mult))
            step(ts(wzs[:, :], W("wz"), W("lng"), None, ALU.mult))
            dve.wait_ge(set_pe.sem, 1)
            step(tt(sm[:, 9:10], banks_v[0][:, 0:1], W("bz"), ALU.add))
            f4 = [pj[:, 512 * i:512 * i + 512] for i in range(4)]
            for i, op in enumerate((ALU.add, ALU.subtract, ALU.add, ALU.subtract)):
                step(tt(f4[i][:, 0:KX], f4[i][:, 0:KX], pj[:, 2048 + 32 * i:2080 + 32 * i], op))
                step(ts(f4[i][:, 0:KX], f4[i][:, 0:KX], 0.5, None, ALU.mult))
            swv8, psw8 = pj[:, 2176:2177], pj[:, 2177:2178]
            cr, ci = crt[:, 0:512], crt[:, 512:1024]
            tmp8, vr8 = big1[0:8, 0:512], big1[0:8, 512:1024]
            step(ts(vr8, f4[2], swv8, None, ALU.add))
            step(tt(cr, f4[0], vr8, ALU.mult))
            step(tt(tmp8, f4[1], f4[3], ALU.mult))
            step(tt(cr, cr, tmp8, ALU.subtract))
            step(stt(cr, f4[2], psw8, cr, ALU.mult, ALU.add))
            step(tt(ci, f4[0], f4[3], ALU.mult))
            step(tt(tmp8, f4[1], vr8, ALU.mult))
            step(tt(ci, ci, tmp8, ALU.add))
            stt(ci, f4[3], psw8, ci, ALU.mult, ALU.add).then_inc(set_crt.sem, 1)
            for i in range(4):
                v.memset(gs[:, 112 + i:113 + i], 0.0).then_inc(act_done.sem, 1)
                v.memset(gs[:, 116 + i:117 + i], 0.0).then_inc(vec_done.sem, 1)
            v.memset(gs[:, 110:111], 0.0).then_inc(set_dve.sem, 1)

            with dve.Fori(0, BATCH) as b:
                steps, roots = [0], [0]

                def link(ins):
                    steps[0] += 1
                    ins.then_inc(dve_step.sem, 1)
                    dve.wait_ge(dve_step.sem, dve_step.at(b, steps[0]))

                def link_done(ins, n):
                    ins.then_inc(vec_done.sem, 1)
                    dve.wait_ge(vec_done.sem, vec_done.emptied(b, n))

                def inverse_root(dst, n):
                    roots[0] += 1
                    dve.wait_ge(root_got.sem, root_got.at(b, roots[0]))
                    link(v.reciprocal(dst, root[:, 0:n]))

                def inverse(k):
                    for u in range(4):
                        dve.wait_ge(vec_full.sem, vec_full.full(b, VU(f"inv{k}", u)))
                        v.tensor_copy(inverse_rows(za, 2 * u + 1),
                                           V(VU(f"inv{k}", u))[:, :].rearrange("p (y r h) -> p y r h", y=2, r=2)).then_inc(vec_done.sem, 1)
                    for u in range(4, 8):
                        dve.wait_ge(vec_full.sem, vec_full.full(b, VU(f"inv{k}", u)))
                        q = 2 * (u - 4) + 1
                        v.tensor_copy(zb[:, TILE * q:TILE * q + TILE], V(VU(f"inv{k}", u))[:, :]).then_inc(vec_done.sem, 1)

                for j in range(8):
                    dve.wait_ge(x_in[j].sem, x_in[j].at(b, 16))
                    red(s1p[:, j, :], big1[:, 2048 * j:2048 * j + 2048].rearrange("p (h w) -> p w h", w=N), AX.X, ALU.add)
                    dve.wait_ge(squared.sem, squared.at(b, j + 1))
                    red(s2p[:, j, :], sq[j % 2].rearrange("p (h w) -> p w h", w=N), AX.X, ALU.add)\
                        .then_inc(square_used.sem, 1)
                dve.wait_ge(square_used.sem, square_used.at(b, 8))
                s1, s2 = s12[:, 0:N], s12[:, N:2 * N]
                link(red(s1, s1p.rearrange("p j w -> p w j"), AX.X, ALU.add))
                red(s2, s2p.rearrange("p j w -> p w j"), AX.X, ALU.add).then_inc(sums_ready.sem, 1)
                dve.wait_ge(sums_ready.sem, sums_ready.at(b, 1))
                dve.wait_ge(vec_full.sem, vec_full.full(b, VU("sum")))
                link_done(red(gs[:, 0:64], V(VU("sum"))[:, 0:256].rearrange("p (g q) -> p g q", q=4), AX.X, ALU.add), VU("sum"))
                link(ts(gs[:, 0:64], gs[:, 0:64], 1.0 / (4 * HW), None, ALU.mult))
                link(tt(gs[:, 64:96], gs[:, 0:32], gs[:, 0:32], ALU.mult))
                tt(root[:, 0:32], gs[:, 32:64], gs[:, 64:96], ALU.subtract).then_inc(root_ask.sem, 1)
                mean, rstd = mr_bc[:, 0:N], mr_bc[:, N:2 * N]
                link(v.tensor_copy(mean.rearrange("p (g q) -> p g q", q=4), bc(gs[:, 0:32], 2, 4)))
                inverse_root(gs[:, 64:96], 32)
                v.tensor_copy(rstd.rearrange("p (g q) -> p g q", q=4), bc(gs[:, 64:96], 2, 4)).then_inc(gn_ready.sem, 1)
                dve.wait_ge(gn_ready.sem, gn_ready.at(b, 1))
                link(tt(tq[:, :], mean, ident, ALU.mult))
                link(red(sm[:, 10:11], tq[:, :], AX.X, ALU.add))
                link(tt(tu[:, :], rstd, ident, ALU.mult))
                link(red(sm[:, 11:12], tu[:, :], AX.X, ALU.add))
                link(ts(sm[:, 10:11], sm[:, 10:11], 128.0 / 16, None, ALU.mult))
                link(ts(fws[:, :], K("fw"), sm[:, 11:12], None, ALU.mult))
                dve.wait_ge(act_done.sem, act_done.emptied(b, AU("st1", 31)))
                ts(yw[:, 0, :], yw[:, 0, :], sm[:, 10:11], None, ALU.subtract).then_inc(fw_ready.sem, 1)
                link(stt(tq[:, :], mean, -128.0, s1, ALU.mult, ALU.add))
                link(tt(tu[:, :], s1, tq[:, :], ALU.add))
                link(tt(tu[:, :], tu[:, :], mean, ALU.mult))
                link(tt(tu[:, :], s2, tu[:, :], ALU.subtract))
                link(tt(tu[:, :], tu[:, :], rstd, ALU.mult))
                link(tt(tu[:, :], tu[:, :], rstd, ALU.mult))
                link(tt(tq[:, :], tq[:, :], rstd, ALU.mult))
                link(red(sm[:, 12:13], tq[:, :], AX.X, ALU.add))
                link(red(sm[:, 13:14], tu[:, :], AX.X, ALU.add))
                link(ts(sm[:, 12:14], sm[:, 12:14], 1.0 / HW, None, ALU.mult))
                link(tt(sm[:, 14:15], sm[:, 12:13], sm[:, 12:13], ALU.mult))
                tt(root[:, 0:1], sm[:, 13:14], sm[:, 14:15], ALU.subtract).then_inc(root_ask.sem, 1)
                inverse_root(sm[:, 15:16], 1)
                scol = sm[:, 16:17]
                link(tt(scol, sm[:, 15:16], B("n1w"), ALU.mult))
                ts(diag[:, 0:N], ident, scol, None, ALU.mult).then_inc(diag_ready.sem, 1)
                link(tt(sm[:, 17:18], scol, sm[:, 12:13], ALU.mult))
                link(tt(sm[:, 17:18], B("n1b"), sm[:, 17:18], ALU.subtract))
                link(ts(dmat[:, 0:1], sm[:, 17:18], DC, None, ALU.mult))
                dve.wait_ge(vec_full.sem, vec_full.full(b, VU("sbc")))

                dve.wait_ge(act_done.sem, act_done.emptied(b, AU("st2", 7)))
                xf = za[:, :].rearrange("p (a b) -> p a b", b=64)

                def f(a0, a1, b0, b1):
                    return xf[:, a0:a1, b0:b1].rearrange("p a b -> p b a")

                plane = lambda ap: ap.rearrange("p (y r k) -> p y r k", r=2, k=KX)
                m = plane(xcg)
                tt(m[:, 1:16, 0, 1:16], f(1, 16, 1, 16), f(32, 47, 33, 48), ALU.subtract)
                stt(m[:, 1:16, 1, 1:16], f(32, 47, 1, 16), -1.0, f(1, 16, 33, 48), ALU.mult, ALU.subtract)
                tt(m[:, 1:16, 0, 16:32], f(1, 17, 1, 16), f(32, 48, 33, 48), ALU.add)
                tt(m[:, 1:16, 1, 16:32], f(32, 48, 1, 16), f(1, 17, 33, 48), ALU.subtract)
                v.tensor_copy(m[:, 1:16, 0, 0], xf[:, 0, 1:16])
                ts(m[:, 1:16, 1, 0], xf[:, 0, 33:48], -1.0, None, ALU.mult)
                v.tensor_copy(m[:, 0, 0, 0:16], xf[:, 0:16, 0])
                v.tensor_copy(m[:, 0, 0, 16:32], xf[:, 1:17, 0])
                ts(m[:, 0, 1, 1:16], xf[:, 32:47, 0], -1.0, None, ALU.mult)
                v.tensor_copy(m[:, 0, 1, 16:32], xf[:, 32:48, 0])
                link(v.memset(m[:, 0, 1, 0:1], 0.0))
                v.memset(xf[:, 0, 0:1], 0.0).then_inc(xf_ready.sem, 1)
                link_done(v.tensor_copy(sbc[:, :], V(VU("sbc"))[:, 0:N]), VU("sbc"))
                link(ts(xc, xcg, scol, None, ALU.mult))
                link(v.tensor_copy(xc[:, 0:1], sm[:, 8:9]))
                link(ts(plane(xs)[:, :, 0, :], plane(xc)[:, :, 1, :], -1.0, None, ALU.mult))
                v.tensor_copy(plane(xs)[:, :, 1, :], plane(xc)[:, :, 0, :]).then_inc(xc_ready.sem, 1)
                dve.wait_ge(act_done.sem, act_done.emptied(b, AU("xct", 1)))
                link(v.memset(xct[32:33, 0:N], DC))
                v.memset(xst[0:1, 0:N], -DC).then_inc(low_ready.sem, 1)
                dve.wait_ge(low_ready.sem, low_ready.at(b, 1))
                tiles4 = lambda ap: ap.rearrange("p (c t) -> p c t", t=N)
                for h in range(HEADS):
                    if h == 5:
                        dve.wait_ge(vec_full.sem, vec_full.full(b, VU("sc", 0)))
                    elif h >= 2:
                        dve.wait_ge(rh_used.sem, rh_used.at(b, h - 1 - (h > 5)))
                    link(tt(tiles4(rh[h % 2]), tiles4(xct), bc(chunks(mrt[:, :])[:, :, h], 2, N), ALU.mult))
                    dve.wait_ge(rh_t2.sem, rh_t2.at(b, h + 1))
                    tt(rh[h % 2], rh[h % 2], t2[h % 2][:, 0:512], ALU.add).then_inc(rh_ready.sem, 1)
                dve.wait_ge(vec_full.sem, vec_full.full(b, VU("gram")))
                link_done(ts(gram[:, :], V(VU("gram"))[:, 0:N], scol, None, ALU.mult), VU("gram"))
                link(tt(gram[:, :], gram[:, :], sbc[:, :], ALU.mult))
                sc8 = tiles4(sc)
                link(tt(sc8, bc(gram[:, :], 1, HEADS), bc(wsum[:, :], 2, N), ALU.mult))
                for u in range(2):
                    dve.wait_ge(vec_full.sem, vec_full.full(b, VU("sc", u)))
                    at = slice(512 * u, 512 * u + 512)
                    link_done(tt(sc[:, at], sc[:, at], V(VU("sc", u))[:, :], ALU.add), VU("sc", u))
                link(red(sm[:, 20:28], sc8, AX.X, ALU.max))
                tt(sc8, sc8, bc(sm[:, 20:28], 2, N), ALU.subtract).then_inc(score_ready.sem, 1)
                dve.wait_ge(exp_ready.sem, exp_ready.at(b, 1))
                link(red(sm[:, 20:28], sc8, AX.X, ALU.add))
                link(v.reciprocal(sm[:, 20:28], sm[:, 20:28]))
                tt(tiles4(prob), sc8, bc(sm[:, 20:28], 2, N), ALU.mult).then_inc(prob_ready.sem, 1)
                for h in range(HEADS):
                    dve.wait_ge(cri_in[h % 2].sem, cri_in[h % 2].at(b, 16 * (h // 2 + 1)))
                    if h >= 2:
                        dve.wait_ge(wh_used.sem, wh_used.at(b, h - 1))
                    link(tt(plane(wh[h % 2]), plane(xc), bc(cri[h % 2][:, 0:512].rearrange("p (y k) -> p y k", k=KX), 2, 2), ALU.mult))
                    link(ts(wh[h % 2][:, 0:1], wh[h % 2][:, 0:1], ccol[:, h:h + 1], None, ALU.add))
                    dve.wait_ge(wh_t2.sem, wh_t2.at(b, h + 1))
                    tt(wh[h % 2], wh[h % 2], t2[h % 2], ALU.add).then_inc(wh_ready.sem, 1)
                    if h == 1:
                        dve.wait_ge(act_done.sem, act_done.emptied(b, AU("pt", 1)))
                        link(tt(sc8, tiles4(pt), bc(vsum, 2, N), ALU.mult))
                        link(red(at_[:, :], sc8.rearrange("p h t -> p t h"), AX.X, ALU.add))
                        stt(bt[:, :], at_[:, :], scol, ident, ALU.mult, ALU.add).then_inc(bt_ready.sem, 1)
                for u in range(2):
                    dve.wait_ge(vec_full.sem, vec_full.full(b, VU("u", u)))
                    at = slice(512 - 512 * u, 1024 - 512 * u)
                    link_done(v.tensor_copy(ul[:, at], V(VU("u", u))[:, :]), VU("u", u))
                for u in range(2):
                    dve.wait_ge(vec_full.sem, vec_full.full(b, VU("fy", u)))
                    at = slice(512 * u, 512 * u + 512)
                    tt(fy[:, at], V(VU("fy", u))[:, :], ul[:, at], ALU.add).then_inc(vec_done.sem, 1)
                inverse(0)

                def statistics(src, unit):
                    for g in range(TILES):
                        dve.wait_ge(act_done.sem, act_done.emptied(b, unit(g)))
                        ins = v.bn_stats(bn[:, 6 * g:6 * g + 6], src[:, TILE * g:TILE * g + TILE])
                    link(ins)
                    v.memset(gs[:, 100:101], 0.0)
                    link(v.bn_aggr(sm[:, 18:20], bn[:, :]))

                statistics(big1, lambda g: AU("y", g))
                v.tensor_copy(root[:, 0:1], sm[:, 19:20]).then_inc(root_ask.sem, 1)
                inverse_root(sm[:, 28:29], 1)
                ay, by, a0, b0 = sm[:, 28:29], sm[:, 29:30], sm[:, 32:33], sm[:, 33:34]
                link(tt(ay, ay, B("anw"), ALU.mult))
                link(tt(by, ay, sm[:, 18:19], ALU.mult))
                link(tt(by, B("anb"), by, ALU.subtract))
                link(tt(sm[:, 34:35], ay, ay, ALU.mult))
                tt(root[:, 0:1], sm[:, 34:35], sm[:, 19:20], ALU.mult).then_inc(root_ask.sem, 1)
                inverse_root(a0, 1)
                link(tt(a0, a0, ay, ALU.mult))
                link(tt(a0, a0, W("n2w"), ALU.mult))
                link(tt(b0, a0, sm[:, 18:19], ALU.mult))
                link(tt(b0, W("n2b"), b0, ALU.subtract))
                link(ts(m1s[:, :], W("skip")[:, 0:N], a0, None, ALU.mult))
                link(ts(sm[:, 35:36], b0, DC, None, ALU.mult))
                link(ts(diag[:, 0:N], ident, a0, None, ALU.mult))
                link(ts(diag[:, N:2 * N], ident, sm[:, 35:36], None, ALU.mult))
                ts(diag[:, 2 * N:3 * N], W("skip")[:, 0:N], sm[:, 35:36], None, ALU.mult).then_inc(rows_ready.sem, 1)
                n = VU("rows")
                dve.wait_ge(vec_full.sem, vec_full.full(b, n))
                link(tt(tiles4(hc), tiles4(fy), bc(V(n)[:, 0:N], 1, CH), ALU.mult))
                link(tt(crow[0:1, 0:N], V(n)[0:1, 2 * N:3 * N], vc[0:1, VEC["mixsb"].start:VEC["mixsb"].start + N], ALU.add))
                link_done(tt(hc[0:1, 0:N], hc[0:1, 0:N], V(n)[0:1, N:2 * N], ALU.add), n)

                def mix(layer):
                    w = W("mix")[:, 256 * layer:256 * layer + 128].rearrange("p (c i o) -> p c i o", c=CH, i=4)
                    src = hc.rearrange("p (c g i) -> p c g i", c=CH, i=4)
                    for i in range(4):
                        dst = (tmp if i else acc).rearrange("p (c g o) -> p c g o", c=CH, o=4)
                        link(tt(dst, bc(src[:, :, :, i], 3, 4), bc(w[:, :, i, :], 2, 32), ALU.mult))
                        if i:
                            link(tt(acc, acc, tmp, ALU.add))
                    dve.wait_ge(poolmix.sem, poolmix.at(b, layer + 1))
                    link(tt(oc, acc, accp, ALU.add))
                    tt(osq, oc, oc, ALU.mult).then_inc(osq_ready.sem, 1)
                    n = VU(f"var{layer}")
                    dve.wait_ge(vec_full.sem, vec_full.full(b, n))
                    v.tensor_copy(root[:, :], V(n)[:, 0:N]).then_inc(vec_done.sem, 1)
                    inverse_root(tq[:, :], N)
                    link(tt(tiles4(oc), tiles4(oc), bc(tq[:, :], 1, CH), ALU.mult))
                    row = crow[0:1, 0:N] if layer == 0 else vc[0:1, VEC["mixsb"].start + N:VEC["mixsb"].stop]
                    v.tensor_copy(oc[0:1, 0:N], row).then_inc(oc_ready.sem, 1)
                    inverse(layer + 1)

                mix(0)
                for g in range(TILES):
                    dve.wait_ge(vec_full.sem, vec_full.full(b, VU("h1t", g)))
                    v.tensor_copy(h1w[:, TILE * (g % 4):TILE * (g % 4) + TILE], V(VU("h1t", g))[:, :]).then_inc(vec_done.sem, 1)
                for u in range(4):
                    dve.wait_ge(vec_full.sem, vec_full.full(b, VU("zh", u)))
                    v.tensor_copy(zb[:, TILE * (2 * u + 1):TILE * (2 * u + 2)], V(VU("zh", u))[:, :]).then_inc(vec_done.sem, 1)
                for u in range(2):
                    dve.wait_ge(vec_full.sem, vec_full.full(b, VU("hc", u)))
                    link_done(v.tensor_copy(hc[:, 512 * u:512 * u + 512], V(VU("hc", u))[:, :]), VU("hc", u))
                mix(1)
                statistics(big2, lambda g: AU("p2", g))
                v.tensor_copy(root[:, 0:1], sm[:, 19:20]).then_inc(root_ask.sem, 1)
                a2, b2 = sm[:, 30:31], sm[:, 31:32]
                inverse_root(a2, 1)
                link(tt(a2, a2, W("monw"), ALU.mult))
                link(tt(b2, a2, sm[:, 18:19], ALU.mult))
                link(tt(b2, W("monb"), b2, ALU.subtract))
                tt(b2, b2, by, ALU.add).then_inc(coef2_ready.sem, 1)

                for g in range(TILES + 3):
                    if g < TILES:
                        j, at = g // 4, slice(TILE * g, TILE * g + TILE)
                        if g % 4 == 0:
                            dve.wait_ge(xr_in[j % 2].sem, xr_in[j % 2].at(b, 16 * (j // 2 + 1)))
                        stt(big1[:, at], big1[:, at], ay, xr[j % 2][:, TILE * (g % 4):TILE * (g % 4) + TILE],
                            ALU.mult, ALU.add).then_inc(x2_half.sem, 1)
                    if g >= 3:
                        k = g - 3
                        dve.wait_ge(act_done.sem, act_done.emptied(b, AU("x2t", k)))
                        ins = v.bn_stats(bn[:, 6 * k:6 * k + 6], big1[:, TILE * k:TILE * k + TILE])
                link(ins)
                v.memset(gs[:, 100:101], 0.0)
                link(v.bn_aggr(sm[:, 40:42], bn[:, :]))
                link(tt(sm[:, 42:43], sm[:, 40:41], sm[:, 40:41], ALU.mult))
                tt(sm[:, 41:42], sm[:, 41:42], sm[:, 42:43], ALU.add).then_inc(gn2_ready.sem, 1)
                n = VU("gn2")
                dve.wait_ge(vec_full.sem, vec_full.full(b, n))
                link_done(v.tensor_copy(sm[:, 44:46], V(n)[:, 0:2]), n)
                link(tt(sm[:, 46:47], sm[:, 44:45], sm[:, 44:45], ALU.mult))
                tt(root[:, 0:1], sm[:, 45:46], sm[:, 46:47], ALU.subtract).then_inc(root_ask.sem, 1)
                inverse_root(sm[:, 47:48], 1)
                link(ts(wabs[:, :], W("wab"), sm[:, 47:48], None, ALU.mult))
                link(ts(wgs[:, :], W("wg"), sm[:, 47:48], None, ALU.mult))
                ts(sm[:, 48:49], sm[:, 44:45], -1.0, None, ALU.mult).then_inc(w2_ready.sem, 1)
                n = VU("bias")
                dve.wait_ge(vec_full.sem, vec_full.full(b, n))
                link(tt(sm[:, 50:51], V(n)[:, 2:3], W("bg"), ALU.add))
                link_done(tt(sm[:, 51:53], V(n)[:, 0:2], W("bab"), ALU.add), n)
                for k in range(8 + 2):
                    if k < 8:
                        n = aby_unit(k)
                        dve.wait_ge(vec_full.sem, vec_full.full(b, n))
                        dve.wait_ge(act_done.sem, act_done.emptied(b, AU("abx", k)))
                        if k >= 2:
                            dve.wait_ge(vec_full.sem, vec_full.full(b, abt_unit(k - 2)))
                        stt(prods[k % 2], V(n)[:, :], sm[:, 52:53], firsts[k % 2], ALU.add, ALU.mult)\
                            .then_inc(vec_done.sem, 1)
                    if k >= 2:
                        n = abt_unit(k - 2)
                        dve.wait_ge(vec_full.sem, vec_full.full(b, n))
                        dst = abt[:, :, 16 * (k - 2):16 * (k - 2) + 16].rearrange("p n (j l) -> p l j n", l=4)
                        v.tensor_copy(dst, V(n)[:, :].rearrange("p (l j n) -> p l j n", l=4, j=4)).then_inc(vec_done.sem, 1)
                for u in range(4):
                    n = VU("z", u)
                    dve.wait_ge(vec_full.sem, vec_full.full(b, n))
                    link_done(v.tensor_copy(z[:, 4 * u:4 * u + 4, :], V(n)[:, :].rearrange("p (c j) -> p c j", j=N)), n)
                link(red(tq[:, :], z.rearrange("p c j -> p j c"), AX.X, ALU.add))
                link(ts(tq[:, :], tq[:, :], 1.0 / C, None, ALU.mult))
                link(tt(z, z, bc(tq[:, :], 1, C), ALU.subtract))
                zsq = z2.rearrange("p (c j) -> p c j", j=N)
                link(tt(zsq, z, z, ALU.mult))
                link(red(tu[:, :], zsq.rearrange("p c j -> p j c"), AX.X, ALU.add))
                ts(root[:, :], tu[:, :], 1.0 / C, None, ALU.mult).then_inc(root_ask.sem, 1)
                inverse_root(tq[:, :], N)
                tt(z2.rearrange("p (j c) -> p c j", c=C), z, bc(tq[:, :], 1, C), ALU.mult).then_inc(zn_ready.sem, 1)
                for g in range(TILES + 1):
                    if g < TILES:
                        dve.wait_ge(vec_full.sem, vec_full.full(b, zz_unit(g)))
                        dve.wait_ge(act_done.sem, act_done.emptied(b, AU("g", g)))
                        stt(ow[g % 2], V(zz_unit(g))[:, :], sm[:, 9:10], gt[g % 2], ALU.add, ALU.mult).then_inc(vec_done.sem, 1)
                    if g >= 1:
                        n, at = back_unit(g - 1), slice(TILE * (g - 1), TILE * g)
                        dve.wait_ge(vec_full.sem, vec_full.full(b, n))
                        tt(big2[:, at], big2[:, at], V(n)[:, :], ALU.add).then_inc(vec_done.sem, 1)
                assert steps[0] == DVE_STEPS, ("DVE_STEPS", steps[0])


def constants():
    n, k31, ky = np.arange(N), np.arange(1, 32), np.arange(KY)

    def cos(k):
        return np.cos(2 * np.pi * (np.outer(n, np.atleast_1d(k)) % N) / N)

    def sin(k):
        return np.sin(2 * np.pi * (np.outer(n, np.atleast_1d(k)) % N) / N)

    lx = np.where(KX_ORDER == 0, L0, L1)
    ly = np.where(ky == 0, L0, L1)
    t = {}
    t["fh"] = np.concatenate([L0 * cos(0), L1 * cos(k31), L1 * sin(k31), L0 * cos(32), L0 * sin(32)], 1) / N
    t["fw"] = np.concatenate([L0 * cos(0), L1 * cos(k31), L0 * cos(32), L1 * sin(k31),
                              0 * cos(0), L1 * sin(k31), L0 * sin(32), -L1 * cos(k31)], 1) / N
    c, s = cos(KX_ORDER), sin(KX_ORDER)
    step = np.stack([np.stack([c.T, s.T], 1), np.stack([-s.T, c.T], 1)]) / lx[None, :, None, None]
    inv1 = np.zeros((2, 2, 2, KX, 2, 2, N))
    for y in range(2):
        inv1[:, y, :, :, y] = step
    inv1[0, 0, :, KX - 1, 0] *= 2
    t["inv1"] = inv1.reshape(2, N, 512).transpose(1, 0, 2).reshape(N, 1024)
    weight = (np.where(ky == 0, 1.0, 2.0) / ly)[:, None]
    inv2 = np.zeros((4, 2, KY, 4, N))
    for j in range(4):
        inv2[j, 0, :, j], inv2[j, 1, :, j] = cos(ky).T * weight, -sin(ky).T * weight
    t["inv2"] = inv2.reshape(N, 512)
    t["f2w"] = np.stack([cos(ky) * ly, -sin(ky) * ly], 2).reshape(N, 32) / N
    f2h = np.zeros((N, 2, 2, 2, 2, KX))
    for y in range(2):
        f2h[:, y, 0, y, 0], f2h[:, y, 0, y, 1] = c * lx, -s * lx
        f2h[:, y, 1, y, 0], f2h[:, y, 1, y, 1] = s * lx, c * lx
    t["f2h"] = f2h.reshape(N, 512) / N
    swap = np.zeros((2, 2, KX, 2, 2, KX))
    for y in range(2):
        swap[y, 1, :, y, 0], swap[y, 0, :, y, 1] = -np.eye(KX), np.eye(KX)
    t["swap"] = swap.reshape(N, N)
    varw = np.zeros((2, 2, 2, KX))
    varw[:] = 2 / (lx * L1) ** 2
    varw[0, 0] = 1 / (lx * L0) ** 2
    varw[0, 0, :, KX - 1] *= 2
    varw[0, 0, :, 0] = 0
    t["varw"] = np.repeat(varw.reshape(2, N).T, N, 1)
    t["ident"], t["ones"] = np.eye(N), np.ones((N, N))
    t["quad"] = np.kron(np.eye(N // 4), np.full((4, 4), 0.25))
    t["rho"] = np.tile(np.where(KX_ORDER == 0, 1.0, 0.5), 4)[:, None]
    return np.concatenate([t[name].reshape(N, size) for name, size in CONST_PARTS], 1).astype(np.float32)


def on_modes(w):
    m1, m2 = w.shape[-2:]
    out = np.zeros((2,) + w.shape[:-2] + (KY, KX), w.dtype)
    for i, k in enumerate(KX_ORDER):
        for r, q in enumerate((k, -k)):
            if -(m1 // 2) <= q < m1 // 2:
                out[r][..., :m2, i] = w[..., q % m1, :]
    return out


def chunked(w):
    v = np.stack([w, w], -2)
    return np.moveaxis(v.reshape(w.shape[:-2] + (CH, N)), (-1, -2), (0, 1))


def lay_out(i):
    l0 = {k[8:]: np.asarray(v) for k, v in i.items() if k.startswith("L0_conv_")}
    l1 = {k[8:]: np.asarray(v) for k, v in i.items() if k.startswith("L1_conv_")}
    f = np.float32
    cols = np.zeros((N, COL_N), f)

    def put(name, a):
        cols[:, COL[name]] = a.reshape(N, -1)

    for name, a in (("n2w", "norm2_w"), ("n2b", "norm2_b"), ("monw", "mon_w"), ("monb", "mon_b")):
        put(name, np.tile(l0[a], N // 4))
    put("bz", l1["bz"])
    put("bg", l1["bg"])
    put("lng", np.tile(l1["ln2_g"], N // C))
    put("lnb", np.tile(l1["ln2_b"], N // C))
    kq = [chunked(on_modes(l0[a][0:2, 0])[r])[:, 0:4] for a in ("kqv_wr", "kqv_wi") for r in range(2)]
    put("kq", np.stack(kq, 1).transpose(0, 1, 3, 2, 4))
    mix = np.stack([on_modes(l0["mix_wr"]), on_modes(l0["mix_wi"])])
    mixed = chunked(mix)
    put("mix", mixed[:, :, :, 0].transpose(0, 3, 2, 1, 4, 5))
    put("mixrev", mixed[:, 0, :, 1].transpose(0, 2, 1, 3, 4))
    skip, wz = np.zeros((N, 2, N), f), np.zeros((N, 8, N), f)
    for g in range(N // 4):
        for layer in range(2):
            skip[4 * g:4 * g + 4, layer, 4 * g:4 * g + 4] = l0["mix_sw"][layer].T
    for j in range(8):
        wz[C * j:C * j + C, j] = l1["Wz"]
    put("skip", skip)
    put("wz", wz)
    put("wg", l1["Wg"])
    put("wab", np.concatenate([l1[k] for k in 4 * ("Wa1", "Wb1") + 4 * ("Wa2", "Wb2")], 1))
    put("bab", np.stack([np.concatenate([l1[k] for k in 4 * pair]) for pair in (("ba1", "bb1"), ("ba2", "bb2"))], 1))
    vec = {"sw": l0["kqv_sw"], "sb": l0["kqv_sb"], "bias": l0["kqv_bias"], "psw": l0["p_sw"], "n1w": l0["norm1_w"],
           "n1b": l0["norm1_b"], "pbias": l0["p_bias"], "psb": l0["p_sb"], "anw": l0["attn_norm_w"],
           "anb": l0["attn_norm_b"], "pdc": l0["p_wr"][:, 0, 0, 0], "mixsb": np.tile(l0["mix_sb"], (1, N // 4))}
    vec = np.concatenate([vec[name].reshape(1, n) for name, n in VEC_PARTS], 1)
    modes = [on_modes(a) for a in (l0["p_wr"][:, 0], l0["p_wi"][:, 0], l0["kqv_wr"][2, 0], l0["kqv_wi"][2, 0])]
    proj = np.concatenate([m[0].reshape(HEADS, 512) for m in modes] + [m[1][:, 0] for m in modes]
                          + [l0["kqv_sw"][2].reshape(HEADS, 1), l0["p_sw"].reshape(HEADS, 1)], 1)
    return cols, vec, proj


def kernel(**inputs):
    import concourse.bacc as bacc
    from concourse.bass_utils import run_bass_kernel_spmd as run

    nc = bacc.Bacc("TRN2", target_bir_lowering=False, num_devices=1)
    cols, vec, proj = lay_out(inputs)
    arrays = {"x": np.ascontiguousarray(inputs["x"]), "const": constants(), "cols": cols, "vec": vec, "proj": proj}
    aps = [nc.dram_tensor(k, a.shape, F32, kind="ExternalInput").ap() for k, a in arrays.items()]
    tables = nc.dram_tensor("head_tables", (HEADS, 1024), F32, kind="Internal").ap()
    out = nc.dram_tensor("out", (BATCH, N, N, N), F32, kind="ExternalOutput").ap()
    build(nc, *aps, tables, out)
    return run(nc, [arrays], core_ids=[0]).results[0]["out"]
```

```python
from contextlib import ExitStack

import numpy as np

import concourse.bass as bass
from concourse import mybir

F32 = mybir.dt.float32
ALU = mybir.AluOpType
ACT = mybir.ActivationFunctionType
AX = mybir.AxisListType

BATCH = 2
N = 128
HW = N * N
HEADS = 8
KX, KY = 32, 16
CH = 8
TILE = 512
TILES = HW // TILE
C = 16
EPS = 1e-5
L0, L1 = 8.0, float(np.sqrt(128.0))
DC = L0 * L0
KX_ORDER = np.concatenate([np.arange(0, 16), -np.arange(1, 17)])

CONST_PARTS = [("fh", 128), ("fw", 128), ("inv1", 1024), ("inv2", 512), ("f2w", 32), ("f2h", 512),
               ("swap", 128), ("varw", 256), ("ident", 128), ("ones", 128), ("quad", 128), ("rho", 1), ("pair", 2)]
COL_PARTS = [("n2w", 1), ("n2b", 1), ("monw", 1), ("monb", 1), ("lng", 1),
             ("lnb", 1), ("kq", 256), ("mix", 512), ("mixrev", 64), ("skip", 256),
             ("wz", 256), ("wg", 128), ("wab", 256), ("bab", 2)]
VEC_PARTS = [("sw", 24), ("sb", 24), ("bias", 24), ("psw", 8), ("n1w", 1), ("n1b", 1), ("pbias", 1),
             ("psb", 1), ("anw", 1), ("anb", 1), ("pdc", 8), ("mixsb", 256), ("bg", 128), ("bz", 256)]


def spans(parts):
    at, out = 0, {}
    for name, n in parts:
        out[name] = slice(at, at + n)
        at += n
    return out, at


CONST, CONST_N = spans(CONST_PARTS)
COL, COL_N = spans(COL_PARTS)
VEC, VEC_N = spans(VEC_PARTS)


def inverse_rows(za, c):
    return za[:, :].rearrange("p (h r k) -> p k r h", r=2, k=KY)[:, 2 * c:2 * c + 2]


LEAD = 16


def features(za, u):
    return za[:, TILE * u:TILE * u + TILE].rearrange("p (j s b) -> p s j b", j=2, s=4)


class Units:

    def __init__(self, parts):
        self.at, self.n = {}, 0
        for name, n in parts:
            self.at[name] = self.n
            self.n += n
        assert self.n % 4 == 0, self.n

    def __call__(self, name, k=0):
        return self.at[name] + k


AU = Units([("st1", 32), ("st2", 8), ("xft", 4), ("xct", 2), ("pt", 2), ("inv0", 8), ("y", 32),
            ("swap0", 2), ("inv1", 8), ("p1", 48), ("zh", 4), ("swap1", 2), ("inv2", 8), ("p2", 32),
            ("x2t", 32), ("abx", 8), ("af", 4), ("lead", LEAD), ("znt", 4), ("zz", 32)])
VU = Units([("s1t", 1), ("sum", 2), ("sbc", 1), ("xft", 4), ("gram", 1), ("sc", 2), ("u", 2), ("fy", 2), ("inv0", 8),
            ("rows", 2), ("var0", 1), ("inv1", 8), ("h1t", 32), ("zh", 4), ("hc", 2), ("var1", 1),
            ("inv2", 8), ("gn2", 1), ("bias", 2), ("ab", 16), ("z", 4), ("gate", TILES - LEAD)])


def first_pass():
    order = []
    for g in range(TILES + 4):
        if g < TILES:
            order.append(("tile", g))
        if g >= 5 and g % 4 == 1:
            order.append(("fw", (g - 5) // 4))
        if g >= 7 and g % 4 == 3:
            order.append(("zf", (g - 7) // 4))
    return order


FIRST_PASS = first_pass()


def p1_unit(kind, k):
    return AU("p1", FIRST_PASS.index((kind, k)))


def added_by_dve(g):
    return (g + 1) // 3


def aby_unit(k):
    return VU("ab", k + max(0, k - 2))


def abt_unit(k):
    return VU("ab", min(k + 2, 7) + k + 1)


def tile_rows(image, g):
    at = 2048 * (g // 4)
    return image[:, at:at + 2048].rearrange("p (e q n) -> p e q n", e=2, q=4)[:, :, g % 4, :]


class Signal:

    def __init__(self, nc, ctx, name, per):
        self.sem, self.per = ctx.enter_context(nc.semaphore(name)), per

    def at(self, b, n):
        return b * self.per + n

    def full(self, b, unit):
        return b * self.per + unit + 1

    def free(self, b, unit):
        return b * self.per + unit + 1

    def emptied(self, b, unit):
        return b * self.per + unit + 5


def bc(ap, axis, n):
    v = ap.unsqueeze(axis)
    shape = list(v.shape)
    shape[axis] = n
    return v.to_broadcast(shape)


DVE_STEPS = 129
POOL_STEPS = 20


def build(nc, x, const, cols, vec, proj, kernels_dram, out):
    ctx = ExitStack()
    with ctx:
        def sb(name, n, parts=N):
            return ctx.enter_context(nc.sbuf_tensor(name, [parts, n], F32))

        def sig(name, per):
            return Signal(nc, ctx, name, per)

        big1, big2 = sb("big1", HW), sb("big2", HW)
        za, zb = sb("za", 4096), sb("zb", 4096)
        cst, col, vc = sb("cst", CONST_N), sb("col", COL_N), sb("vc", VEC_N)

        def K(name):
            return cst[:, CONST[name]]

        def W(name):
            return col[:, COL[name]]

        def B(name):
            return vc[:, VEC[name]]

        ident, ones = K("ident"), K("ones")
        inv1, f2h = K("inv1"), K("f2h")

        yw = big2[:, 0:8320].rearrange("p (a t) -> p a t", t=N)
        xh = [big2[:, 8320 + 1024 * s:9344 + 1024 * s].rearrange("p (t w) -> p t w", w=N) for s in range(4)]
        s2p = za[:, 0:2048].rearrange("p (j w) -> p j w", w=N)

        def part(n, size=1024):
            return big2[:, 1024 * n:1024 * n + size]

        xcg, xc, xs = part(0), part(1), part(2)
        xct, xst = part(3, 512), part(4, 512)
        rh = [part(5, 512), big2[:, 5632:6144]]
        t2 = [part(6), part(7)]
        sc, prob, pt = part(8), part(9), part(10)
        wh = [part(11), part(12)]
        ul, fy = part(13), part(14)
        cri = [part(15), part(3)]
        hc, hs, acc, tmp = (za[:, 1024 * i:1024 * i + 1024] for i in range(4))
        accp, tmpp, oc, osq = (zb[:, 1024 * i:1024 * i + 1024] for i in range(4))
        abt = za[:, :].rearrange("p (n h) -> p n h", h=N)
        bf, af = za[:, 2048:4096], zb[:, 0:2048]
        firsts = [zb[:, 2048 + 512 * i:2560 + 512 * i] for i in range(2)]
        prods = [zb[:, 3072 + 512 * i:3584 + 512 * i] for i in range(2)]
        z = za[:, 0:2048].rearrange("p (c n) -> p c n", n=N)
        z2 = zb[:, 2048:4096]
        znt = za[:, 0:2048].rearrange("p (j i) -> p j i", i=N)
        zz = [zb[:, 512 * i:512 * i + 512] for i in range(4)]
        xr = [za[:, 0:2048], za[:, 2048:4096]]

        h1w = sb("h1w", 4 * TILE)
        fwr = sb("fwr", 2 * TILE)
        sq = [h1w[:, 0:1024], h1w[:, 1024:2048]]
        s12, mr_bc, root = sb("s12", 256), sb("mr_bc", 256), sb("root", 128)
        fws, gram, sbc, tq, tu = (sb(n, m) for n, m in (("fws", 128), ("gram", 128), ("sbc", 128), ("tq", 128), ("tu", 128)))
        at_, bt, dmat, m1s = (sb(n, 128) for n in ("at", "bt", "dmat", "m1s"))
        diag, crow = sb("diag", 384), sb("crow", 128)
        gs, sm = sb("gs", 128), sb("sm", 64)
        bn = sb("bn", TILES * 6)
        wabs, wgs, wzs, bgs = sb("wabs", 256), sb("wgs", 128), sb("wzs", 256), sb("bgs", 128)
        mrt, mit, ccol, wsum = sb("mrt", 32), sb("mit", 32), sb("ccol", 8), sb("wsum", 8)
        pj, crt = big1[0:HEADS, 1024:3202], big1[0:HEADS, 4096:5120]

        banks_a = [ctx.enter_context(nc.psum_tensor(f"bank_a{i}", [N, TILE], F32)) for i in range(4)]
        banks_v = [ctx.enter_context(nc.psum_tensor(f"bank_v{i}", [N, TILE], F32)) for i in range(4)]

        def A(n):
            return banks_a[n % 4]

        def V(n):
            return banks_v[n % 4]

        loaded = sig("loaded", 0)
        set_dve, set_lnb, set_pe, set_crt, set_step = (sig(n, 0) for n in ("set_dve", "set_lnb", "set_pe", "set_crt", "set_step"))
        act_full, act_done = sig("act_full", AU.n), sig("act_done", AU.n)
        vec_full, vec_done = sig("vec_full", VU.n), sig("vec_done", VU.n)
        dve_step, pool_step = sig("dve_step", DVE_STEPS), sig("pool_step", POOL_STEPS)
        root_ask, root_got = sig("root_ask", 7), sig("root_got", 9)
        x_in = [sig(f"x_in{j}", 16) for j in range(8)]
        xh_in = [sig(f"xh_in{s}", 64) for s in range(4)]
        squared, square_used = sig("squared", 16), sig("square_used", 16)
        sums_ready, gn_ready, fw_ready, diag_ready = (sig(n, 1) for n in ("sums_ready", "gn_ready", "fw_ready", "diag_ready"))
        gx_ready = sig("gx_ready", 8)
        xf_ready, xc_ready, low_ready = (sig(n, 1) for n in ("xf_ready", "xc_ready", "low_ready"))
        rh_t2, rh_ready, rh_used = sig("rh_t2", 8), sig("rh_ready", 8), sig("rh_used", 6)
        score_ready, exp_ready, prob_ready, bt_ready = (sig(n, 1) for n in ("score_ready", "exp_ready", "prob_ready", "bt_ready"))
        cri_in = [sig(f"cri_in{s}", 64) for s in range(2)]
        wh_t2, wh_ready, wh_used = sig("wh_t2", 8), sig("wh_ready", 8), sig("wh_used", 7)
        rows_ready, poolmix, osq_ready, oc_ready = sig("rows_ready", 1), sig("poolmix", 2), sig("osq_ready", 2), sig("oc_ready", 2)
        coef2_ready, x2_half, scaled, x2_pool, x2_dve, stored = sig("coef2_ready", 1), sig("x2_half", TILES), sig("scaled", TILES - added_by_dve(TILES - 1)), sig("x2_pool", TILES - added_by_dve(TILES - 1)), sig("x2_dve", added_by_dve(TILES - 1)), sig("stored", 128)
        xr_in = [sig(f"xr_in{s}", 64) for s in range(2)]
        gn2_ready, w2_ready, ab_ready = sig("gn2_ready", 1), sig("w2_ready", 1), sig("ab_ready", 8)
        zn_ready, biased, gated, weighed, out_ready = sig("zn_ready", 1), sig("biased", LEAD), sig("gated", TILES), sig("weighed", TILES), sig("out_ready", TILES)

        block = ctx.enter_context(nc.Block())

        @block.sync
        def _(sync):
            def load_rows(b, k):
                sync.dma_start(big1[:, 2048 * k:2048 * k + 2048],
                               x[b, :, 16 * k:16 * k + 16].rearrange("t h w -> t (h w)")).then_inc(x_in[k].sem, 16)

            sync.dma_start(cst[:, :], const).then_inc(loaded.sem, 16)
            sync.dma_start(col[:, :], cols).then_inc(loaded.sem, 16)
            sync.dma_start(vc[:, :], vec.to_broadcast([N, VEC_N])).then_inc(loaded.sem, 16)
            sync.dma_start(pj, proj).then_inc(loaded.sem, 16)
            sync.wait_ge(set_crt.sem, 1)
            sync.dma_start(kernels_dram, crt).then_inc(stored.sem, 16)
            sync.wait_ge(stored.sem, 16)
            for b in range(BATCH):
                for j in range(16):
                    if j >= 4:
                        sync.wait_ge(act_done.sem, act_done.emptied(b, AU("st1", 2 * j - 7)))
                    sync.dma_start(xh[j % 4], x[b, 8 * j:8 * j + 8].rearrange("t h w -> h t w"))\
                        .then_inc(xh_in[j % 4].sem, 16)
                    if b == 0 and j % 2 == 1:
                        load_rows(b, j // 2)
                for h in range(HEADS):
                    if h >= 2:
                        sync.wait_ge(wh_ready.sem, wh_ready.at(b, h - 1))
                        sync.wait_ge(wh_t2.sem, wh_t2.at(b, h - 1))
                    else:
                        sync.wait_ge(vec_done.sem, vec_done.emptied(b, VU("sc", 1)))
                    sync.dma_start(cri[h % 2], kernels_dram[h:h + 1, :].to_broadcast([N, 1024]))\
                        .then_inc(cri_in[h % 2].sem, 16)
                for j in range(8):
                    if j < 2:
                        sync.wait_ge(vec_full.sem, vec_full.full(b, VU("inv2", 7)))
                    else:
                        sync.wait_ge(x2_half.sem, x2_half.at(b, 4 * (j - 1)))
                    sync.dma_start(xr[j % 2], x[b, :, 16 * j:16 * j + 16].rearrange("t h w -> t (h w)"))\
                        .then_inc(xr_in[j % 2].sem, 16)
                for j in range(8):
                    sync.wait_ge(out_ready.sem, out_ready.at(b, 4 * (j + 1)))
                    sync.dma_start(out[b, :, 16 * j:16 * j + 16].rearrange("t h w -> t (h w)"),
                                   big2[:, 2048 * j:2048 * j + 2048]).then_inc(stored.sem, 16)
                    if b + 1 < BATCH:
                        load_rows(b + 1, j)
                sync.wait_ge(stored.sem, stored.at(b + 1, 16))

        @block.tensor
        def _(pe):
            mm, tr = nc.tensor.matmul, nc.tensor.transpose

            pe.wait_ge(loaded.sem, 64)
            pe.wait_ge(set_lnb.sem, 1)
            mm(banks_v[0][:, 0:256], m1s[:, :], W("wz"), start=True, stop=True).then_inc(set_pe.sem, 1)
            pe.wait_ge(set_dve.sem, 1)

            with pe.Fori(0, BATCH) as b:
                def inverse(k, coef):
                    for c in range(CH):
                        u = c // 2
                        bank = V(VU(f"inv{k}", u)) if c % 2 else A(AU(f"inv{k}", u))
                        if c % 2:
                            pe.wait_ge(vec_done.sem, vec_done.free(b, VU(f"inv{k}", u)))
                        else:
                            pe.wait_ge(act_done.sem, act_done.free(b, AU(f"inv{k}", u)))
                        mm(bank[:, :], coef[:, N * c:N * c + N], inv1[:, 512 * (c > 0):512 * (c > 0) + 512],
                           start=True, stop=True).then_inc(vec_full.sem if c % 2 else act_full.sem, 1)
                    pe.wait_ge(act_done.sem, act_done.emptied(b, AU(f"inv{k}", 3)))
                    pe.wait_ge(vec_done.sem, vec_done.emptied(b, VU(f"inv{k}", 3)))
                    for q in range(8):
                        u = 4 + q // 2
                        bank = V(VU(f"inv{k}", u)) if q % 2 else A(AU(f"inv{k}", u))
                        if q % 2:
                            pe.wait_ge(vec_done.sem, vec_done.free(b, VU(f"inv{k}", u)))
                        else:
                            pe.wait_ge(act_done.sem, act_done.free(b, AU(f"inv{k}", u)))
                        for j in range(4):
                            g = 4 * q + j
                            last = tr(bank[:, N * j:N * j + N], za[:, N * g:N * g + N], ident)
                        last.then_inc(vec_full.sem if q % 2 else act_full.sem, 1)
                    pe.wait_ge(act_done.sem, act_done.emptied(b, AU(f"inv{k}", 7)))
                    pe.wait_ge(vec_done.sem, vec_done.emptied(b, VU(f"inv{k}", 7)))

                def tile(unit, weights, image, g):
                    pe.wait_ge(act_done.sem, act_done.free(b, unit))
                    mm(A(unit)[:, :], weights, image[:, TILE * g:TILE * g + TILE], start=True, stop=False)
                    mm(A(unit)[:, :], zb[:, N * g:N * g + N], K("inv2"), start=False, stop=True)\
                        .then_inc(act_full.sem, 1)

                for q in range(16):
                    pe.wait_ge(xh_in[q % 4].sem, xh_in[q % 4].at(b, 16 * (q // 4 + 1)))
                    for r in range(2):
                        n = AU("st1", 2 * q + r)
                        pe.wait_ge(act_done.sem, act_done.free(b, n))
                        for j in range(4):
                            last = mm(A(n)[:, N * j:N * j + N], xh[q % 4][:, 4 * r + j, :], K("fh"),
                                      start=True, stop=True)
                        last.then_inc(act_full.sem, 1)

                n = VU("s1t")
                pe.wait_ge(act_done.sem, act_done.emptied(b, AU("st1", 31)))
                pe.wait_ge(vec_done.sem, vec_done.free(b, n))
                tr(V(n)[:, 0:N], yw[:, 0, :], ident).then_inc(vec_full.sem, 1)
                for k in range(2):
                    n = VU("sum", k)
                    if k:
                        pe.wait_ge(sums_ready.sem, sums_ready.at(b, 1))
                    else:
                        pe.wait_ge(vec_done.sem, vec_done.emptied(b, VU("s1t")))
                    pe.wait_ge(vec_done.sem, vec_done.free(b, n))
                    mm(V(n)[:, 0:N], ones, s12[:, N * k:N * k + N], start=True, stop=True).then_inc(vec_full.sem, 1)

                pe.wait_ge(fw_ready.sem, fw_ready.at(b, 1))
                for u in range(8):
                    n = AU("st2", u)
                    pe.wait_ge(act_done.sem, act_done.free(b, n))
                    for j in range(2):
                        a = 8 * u + 4 * j
                        o = A(n)[64 * j:64 * j + 64, :]
                        if a < 60:
                            last = mm(o, fws[:, 0:64], yw[:, a:a + 4, :], start=True, stop=True)
                        else:
                            mm(o[:, 0:3 * N], fws[:, 0:64], yw[:, 60:63, :], start=True, stop=True)
                            mm(o[:, 3 * N:4 * N], fws[:, 0:64], yw[:, 63, :], start=True, stop=False)
                            last = mm(o[:, 3 * N:4 * N], fws[:, 64:128], yw[:, 64, :], start=False, stop=True)
                    last.then_inc(act_full.sem, 1)

                n = VU("sbc")
                pe.wait_ge(diag_ready.sem, diag_ready.at(b, 1))
                pe.wait_ge(vec_done.sem, vec_done.free(b, n))
                mm(V(n)[:, 0:N], ones, diag[:, 0:N], start=True, stop=True).then_inc(vec_full.sem, 1)

                for u in range(8):
                    pe.wait_ge(act_done.sem, act_done.emptied(b, AU("st2", u)))
                    n = VU("xft", u // 2) if u % 2 else AU("xft", u // 2)
                    if u % 2:
                        pe.wait_ge(vec_done.sem, vec_done.free(b, n))
                    else:
                        pe.wait_ge(act_done.sem, act_done.free(b, n))
                    bank = V(n) if u % 2 else A(n)
                    for k in range(4):
                        c = 4 * u + k
                        last = tr(bank[:, N * k:N * k + N], zb[:, N * c:N * c + N], ident)
                    last.then_inc(vec_full.sem if u % 2 else act_full.sem, 1)
                n = VU("gram")
                pe.wait_ge(xf_ready.sem, xf_ready.at(b, 1))
                pe.wait_ge(vec_done.sem, vec_done.free(b, n))
                for c in range(32):
                    last = mm(V(n)[:, 0:N], zb[:, N * c:N * c + N], zb[:, N * c:N * c + N], start=c == 0, stop=c == 31)
                last.then_inc(vec_full.sem, 1)

                pe.wait_ge(xc_ready.sem, xc_ready.at(b, 1))
                for u, src in enumerate((xc, xs)):
                    n = AU("xct", u)
                    pe.wait_ge(act_done.sem, act_done.free(b, n))
                    for c in range(4):
                        last = tr(A(n)[:, N * c:N * c + N], src[:, N * c:N * c + N], ident)
                    last.then_inc(act_full.sem, 1)

                pe.wait_ge(low_ready.sem, low_ready.at(b, 1))
                for h in range(HEADS):
                    n = VU("sc", h // 4)
                    if h % 4 == 0:
                        pe.wait_ge(vec_done.sem, vec_done.free(b, n))
                    pe.wait_ge(rh_ready.sem, rh_ready.at(b, h + 1))
                    for c in range(4):
                        last = mm(V(n)[:, N * (h % 4):N * (h % 4) + N], xct[:, N * c:N * c + N],
                                  rh[h % 2][:, N * c:N * c + N], start=c == 0, stop=c == 3)
                    last.then_inc(vec_full.sem if h % 4 == 3 else rh_used.sem, 1)

                pe.wait_ge(prob_ready.sem, prob_ready.at(b, 1))
                for u in range(2):
                    n = AU("pt", u)
                    pe.wait_ge(act_done.sem, act_done.free(b, n))
                    for j in range(4):
                        h = 4 * u + j
                        last = tr(A(n)[:, N * j:N * j + N], prob[:, N * h:N * h + N], ident)
                    last.then_inc(act_full.sem, 1)

                pe.wait_ge(vec_done.sem, vec_done.free(b, VU("u", 0)))
                pe.wait_ge(vec_done.sem, vec_done.free(b, VU("u", 1)))
                for h in range(HEADS):
                    if h % 4 == 0:
                        pe.wait_ge(act_done.sem, act_done.emptied(b, AU("pt", h // 4)))
                    pe.wait_ge(wh_ready.sem, wh_ready.at(b, h + 1))
                    for c in range(CH):
                        last = mm(V(VU("u", 1 - c // 4))[:, N * (c % 4):N * (c % 4) + N], wh[h % 2][:, N * c:N * c + N],
                                  pt[:, N * h:N * h + N], start=h == 0 and c % 4 == 0,
                                  stop=h == HEADS - 1 and c > 0, skip_group_check=True)
                    last.then_inc(wh_used.sem if h < HEADS - 1 else vec_full.sem, 1)
                pe.wait_ge(bt_ready.sem, bt_ready.at(b, 1))
                mm(V(VU("u", 1))[:, 0:N], dmat[:, :], at_[:, :], start=False, stop=True,
                   skip_group_check=True).then_inc(vec_full.sem, 1)
                for u in range(2):
                    n = VU("fy", u)
                    pe.wait_ge(vec_done.sem, vec_done.free(b, n))
                    for j in range(4):
                        c = 4 * u + j
                        last = mm(V(n)[:, N * j:N * j + N], xcg[:, N * c:N * c + N], bt[:, :], start=True, stop=True)
                    last.then_inc(vec_full.sem, 1)

                pe.wait_ge(vec_done.sem, vec_done.emptied(b, VU("u", 1)))
                inverse(0, ul)

                for g in range(TILES):
                    if g % 4 == 0:
                        pe.wait_ge(gx_ready.sem, gx_ready.at(b, g // 4 + 1))
                    tile(AU("y", g), bt[:, :], big1, g)

                pe.wait_ge(rows_ready.sem, rows_ready.at(b, 1))
                for k, at in enumerate((slice(0, N), slice(N, 3 * N))):
                    n = VU("rows", k)
                    pe.wait_ge(vec_done.sem, vec_done.free(b, n))
                    mm(V(n)[:, at], ones, diag[:, at], start=True, stop=True).then_inc(vec_full.sem, 1)

                def mix(layer):
                    pe.wait_ge(vec_done.sem, vec_done.emptied(b, VU("hc", 1) if layer else VU("rows", 1)))
                    for u in range(2):
                        n = AU(f"swap{layer}", u)
                        pe.wait_ge(act_done.sem, act_done.free(b, n))
                        mm(A(n)[:, :], K("swap"), hc[:, 512 * u:512 * u + 512], start=True, stop=True)\
                            .then_inc(act_full.sem, 1)
                    n = VU(f"var{layer}")
                    pe.wait_ge(osq_ready.sem, osq_ready.at(b, layer + 1))
                    pe.wait_ge(vec_done.sem, vec_done.free(b, n))
                    for c in range(CH):
                        last = mm(V(n)[:, 0:N], varw[:, N * (c > 0):N * (c > 0) + N], osq[:, N * c:N * c + N],
                                  start=c == 0, stop=c == CH - 1)
                    last.then_inc(vec_full.sem, 1)
                    pe.wait_ge(oc_ready.sem, oc_ready.at(b, layer + 1))
                    inverse(layer + 1, oc)

                varw = K("varw")
                mix(0)

                def turn(g):
                    n = VU("h1t", g)
                    pe.wait_ge(act_done.sem, act_done.emptied(b, p1_unit("tile", g)))
                    pe.wait_ge(vec_done.sem, vec_done.free(b, n))
                    for j in range(4):
                        at = TILE * g + N * j
                        last = tr(V(n)[:, N * j:N * j + N], big2[:, at:at + N], ident)
                    last.then_inc(vec_full.sem, 1)

                for g in range(TILES + 4):
                    if g < TILES:
                        tile(p1_unit("tile", g), m1s[:, :], big1, g)
                    if g >= 5 and g % 4 == 1:
                        k = (g - 5) // 4
                        n = p1_unit("fw", k)
                        pe.wait_ge(vec_done.sem, vec_done.emptied(b, VU("h1t", 4 * k + 3)))
                        pe.wait_ge(act_done.sem, act_done.free(b, n))
                        for j in range(4):
                            last = mm(A(n)[32 * j:32 * j + 32, :], K("f2w"), h1w[:, TILE * j:TILE * j + TILE],
                                      start=True, stop=True)
                        last.then_inc(act_full.sem, 1)
                    if 1 <= g <= TILES:
                        turn(g - 1)
                    if g >= 7 and g % 4 == 3:
                        k = (g - 7) // 4
                        n = p1_unit("zf", k)
                        pe.wait_ge(act_done.sem, act_done.emptied(b, p1_unit("fw", k)))
                        pe.wait_ge(act_done.sem, act_done.free(b, n))
                        for j in range(4):
                            at = TILE * (k % 2) + N * j
                            last = tr(A(n)[:, N * j:N * j + N], fwr[:, at:at + N], ident)
                        last.then_inc(act_full.sem, 1)

                for q in range(8):
                    u = q // 2
                    n = VU("zh", u) if q % 2 else AU("zh", u)
                    if q == 0:
                        pe.wait_ge(act_done.sem, act_done.emptied(b, p1_unit("zf", 7)))
                    if q % 2:
                        pe.wait_ge(vec_done.sem, vec_done.free(b, n))
                    else:
                        pe.wait_ge(act_done.sem, act_done.free(b, n))
                    bank = V(n) if q % 2 else A(n)
                    for j in range(4):
                        c = 4 * q + j
                        last = tr(bank[:, N * j:N * j + N], za[:, N * c:N * c + N], ident)
                    last.then_inc(vec_full.sem if q % 2 else act_full.sem, 1)
                pe.wait_ge(act_done.sem, act_done.emptied(b, AU("zh", 3)))
                pe.wait_ge(vec_done.sem, vec_done.emptied(b, VU("zh", 3)))
                for u in range(2):
                    n = VU("hc", u)
                    pe.wait_ge(vec_done.sem, vec_done.free(b, n))
                    for j in range(4):
                        c = 4 * u + j
                        for v in range(4):
                            r = 4 * c + v
                            last = mm(V(n)[:, N * j:N * j + N], f2h[:, N * v:N * v + N], zb[:, N * r:N * r + N],
                                      start=v == 0, stop=v == 3)
                    last.then_inc(vec_full.sem, 1)
                mix(1)

                for g in range(TILES):
                    tile(AU("p2", g), W("skip")[:, N:2 * N], big2, g)

                for g in range(TILES):
                    n = AU("x2t", g)
                    if g % 3 == 2:
                        pe.wait_ge(x2_dve.sem, x2_dve.at(b, added_by_dve(g)))
                    else:
                        pe.wait_ge(x2_pool.sem, x2_pool.at(b, g + 1 - added_by_dve(g)))
                    pe.wait_ge(act_done.sem, act_done.free(b, n))
                    for j in range(4):
                        at = TILE * g + N * j
                        last = tr(A(n)[:, N * j:N * j + N], big2[:, at:at + N], ident)
                    last.then_inc(act_full.sem, 1)

                n = VU("gn2")
                pe.wait_ge(gn2_ready.sem, gn2_ready.at(b, 1))
                pe.wait_ge(vec_done.sem, vec_done.free(b, n))
                mm(V(n)[:, 0:2], K("quad"), sm[:, 40:42], start=True, stop=True).then_inc(vec_full.sem, 1)
                n = VU("bias")
                pe.wait_ge(w2_ready.sem, w2_ready.at(b, 1))
                pe.wait_ge(vec_done.sem, vec_done.free(b, n))
                mm(V(n)[:, 0:1], wabs[:, 0:N], sm[:, 48:49], start=True, stop=True)
                mm(V(n)[:, 1:2], wabs[:, N:2 * N], sm[:, 48:49], start=True, stop=True).then_inc(vec_full.sem, 1)
                n = VU("bias", 1)
                pe.wait_ge(vec_done.sem, vec_done.free(b, n))
                mm(V(n)[:, 0:N], tq[:, :], wgs[:, :], start=True, stop=True).then_inc(vec_full.sem, 1)

                for k in range(8 + 2):
                    if k < 8:
                        n, m = AU("abx", k), aby_unit(k)
                        pe.wait_ge(act_done.sem, act_done.free(b, n))
                        for j in range(4):
                            at = TILE * (4 * k + j)
                            last = mm(A(n)[32 * j:32 * j + 32, :], wabs[:, 0:32], big1[:, at:at + TILE], start=True,
                                      stop=True)
                        last.then_inc(act_full.sem, 1)
                        pe.wait_ge(vec_done.sem, vec_done.free(b, m))
                        for j in range(4):
                            at = TILE * (4 * k + j)
                            last = mm(V(m)[32 * j:32 * j + 32, :], wabs[:, N:N + 32], big1[:, at:at + TILE], start=True,
                                      stop=True)
                        last.then_inc(vec_full.sem, 1)
                    if k >= 2:
                        m = abt_unit(k - 2)
                        pe.wait_ge(ab_ready.sem, ab_ready.at(b, k - 1))
                        pe.wait_ge(vec_done.sem, vec_done.free(b, m))
                        for j in range(4):
                            last = tr(V(m)[:, N * j:N * j + N], prods[k % 2][:, N * j:N * j + N], ident)
                        last.then_inc(vec_full.sem, 1)
                pe.wait_ge(vec_done.sem, vec_done.emptied(b, abt_unit(7)))
                for u in range(4):
                    n = AU("af", u)
                    pe.wait_ge(act_done.sem, act_done.free(b, n))
                    for j in range(4):
                        c = 4 * u + j
                        last = tr(A(n)[:, N * j:N * j + N], abt[:, c, :], ident)
                    last.then_inc(act_full.sem, 1)
                for u in range(4):
                    n = VU("z", u)
                    if u == 0:
                        pe.wait_ge(act_done.sem, act_done.emptied(b, AU("af", 3)))
                    pe.wait_ge(vec_done.sem, vec_done.free(b, n))
                    for j in range(4):
                        c = 4 * u + j
                        last = mm(V(n)[:, N * j:N * j + N], af[:, N * c:N * c + N], bf[:, N * c:N * c + N], start=True,
                                  stop=True)
                    last.then_inc(vec_full.sem, 1)

                def gate(bank, g):
                    for j in range(4):
                        at = 2048 * (g // 4) + 1024 * (j // 2) + 256 * (g % 4) + N * (j % 2)
                        last = mm(bank[:, N * j:N * j + N], big1[:, at:at + N], wgs[:, :], start=True, stop=True)
                    return last

                for g in range(LEAD):
                    n = AU("lead", g)
                    pe.wait_ge(act_done.sem, act_done.free(b, n))
                    gate(A(n), g).then_inc(act_full.sem, 1)
                pe.wait_ge(zn_ready.sem, zn_ready.at(b, 1))
                for u in range(4):
                    n = AU("znt", u)
                    pe.wait_ge(act_done.sem, act_done.free(b, n))
                    for j in range(4):
                        c = 4 * u + j
                        last = tr(A(n)[:, N * j:N * j + N], z2[:, N * c:N * c + N], ident)
                    last.then_inc(act_full.sem, 1)
                pe.wait_ge(act_done.sem, act_done.emptied(b, AU("znt", 3)))

                for k in range(TILES // 2):
                    if k < TILES - LEAD:
                        n = VU("gate", k)
                        pe.wait_ge(vec_done.sem, vec_done.free(b, n))
                        gate(V(n), LEAD + k).then_inc(vec_full.sem, 1)
                    n = AU("zz", 2 * k)
                    pe.wait_ge(act_done.sem, act_done.free(b, n + 1))
                    for e in range(2):
                        for g in range(2 * k, 2 * k + 2):
                            quarter = 32 * (g % 4)
                            last = mm(A(AU("zz", g))[:, 256 * e:256 * e + 256], znt[quarter:quarter + 32, 2 * (g // 4) + e, :],
                                      wzs[quarter:quarter + 32, :], start=True, stop=True)
                            if e:
                                last.then_inc(act_full.sem, 1)

        @block.scalar
        def _(act):
            act.wait_ge(loaded.sem, 64)
            act.wait_ge(set_dve.sem, 1)
            with act.Fori(0, BATCH) as b:
                roots = [0]

                def square_root(n, unit=None):
                    if unit is None:
                        roots[0] += 1
                        act.wait_ge(root_ask.sem, root_ask.at(b, roots[0]))
                    else:
                        act.wait_ge(vec_done.sem, vec_done.emptied(b, unit))
                    nc.scalar.activation(root[:, 0:n], root[:, 0:n], ACT.Sqrt, bias=sm[:, 63:64])\
                        .then_inc(root_got.sem, 1)

                def inverse(k):
                    for u in range(4):
                        act.wait_ge(act_full.sem, act_full.full(b, AU(f"inv{k}", u)))
                        nc.scalar.activation(inverse_rows(za, 2 * u), A(AU(f"inv{k}", u))[:, :].rearrange("p (y r h) -> p y r h", y=2, r=2), ACT.Copy).then_inc(act_done.sem, 1)
                    for u in range(4, 8):
                        act.wait_ge(act_full.sem, act_full.full(b, AU(f"inv{k}", u)))
                        q = 2 * (u - 4)
                        nc.scalar.activation(zb[:, TILE * q:TILE * q + TILE], A(AU(f"inv{k}", u))[:, :], ACT.Copy).then_inc(act_done.sem, 1)

                for j in range(16):
                    if j % 2 == 0:
                        act.wait_ge(x_in[j // 2].sem, x_in[j // 2].at(b, 16))
                    if j >= 2:
                        act.wait_ge(square_used.sem, square_used.at(b, j - 1))
                    nc.scalar.activation(sq[j % 2], big1[:, 1024 * j:1024 * j + 1024], ACT.Square)\
                        .then_inc(squared.sem, 1)
                    for u in range(2 * j, 2 * j + 2):
                        n = AU("st1", u)
                        act.wait_ge(act_full.sem, act_full.full(b, n))
                        nc.scalar.activation(yw[:, :, 4 * u:4 * u + 4].rearrange("p a t -> p t a"),
                             A(n)[:, :].rearrange("p (t a) -> p t a", t=4)[:, :, 0:65], ACT.Copy).then_inc(act_done.sem, 1)
                square_root(32)
                square_root(1)
                for u in range(8):
                    act.wait_ge(act_full.sem, act_full.full(b, AU("st2", u)))
                    nc.scalar.activation(zb[:, TILE * u:TILE * u + TILE], A(AU("st2", u))[:, :], ACT.Copy).then_inc(act_done.sem, 1)
                for u in range(4):
                    n = AU("xft", u)
                    act.wait_ge(act_full.sem, act_full.full(b, n))
                    if u == 0:
                        act.wait_ge(sums_ready.sem, sums_ready.at(b, 1))
                    nc.scalar.activation(features(za, 2 * u), A(n)[:, :].rearrange("p (s j b) -> p s j b", s=4, j=2),
                         ACT.Copy).then_inc(act_done.sem, 1)
                for u, dst in enumerate((xct, xst)):
                    act.wait_ge(act_full.sem, act_full.full(b, AU("xct", u)))
                    nc.scalar.activation(dst, A(AU("xct", u))[:, :], ACT.Copy).then_inc(act_done.sem, 1)
                act.wait_ge(score_ready.sem, score_ready.at(b, 1))
                nc.scalar.activation(sc, sc, ACT.Exp, scale=1.0 / 64).then_inc(exp_ready.sem, 1)
                for u in range(2):
                    act.wait_ge(act_full.sem, act_full.full(b, AU("pt", u)))
                    nc.scalar.activation(pt[:, TILE * u:TILE * u + TILE], A(AU("pt", u))[:, :], ACT.Copy).then_inc(act_done.sem, 1)
                inverse(0)
                for g in range(TILES):
                    act.wait_ge(act_full.sem, act_full.full(b, AU("y", g)))
                    nc.scalar.activation(big1[:, TILE * g:TILE * g + TILE], A(AU("y", g))[:, :], ACT.Copy).then_inc(act_done.sem, 1)
                square_root(1)
                square_root(1)

                def mix(layer):
                    for u in range(2):
                        act.wait_ge(act_full.sem, act_full.full(b, AU(f"swap{layer}", u)))
                        nc.scalar.activation(hs[:, TILE * u:TILE * u + TILE], A(AU(f"swap{layer}", u))[:, :], ACT.Copy).then_inc(act_done.sem, 1)
                    square_root(N, VU(f"var{layer}"))
                    inverse(layer + 1)

                mix(0)

                for kind, k in FIRST_PASS:
                    n = p1_unit(kind, k)
                    act.wait_ge(act_full.sem, act_full.full(b, n))
                    if kind == "tile":
                        dst, src, func = big2[:, TILE * k:TILE * k + TILE], A(n)[:, :], ACT.Gelu
                    elif kind == "fw":
                        dst, src, func = fwr[:, TILE * (k % 2):TILE * (k % 2) + TILE], A(n)[:, :], ACT.Copy
                    else:
                        dst = za[:, :].rearrange("p (k h) -> p h k", h=N)[:, 16 * k:16 * k + 16, :]
                        dst = dst.rearrange("p (j l) k -> p l j k", l=4)
                        src, func = A(n)[:, :].rearrange("p (l j k) -> p l j k", l=4, j=4), ACT.Copy
                    nc.scalar.activation(dst, src, func).then_inc(act_done.sem, 1)
                for u in range(4):
                    act.wait_ge(act_full.sem, act_full.full(b, AU("zh", u)))
                    nc.scalar.activation(zb[:, 2 * TILE * u:2 * TILE * u + TILE], A(AU("zh", u))[:, :], ACT.Copy).then_inc(act_done.sem, 1)
                mix(1)
                for g in range(TILES):
                    act.wait_ge(act_full.sem, act_full.full(b, AU("p2", g)))
                    nc.scalar.activation(big2[:, TILE * g:TILE * g + TILE], A(AU("p2", g))[:, :], ACT.Copy).then_inc(act_done.sem, 1)
                square_root(1)

                act.wait_ge(coef2_ready.sem, coef2_ready.at(b, 1))
                for g in range(TILES + 4):
                    if g < TILES and g % 3 < 2:
                        at = slice(TILE * g, TILE * g + TILE)
                        nc.scalar.activation(big2[:, at], big2[:, at], ACT.Identity, bias=sm[:, 31:32],
                                             scale=sm[:, 30:31]).then_inc(scaled.sem, 1)
                    if g >= 4:
                        n = AU("x2t", g - 4)
                        act.wait_ge(act_full.sem, act_full.full(b, n))
                        nc.scalar.activation(big1[:, TILE * (g - 4):TILE * (g - 4) + TILE], A(n)[:, :], ACT.Copy).then_inc(act_done.sem, 1)
                square_root(1)
                for k in range(8 + 1):
                    if k < 8:
                        n = AU("abx", k)
                        act.wait_ge(act_full.sem, act_full.full(b, n))
                        if k == 0:
                            act.wait_ge(vec_done.sem, vec_done.emptied(b, VU("bias", 1)))
                        elif k >= 2:
                            act.wait_ge(vec_done.sem, vec_done.emptied(b, aby_unit(k - 2)))
                        nc.scalar.activation(firsts[k % 2], A(n)[:, :], ACT.Identity, bias=sm[:, 51:52])\
                            .then_inc(act_done.sem, 1)
                    if k >= 1:
                        act.wait_ge(vec_done.sem, vec_done.emptied(b, aby_unit(k - 1)))
                        nc.scalar.activation(prods[(k - 1) % 2], prods[(k - 1) % 2], ACT.Sigmoid).then_inc(ab_ready.sem, 1)
                for u in range(4):
                    act.wait_ge(act_full.sem, act_full.full(b, AU("af", u)))
                    nc.scalar.activation(af[:, TILE * u:TILE * u + TILE], A(AU("af", u))[:, :], ACT.Copy).then_inc(act_done.sem, 1)
                for g in range(LEAD):
                    if g == 8:
                        square_root(N)
                    act.wait_ge(act_full.sem, act_full.full(b, AU("lead", g)))
                    nc.scalar.activation(tile_rows(big1, g), A(AU("lead", g))[:, :].rearrange("p (e n) -> p e n", e=2), ACT.Copy)\
                        .then_inc(act_done.sem, 1)
                for u in range(4):
                    act.wait_ge(act_full.sem, act_full.full(b, AU("znt", u)))
                    nc.scalar.activation(znt[:, 4 * u:4 * u + 4, :], A(AU("znt", u))[:, :].rearrange("p (j i) -> p j i", i=N),
                         ACT.Identity, bias=ones[:, 0:1]).then_inc(act_done.sem, 1)
                for g in range(TILES):
                    if g < LEAD:
                        act.wait_ge(biased.sem, biased.at(b, g + 1))
                    else:
                        act.wait_ge(vec_done.sem, vec_done.emptied(b, VU("gate", g - LEAD)))
                    nc.scalar.activation(tile_rows(big1, g), tile_rows(big1, g), ACT.Sigmoid).then_inc(gated.sem, 1)
                    act.wait_ge(act_full.sem, act_full.full(b, AU("zz", g)))
                    if g >= 4:
                        act.wait_ge(out_ready.sem, out_ready.at(b, g - 3))
                    nc.scalar.activation(zz[g % 4], A(AU("zz", g))[:, :], ACT.Copy).then_inc(act_done.sem, 1)

        @block.gpsimd
        def _(pool):
            pool.wait_ge(loaded.sem, 64)
            pool.wait_ge(set_dve.sem, 1)
            tt = nc.gpsimd.tensor_tensor
            with pool.Fori(0, BATCH) as b:
                steps = [0]

                def link(ins):
                    steps[0] += 1
                    ins.then_inc(pool_step.sem, 1)
                    pool.wait_ge(pool_step.sem, pool_step.at(b, steps[0]))

                def gx(j):
                    v = big1[:, 2048 * j:2048 * j + 2048].rearrange("p (h w) -> p h w", w=N)
                    link(tt(v, v, bc(mr_bc[:, 0:N], 1, 16), ALU.subtract))
                    tt(v, v, bc(mr_bc[:, N:2 * N], 1, 16), ALU.mult).then_inc(gx_ready.sem, 1)

                pool.wait_ge(gn_ready.sem, gn_ready.at(b, 1))
                pool.wait_ge(act_done.sem, act_done.emptied(b, AU("st1", 31)))
                for j in range(3):
                    gx(j)
                pool.wait_ge(low_ready.sem, low_ready.at(b, 1))
                for h in range(HEADS):
                    if h >= 2:
                        pool.wait_ge(rh_ready.sem, rh_ready.at(b, h - 1))
                    tt(t2[h % 2][:, 0:512].rearrange("p (c t) -> p c t", t=N), xst.rearrange("p (c t) -> p c t", t=N),
                       bc(mit[:, :].rearrange("p (c h) -> p c h", h=HEADS)[:, :, h], 2, N), ALU.mult)\
                        .then_inc(rh_t2.sem, 1)
                for h in range(HEADS):
                    pool.wait_ge(cri_in[h % 2].sem, cri_in[h % 2].at(b, 16 * (h // 2 + 1)))
                    if h >= 2:
                        pool.wait_ge(wh_ready.sem, wh_ready.at(b, h - 1))
                    elif h == 0:
                        pool.wait_ge(rh_ready.sem, rh_ready.at(b, HEADS))
                    tt(t2[h % 2].rearrange("p (y r k) -> p y r k", r=2, k=KX), xs.rearrange("p (y r k) -> p y r k", r=2, k=KX),
                       bc(cri[h % 2][:, 512:1024].rearrange("p (y k) -> p y k", k=KX), 2, 2), ALU.mult)\
                        .then_inc(wh_t2.sem, 1)
                for j in range(3, 8):
                    gx(j)

                def mix(layer):
                    w = W("mix")[:, 256 * layer + 128:256 * layer + 256].rearrange("p (c i o) -> p c i o", c=CH, i=4)
                    src = hs.rearrange("p (c g i) -> p c g i", c=CH, i=4)
                    pool.wait_ge(act_done.sem, act_done.emptied(b, AU(f"swap{layer}", 1)))
                    for i in range(4):
                        dst = (tmpp if i else accp).rearrange("p (c g o) -> p c g o", c=CH, o=4)
                        link(tt(dst, bc(src[:, :, :, i], 3, 4), bc(w[:, :, i, :], 2, 32), ALU.mult))
                        if 0 < i < 3:
                            link(tt(accp, accp, tmpp, ALU.add))
                    tt(accp, accp, tmpp, ALU.add).then_inc(poolmix.sem, 1)

                mix(0)
                mix(1)
                for g in range(TILES):
                    if g % 3 < 2:
                        at = slice(TILE * g, TILE * g + TILE)
                        pool.wait_ge(x2_half.sem, x2_half.at(b, g + 1))
                        pool.wait_ge(scaled.sem, scaled.at(b, g + 1 - added_by_dve(g)))
                        tt(big2[:, at], big2[:, at], big1[:, at], ALU.add).then_inc(x2_pool.sem, 1)
                for g in range(LEAD):
                    pool.wait_ge(act_done.sem, act_done.emptied(b, AU("lead", g)))
                    rows4 = tile_rows(big1, g).rearrange("p e (r w) -> p e r w", w=N)
                    tt(rows4, rows4, bc(bc(bgs[:, :], 1, 2), 1, 2), ALU.add).then_inc(biased.sem, 1)
                for g in range(TILES):
                    pool.wait_ge(weighed.sem, weighed.at(b, g + 1))
                    dst = tile_rows(big2, g)
                    tt(dst, dst, zz[g % 4].rearrange("p (e n) -> p e n", e=2), ALU.add).then_inc(out_ready.sem, 1)
                assert steps[0] == POOL_STEPS, ("POOL_STEPS", steps[0])

        @block.vector
        def _(dve):
            v = nc.vector
            tt, ts, stt, red = v.tensor_tensor, v.tensor_scalar, v.scalar_tensor_tensor, v.tensor_reduce
            count = [0]

            def step(ins):
                count[0] += 1
                ins.then_inc(set_step.sem, 1)
                dve.wait_ge(set_step.sem, count[0])

            v.memset(sm[:, 63:64], EPS)
            v.memset(dmat[:, :], 0.0)
            dve.wait_ge(loaded.sem, 64)
            step(tt(sm[:, 9:10], W("lnb"), W("lng"), ALU.subtract))
            ts(m1s[:, :], ones, sm[:, 9:10], None, ALU.mult).then_inc(set_lnb.sem, 1)
            kq = W("kq").rearrange("p (f g n) -> p f g n", f=4, g=2)
            for f, op in ((0, ALU.add), (2, ALU.subtract)):
                for g in range(2):
                    step(tt(kq[0:64, f, g, 0:8], kq[0:64, f, g, 0:8], kq[0:64, f + 1, g, 0:8], op))
                    step(ts(kq[0:64, f, g, 0:8], kq[0:64, f, g, 0:8], 0.5, None, ALU.mult))
            for layer in range(2):
                for f, op in ((0, ALU.add), (1, ALU.subtract)):
                    at = COL["mix"].start + 256 * layer + 128 * f
                    rv = COL["mixrev"].start + 32 * layer + 16 * f
                    step(tt(col[0:64, at:at + 16], col[0:64, at:at + 16], col[0:64, rv:rv + 16], op))
                    step(ts(col[0:64, at:at + 16], col[0:64, at:at + 16], 0.5, None, ALU.mult))
            swk, swq, swv = (B("sw")[:, 8 * i:8 * i + 8] for i in range(3))
            step(tt(B("sb"), B("sb"), B("bias"), ALU.add))
            cbk, cbq, cbv = (B("sb")[:, 8 * i:8 * i + 8] for i in range(3))
            kr, qr, ki, qi = kq[:, 0, 0, :], kq[:, 0, 1, :], kq[:, 2, 0, :], kq[:, 2, 1, :]
            chunks = lambda ap: ap.rearrange("p (c h) -> p c h", h=HEADS)
            step(tt(chunks(kr), chunks(kr), bc(swk, 1, 4), ALU.add))
            step(tt(chunks(qr), chunks(qr), bc(swq, 1, 4), ALU.add))
            step(tt(mrt[:, :], qr, kr, ALU.mult))
            step(tt(mit[:, :], qi, ki, ALU.mult))
            step(tt(mrt[:, :], mrt[:, :], mit[:, :], ALU.add))
            step(tt(wsum[:, :], swq, swk, ALU.mult))
            step(tt(chunks(mrt[:, :]), chunks(mrt[:, :]), bc(wsum[:, :], 1, 4), ALU.subtract))
            step(tt(mit[:, :], qr, ki, ALU.mult))
            step(tt(gs[:, 0:32], qi, kr, ALU.mult))
            step(tt(mit[:, :], mit[:, :], gs[:, 0:32], ALU.subtract))
            step(ts(mrt[:, :], mrt[:, :], K("rho"), None, ALU.mult))
            step(ts(mit[:, :], mit[:, :], K("rho"), None, ALU.mult))
            step(tt(mrt[0:1, 0:8], mrt[0:1, 0:8], wsum[0:1, :], ALU.add))
            step(tt(gs[0:1, 32:40], cbk[0:1, :], qr[0:1, 0:8], ALU.mult))
            step(ts(mit[0:1, 0:8], gs[0:1, 32:40], -1.0, None, ALU.mult))
            step(tt(mrt[32:33, 0:8], cbk[32:33, :], cbq[32:33, :], ALU.mult))
            step(tt(mit[32:33, 0:8], cbq[32:33, :], kr[32:33, 0:8], ALU.mult))
            step(tt(ccol[:, :], B("pdc"), B("psw"), ALU.add))
            step(tt(ccol[:, :], ccol[:, :], cbv, ALU.mult))
            step(tt(gs[:, 40:41], B("pbias"), B("psb"), ALU.add))
            step(tt(ccol[:, 0:1], ccol[:, 0:1], gs[:, 40:41], ALU.add))
            step(ts(ccol[:, :], ccol[:, :], DC, None, ALU.mult))
            vsum = sm[:, 0:8]
            step(tt(vsum, B("psw"), swv, ALU.mult))
            step(ts(sm[:, 8:9], B("n1b"), DC, None, ALU.mult))
            step(ts(B("mixsb"), B("mixsb"), DC, None, ALU.mult))
            step(ts(wzs[:, :], W("wz"), W("lng"), None, ALU.mult))
            dve.wait_ge(set_pe.sem, 1)
            step(stt(B("bz"), B("bz"), 4.0, banks_v[0][:, 0:256], ALU.mult, ALU.add))
            for k in range(2):
                at = slice(N * k, N * k + N)
                step(stt(wzs[:, at], B("bz")[:, at], K("pair")[:, k:k + 1], wzs[:, at], ALU.mult, ALU.add))
            f4 = [pj[:, 512 * i:512 * i + 512] for i in range(4)]
            for i, op in enumerate((ALU.add, ALU.subtract, ALU.add, ALU.subtract)):
                step(tt(f4[i][:, 0:KX], f4[i][:, 0:KX], pj[:, 2048 + 32 * i:2080 + 32 * i], op))
                step(ts(f4[i][:, 0:KX], f4[i][:, 0:KX], 0.5, None, ALU.mult))
            swv8, psw8 = pj[:, 2176:2177], pj[:, 2177:2178]
            cr, ci = crt[:, 0:512], crt[:, 512:1024]
            tmp8, vr8 = big1[0:8, 0:512], big1[0:8, 512:1024]
            step(ts(vr8, f4[2], swv8, None, ALU.add))
            step(tt(cr, f4[0], vr8, ALU.mult))
            step(tt(tmp8, f4[1], f4[3], ALU.mult))
            step(tt(cr, cr, tmp8, ALU.subtract))
            step(stt(cr, f4[2], psw8, cr, ALU.mult, ALU.add))
            step(tt(ci, f4[0], f4[3], ALU.mult))
            step(tt(tmp8, f4[1], vr8, ALU.mult))
            step(tt(ci, ci, tmp8, ALU.add))
            stt(ci, f4[3], psw8, ci, ALU.mult, ALU.add).then_inc(set_crt.sem, 1)
            for i in range(4):
                v.memset(gs[:, 112 + i:113 + i], 0.0).then_inc(act_done.sem, 1)
                v.memset(gs[:, 116 + i:117 + i], 0.0).then_inc(vec_done.sem, 1)
            v.memset(gs[:, 110:111], 0.0).then_inc(set_dve.sem, 1)

            with dve.Fori(0, BATCH) as b:
                steps, roots = [0], [0]

                def link(ins):
                    steps[0] += 1
                    ins.then_inc(dve_step.sem, 1)
                    dve.wait_ge(dve_step.sem, dve_step.at(b, steps[0]))

                def link_done(ins, n):
                    ins.then_inc(vec_done.sem, 1)
                    dve.wait_ge(vec_done.sem, vec_done.emptied(b, n))

                def inverse_root(dst, n):
                    roots[0] += 1
                    dve.wait_ge(root_got.sem, root_got.at(b, roots[0]))
                    link(v.reciprocal(dst, root[:, 0:n]))

                def inverse(k):
                    for u in range(4):
                        dve.wait_ge(vec_full.sem, vec_full.full(b, VU(f"inv{k}", u)))
                        v.tensor_copy(inverse_rows(za, 2 * u + 1),
                                           V(VU(f"inv{k}", u))[:, :].rearrange("p (y r h) -> p y r h", y=2, r=2)).then_inc(vec_done.sem, 1)
                    for u in range(4, 8):
                        dve.wait_ge(vec_full.sem, vec_full.full(b, VU(f"inv{k}", u)))
                        q = 2 * (u - 4) + 1
                        v.tensor_copy(zb[:, TILE * q:TILE * q + TILE], V(VU(f"inv{k}", u))[:, :]).then_inc(vec_done.sem, 1)

                for j in range(16):
                    dve.wait_ge(squared.sem, squared.at(b, j + 1))
                    red(s2p[:, j, :], sq[j % 2].rearrange("p (h w) -> p w h", w=N), AX.X, ALU.add)\
                        .then_inc(square_used.sem, 1)
                dve.wait_ge(square_used.sem, square_used.at(b, 16))
                s1, s2 = s12[:, 0:N], s12[:, N:2 * N]
                red(s2, s2p.rearrange("p j w -> p w j"), AX.X, ALU.add).then_inc(sums_ready.sem, 1)
                dve.wait_ge(vec_full.sem, vec_full.full(b, VU("s1t")))
                link_done(ts(s1, V(VU("s1t"))[:, 0:N], N / L0, None, ALU.mult), VU("s1t"))
                for k in range(2):
                    n = VU("sum", k)
                    dve.wait_ge(vec_full.sem, vec_full.full(b, n))
                    link_done(red(gs[:, 32 * k:32 * k + 32], V(n)[:, 0:N].rearrange("p (g q) -> p g q", q=4), AX.X, ALU.add), n)
                link(ts(gs[:, 0:64], gs[:, 0:64], 1.0 / (4 * HW), None, ALU.mult))
                link(tt(gs[:, 64:96], gs[:, 0:32], gs[:, 0:32], ALU.mult))
                tt(root[:, 0:32], gs[:, 32:64], gs[:, 64:96], ALU.subtract).then_inc(root_ask.sem, 1)
                mean, rstd = mr_bc[:, 0:N], mr_bc[:, N:2 * N]
                link(v.tensor_copy(mean.rearrange("p (g q) -> p g q", q=4), bc(gs[:, 0:32], 2, 4)))
                inverse_root(gs[:, 64:96], 32)
                v.tensor_copy(rstd.rearrange("p (g q) -> p g q", q=4), bc(gs[:, 64:96], 2, 4)).then_inc(gn_ready.sem, 1)
                dve.wait_ge(gn_ready.sem, gn_ready.at(b, 1))
                link(tt(tq[:, :], mean, ident, ALU.mult))
                link(red(sm[:, 10:11], tq[:, :], AX.X, ALU.add))
                link(tt(tu[:, :], rstd, ident, ALU.mult))
                link(red(sm[:, 11:12], tu[:, :], AX.X, ALU.add))
                link(ts(sm[:, 10:11], sm[:, 10:11], 128.0 / 16, None, ALU.mult))
                link(ts(fws[:, :], K("fw"), sm[:, 11:12], None, ALU.mult))
                dve.wait_ge(act_done.sem, act_done.emptied(b, AU("st1", 31)))
                ts(yw[:, 0, :], yw[:, 0, :], sm[:, 10:11], None, ALU.subtract).then_inc(fw_ready.sem, 1)
                link(stt(tq[:, :], mean, -128.0, s1, ALU.mult, ALU.add))
                link(tt(tu[:, :], s1, tq[:, :], ALU.add))
                link(tt(tu[:, :], tu[:, :], mean, ALU.mult))
                link(tt(tu[:, :], s2, tu[:, :], ALU.subtract))
                link(tt(tu[:, :], tu[:, :], rstd, ALU.mult))
                link(tt(tu[:, :], tu[:, :], rstd, ALU.mult))
                link(tt(tq[:, :], tq[:, :], rstd, ALU.mult))
                link(red(sm[:, 12:13], tq[:, :], AX.X, ALU.add))
                link(red(sm[:, 13:14], tu[:, :], AX.X, ALU.add))
                link(ts(sm[:, 12:14], sm[:, 12:14], 1.0 / HW, None, ALU.mult))
                link(tt(sm[:, 14:15], sm[:, 12:13], sm[:, 12:13], ALU.mult))
                tt(root[:, 0:1], sm[:, 13:14], sm[:, 14:15], ALU.subtract).then_inc(root_ask.sem, 1)
                inverse_root(sm[:, 15:16], 1)
                scol = sm[:, 16:17]
                link(tt(scol, sm[:, 15:16], B("n1w"), ALU.mult))
                ts(diag[:, 0:N], ident, scol, None, ALU.mult).then_inc(diag_ready.sem, 1)
                link(tt(sm[:, 17:18], scol, sm[:, 12:13], ALU.mult))
                link(tt(sm[:, 17:18], B("n1b"), sm[:, 17:18], ALU.subtract))
                link(ts(dmat[:, 0:1], sm[:, 17:18], DC, None, ALU.mult))
                dve.wait_ge(vec_full.sem, vec_full.full(b, VU("sbc")))
                link_done(v.tensor_copy(sbc[:, :], V(VU("sbc"))[:, 0:N]), VU("sbc"))

                for u in range(4):
                    n = VU("xft", u)
                    dve.wait_ge(vec_full.sem, vec_full.full(b, n))
                    if u == 0:
                        v.memset(zb[0:1, 0:N], 0.0).then_inc(xf_ready.sem, 1)
                    v.tensor_copy(features(za, 2 * u + 1), V(n)[:, :].rearrange("p (s j b) -> p s j b", s=4, j=2))\
                        .then_inc(vec_done.sem, 1)
                dve.wait_ge(vec_done.sem, vec_done.emptied(b, VU("xft", 3)))
                dve.wait_ge(act_done.sem, act_done.emptied(b, AU("xft", 3)))
                xf = za[:, :].rearrange("p (a b) -> p a b", b=64)

                def f(a0, a1, b0, b1):
                    return xf[:, a0:a1, b0:b1].rearrange("p a b -> p b a")

                plane = lambda ap: ap.rearrange("p (y r k) -> p y r k", r=2, k=KX)
                m = plane(xcg)
                tt(m[:, 1:16, 0, 1:16], f(1, 16, 1, 16), f(32, 47, 33, 48), ALU.subtract)
                stt(m[:, 1:16, 1, 1:16], f(32, 47, 1, 16), -1.0, f(1, 16, 33, 48), ALU.mult, ALU.subtract)
                tt(m[:, 1:16, 0, 16:32], f(1, 17, 1, 16), f(32, 48, 33, 48), ALU.add)
                tt(m[:, 1:16, 1, 16:32], f(32, 48, 1, 16), f(1, 17, 33, 48), ALU.subtract)
                v.tensor_copy(m[:, 1:16, 0, 0], xf[:, 0, 1:16])
                ts(m[:, 1:16, 1, 0], xf[:, 0, 33:48], -1.0, None, ALU.mult)
                v.tensor_copy(m[:, 0, 0, 0:16], xf[:, 0:16, 0])
                v.tensor_copy(m[:, 0, 0, 16:32], xf[:, 1:17, 0])
                ts(m[:, 0, 1, 1:16], xf[:, 32:47, 0], -1.0, None, ALU.mult)
                v.tensor_copy(m[:, 0, 1, 16:32], xf[:, 32:48, 0])
                link(v.memset(m[:, 0, 1, 0:1], 0.0))
                link(ts(xc, xcg, scol, None, ALU.mult))
                link(v.tensor_copy(xc[:, 0:1], sm[:, 8:9]))
                link(ts(plane(xs)[:, :, 0, :], plane(xc)[:, :, 1, :], -1.0, None, ALU.mult))
                v.tensor_copy(plane(xs)[:, :, 1, :], plane(xc)[:, :, 0, :]).then_inc(xc_ready.sem, 1)
                dve.wait_ge(act_done.sem, act_done.emptied(b, AU("xct", 1)))
                link(v.memset(xct[32:33, 0:N], DC))
                v.memset(xst[0:1, 0:N], -DC).then_inc(low_ready.sem, 1)
                dve.wait_ge(low_ready.sem, low_ready.at(b, 1))
                tiles4 = lambda ap: ap.rearrange("p (c t) -> p c t", t=N)
                for h in range(HEADS):
                    if h == 5:
                        dve.wait_ge(vec_full.sem, vec_full.full(b, VU("sc", 0)))
                    elif h >= 2:
                        dve.wait_ge(rh_used.sem, rh_used.at(b, h - 1 - (h > 5)))
                    link(tt(tiles4(rh[h % 2]), tiles4(xct), bc(chunks(mrt[:, :])[:, :, h], 2, N), ALU.mult))
                    dve.wait_ge(rh_t2.sem, rh_t2.at(b, h + 1))
                    tt(rh[h % 2], rh[h % 2], t2[h % 2][:, 0:512], ALU.add).then_inc(rh_ready.sem, 1)
                dve.wait_ge(vec_full.sem, vec_full.full(b, VU("gram")))
                link_done(ts(gram[:, :], V(VU("gram"))[:, 0:N], scol, None, ALU.mult), VU("gram"))
                link(tt(gram[:, :], gram[:, :], sbc[:, :], ALU.mult))
                sc8 = tiles4(sc)
                link(tt(sc8, bc(gram[:, :], 1, HEADS), bc(wsum[:, :], 2, N), ALU.mult))
                for u in range(2):
                    dve.wait_ge(vec_full.sem, vec_full.full(b, VU("sc", u)))
                    at = slice(512 * u, 512 * u + 512)
                    link_done(tt(sc[:, at], sc[:, at], V(VU("sc", u))[:, :], ALU.add), VU("sc", u))
                link(red(sm[:, 20:28], sc8, AX.X, ALU.max))
                tt(sc8, sc8, bc(sm[:, 20:28], 2, N), ALU.subtract).then_inc(score_ready.sem, 1)
                dve.wait_ge(exp_ready.sem, exp_ready.at(b, 1))
                link(red(sm[:, 20:28], sc8, AX.X, ALU.add))
                link(v.reciprocal(sm[:, 20:28], sm[:, 20:28]))
                tt(tiles4(prob), sc8, bc(sm[:, 20:28], 2, N), ALU.mult).then_inc(prob_ready.sem, 1)
                for h in range(HEADS):
                    dve.wait_ge(cri_in[h % 2].sem, cri_in[h % 2].at(b, 16 * (h // 2 + 1)))
                    if h >= 2:
                        dve.wait_ge(wh_used.sem, wh_used.at(b, h - 1))
                    link(tt(plane(wh[h % 2]), plane(xc), bc(cri[h % 2][:, 0:512].rearrange("p (y k) -> p y k", k=KX), 2, 2), ALU.mult))
                    link(ts(wh[h % 2][:, 0:1], wh[h % 2][:, 0:1], ccol[:, h:h + 1], None, ALU.add))
                    dve.wait_ge(wh_t2.sem, wh_t2.at(b, h + 1))
                    tt(wh[h % 2], wh[h % 2], t2[h % 2], ALU.add).then_inc(wh_ready.sem, 1)
                    if h == 1:
                        dve.wait_ge(act_done.sem, act_done.emptied(b, AU("pt", 1)))
                        link(tt(sc8, tiles4(pt), bc(vsum, 2, N), ALU.mult))
                        link(red(at_[:, :], sc8.rearrange("p h t -> p t h"), AX.X, ALU.add))
                        stt(bt[:, :], at_[:, :], scol, ident, ALU.mult, ALU.add).then_inc(bt_ready.sem, 1)
                for u in range(2):
                    dve.wait_ge(vec_full.sem, vec_full.full(b, VU("u", u)))
                    at = slice(512 - 512 * u, 1024 - 512 * u)
                    link_done(v.tensor_copy(ul[:, at], V(VU("u", u))[:, :]), VU("u", u))
                for u in range(2):
                    dve.wait_ge(vec_full.sem, vec_full.full(b, VU("fy", u)))
                    at = slice(512 * u, 512 * u + 512)
                    tt(fy[:, at], V(VU("fy", u))[:, :], ul[:, at], ALU.add).then_inc(vec_done.sem, 1)
                inverse(0)

                def statistics(src, unit, beside=None):
                    for g in range(TILES):
                        if beside:
                            beside(g)
                        dve.wait_ge(act_done.sem, act_done.emptied(b, unit(g)))
                        ins = v.bn_stats(bn[:, 6 * g:6 * g + 6], src[:, TILE * g:TILE * g + TILE])
                    link(ins)
                    v.memset(gs[:, 100:101], 0.0)
                    link(v.bn_aggr(sm[:, 18:20], bn[:, :]))

                statistics(big1, lambda g: AU("y", g))
                v.tensor_copy(root[:, 0:1], sm[:, 19:20]).then_inc(root_ask.sem, 1)
                inverse_root(sm[:, 28:29], 1)
                ay, by, a0, b0 = sm[:, 28:29], sm[:, 29:30], sm[:, 32:33], sm[:, 33:34]
                link(tt(ay, ay, B("anw"), ALU.mult))
                link(tt(by, ay, sm[:, 18:19], ALU.mult))
                link(tt(by, B("anb"), by, ALU.subtract))
                link(tt(sm[:, 34:35], ay, ay, ALU.mult))
                tt(root[:, 0:1], sm[:, 34:35], sm[:, 19:20], ALU.mult).then_inc(root_ask.sem, 1)
                inverse_root(a0, 1)
                link(tt(a0, a0, ay, ALU.mult))
                link(tt(a0, a0, W("n2w"), ALU.mult))
                link(tt(b0, a0, sm[:, 18:19], ALU.mult))
                link(tt(b0, W("n2b"), b0, ALU.subtract))
                link(ts(m1s[:, :], W("skip")[:, 0:N], a0, None, ALU.mult))
                link(ts(sm[:, 35:36], b0, DC, None, ALU.mult))
                link(ts(diag[:, 0:N], ident, a0, None, ALU.mult))
                link(ts(diag[:, N:2 * N], ident, sm[:, 35:36], None, ALU.mult))
                ts(diag[:, 2 * N:3 * N], W("skip")[:, 0:N], sm[:, 35:36], None, ALU.mult).then_inc(rows_ready.sem, 1)
                n = VU("rows")
                dve.wait_ge(vec_full.sem, vec_full.full(b, n))
                link_done(tt(tiles4(hc), tiles4(fy), bc(V(n)[:, 0:N], 1, CH), ALU.mult), n)
                n = VU("rows", 1)
                dve.wait_ge(vec_full.sem, vec_full.full(b, n))
                link(tt(crow[0:1, 0:N], V(n)[0:1, 2 * N:3 * N], vc[0:1, VEC["mixsb"].start:VEC["mixsb"].start + N], ALU.add))
                link_done(tt(hc[0:1, 0:N], hc[0:1, 0:N], V(n)[0:1, N:2 * N], ALU.add), n)

                def mix(layer):
                    w = W("mix")[:, 256 * layer:256 * layer + 128].rearrange("p (c i o) -> p c i o", c=CH, i=4)
                    src = hc.rearrange("p (c g i) -> p c g i", c=CH, i=4)
                    for i in range(4):
                        dst = (tmp if i else acc).rearrange("p (c g o) -> p c g o", c=CH, o=4)
                        link(tt(dst, bc(src[:, :, :, i], 3, 4), bc(w[:, :, i, :], 2, 32), ALU.mult))
                        if i:
                            link(tt(acc, acc, tmp, ALU.add))
                    dve.wait_ge(poolmix.sem, poolmix.at(b, layer + 1))
                    link(tt(oc, acc, accp, ALU.add))
                    tt(osq, oc, oc, ALU.mult).then_inc(osq_ready.sem, 1)
                    n = VU(f"var{layer}")
                    dve.wait_ge(vec_full.sem, vec_full.full(b, n))
                    v.tensor_copy(root[:, :], V(n)[:, 0:N]).then_inc(vec_done.sem, 1)
                    inverse_root(tq[:, :], N)
                    link(tt(tiles4(oc), tiles4(oc), bc(tq[:, :], 1, CH), ALU.mult))
                    row = crow[0:1, 0:N] if layer == 0 else vc[0:1, VEC["mixsb"].start + N:VEC["mixsb"].stop]
                    v.tensor_copy(oc[0:1, 0:N], row).then_inc(oc_ready.sem, 1)
                    inverse(layer + 1)

                mix(0)
                for g in range(TILES):
                    dve.wait_ge(vec_full.sem, vec_full.full(b, VU("h1t", g)))
                    v.tensor_copy(h1w[:, TILE * (g % 4):TILE * (g % 4) + TILE], V(VU("h1t", g))[:, :]).then_inc(vec_done.sem, 1)
                for u in range(4):
                    dve.wait_ge(vec_full.sem, vec_full.full(b, VU("zh", u)))
                    v.tensor_copy(zb[:, TILE * (2 * u + 1):TILE * (2 * u + 2)], V(VU("zh", u))[:, :]).then_inc(vec_done.sem, 1)
                for u in range(2):
                    dve.wait_ge(vec_full.sem, vec_full.full(b, VU("hc", u)))
                    link_done(v.tensor_copy(hc[:, 512 * u:512 * u + 512], V(VU("hc", u))[:, :]), VU("hc", u))
                mix(1)

                def skip(g):
                    j, at = g // 4, slice(TILE * g, TILE * g + TILE)
                    if g % 4 == 0:
                        dve.wait_ge(xr_in[j % 2].sem, xr_in[j % 2].at(b, 16 * (j // 2 + 1)))
                    stt(big1[:, at], big1[:, at], ay, xr[j % 2][:, TILE * (g % 4):TILE * (g % 4) + TILE],
                        ALU.mult, ALU.add).then_inc(x2_half.sem, 1)

                statistics(big2, lambda g: AU("p2", g), skip)
                v.tensor_copy(root[:, 0:1], sm[:, 19:20]).then_inc(root_ask.sem, 1)
                a2, b2 = sm[:, 30:31], sm[:, 31:32]
                inverse_root(a2, 1)
                link(tt(a2, a2, W("monw"), ALU.mult))
                link(tt(b2, a2, sm[:, 18:19], ALU.mult))
                link(tt(b2, W("monb"), b2, ALU.subtract))
                tt(b2, b2, by, ALU.add).then_inc(coef2_ready.sem, 1)

                dve.wait_ge(x2_half.sem, x2_half.at(b, TILES))
                dve.wait_ge(coef2_ready.sem, coef2_ready.at(b, 1))
                for g in range(TILES + 5):
                    if g < TILES and g % 3 == 2:
                        at = slice(TILE * g, TILE * g + TILE)
                        link(ts(big2[:, at], big2[:, at], a2, b2, ALU.mult, ALU.add))
                        tt(big2[:, at], big2[:, at], big1[:, at], ALU.add).then_inc(x2_dve.sem, 1)
                    if g >= 5:
                        k = g - 5
                        dve.wait_ge(act_done.sem, act_done.emptied(b, AU("x2t", k)))
                        ins = v.bn_stats(bn[:, 6 * k:6 * k + 6], big1[:, TILE * k:TILE * k + TILE])
                link(ins)
                v.memset(gs[:, 100:101], 0.0)
                link(v.bn_aggr(sm[:, 40:42], bn[:, :]))
                link(tt(sm[:, 42:43], sm[:, 40:41], sm[:, 40:41], ALU.mult))
                tt(sm[:, 41:42], sm[:, 41:42], sm[:, 42:43], ALU.add).then_inc(gn2_ready.sem, 1)
                n = VU("gn2")
                dve.wait_ge(vec_full.sem, vec_full.full(b, n))
                link_done(v.tensor_copy(sm[:, 44:46], V(n)[:, 0:2]), n)
                link(tt(sm[:, 46:47], sm[:, 44:45], sm[:, 44:45], ALU.mult))
                tt(root[:, 0:1], sm[:, 45:46], sm[:, 46:47], ALU.subtract).then_inc(root_ask.sem, 1)
                inverse_root(sm[:, 47:48], 1)
                link(ts(wabs[:, :], W("wab"), sm[:, 47:48], None, ALU.mult))
                link(ts(wgs[:, :], W("wg"), sm[:, 47:48], None, ALU.mult))
                link(ts(sm[:, 48:49], sm[:, 44:45], -1.0, None, ALU.mult))
                ts(tq[:, :], ones, sm[:, 48:49], None, ALU.mult).then_inc(w2_ready.sem, 1)
                n = VU("bias")
                dve.wait_ge(vec_full.sem, vec_full.full(b, n))
                link_done(tt(sm[:, 51:53], V(n)[:, 0:2], W("bab"), ALU.add), n)
                n = VU("bias", 1)
                dve.wait_ge(vec_full.sem, vec_full.full(b, n))
                link_done(tt(bgs[:, :], V(n)[:, 0:N], B("bg"), ALU.add), n)
                for k in range(8 + 2):
                    if k < 8:
                        n = aby_unit(k)
                        dve.wait_ge(vec_full.sem, vec_full.full(b, n))
                        dve.wait_ge(act_done.sem, act_done.emptied(b, AU("abx", k)))
                        if k >= 2:
                            dve.wait_ge(vec_full.sem, vec_full.full(b, abt_unit(k - 2)))
                        stt(prods[k % 2], V(n)[:, :], sm[:, 52:53], firsts[k % 2], ALU.add, ALU.mult)\
                            .then_inc(vec_done.sem, 1)
                    if k >= 2:
                        n = abt_unit(k - 2)
                        dve.wait_ge(vec_full.sem, vec_full.full(b, n))
                        dst = abt[:, :, 16 * (k - 2):16 * (k - 2) + 16].rearrange("p n (j l) -> p l j n", l=4)
                        v.tensor_copy(dst, V(n)[:, :].rearrange("p (l j n) -> p l j n", l=4, j=4)).then_inc(vec_done.sem, 1)
                for u in range(4):
                    n = VU("z", u)
                    dve.wait_ge(vec_full.sem, vec_full.full(b, n))
                    link_done(v.tensor_copy(z[:, 4 * u:4 * u + 4, :], V(n)[:, :].rearrange("p (c j) -> p c j", j=N)), n)
                link(red(tq[:, :], z.rearrange("p c j -> p j c"), AX.X, ALU.add))
                link(ts(tq[:, :], tq[:, :], 1.0 / C, None, ALU.mult))
                link(tt(z, z, bc(tq[:, :], 1, C), ALU.subtract))
                zsq = z2.rearrange("p (c j) -> p c j", j=N)
                link(tt(zsq, z, z, ALU.mult))
                link(red(tu[:, :], zsq.rearrange("p c j -> p j c"), AX.X, ALU.add))
                ts(root[:, :], tu[:, :], 1.0 / C, None, ALU.mult).then_inc(root_ask.sem, 1)
                inverse_root(tq[:, :], N)
                tt(z2.rearrange("p (j c) -> p c j", c=C), z, bc(tq[:, :], 1, C), ALU.mult).then_inc(zn_ready.sem, 1)
                for k in range(TILES):
                    if k % 2 == 0 and k // 2 < TILES - LEAD:
                        n = VU("gate", k // 2)
                        dve.wait_ge(vec_full.sem, vec_full.full(b, n))
                        tt(tile_rows(big1, k // 2 + LEAD).rearrange("p e (r w) -> p e r w", w=N),
                           V(n)[:, :].rearrange("p (e r w) -> p e r w", e=2, w=N), bc(bc(bgs[:, :], 1, 2), 1, 2), ALU.add)\
                            .then_inc(vec_done.sem, 1)
                    dve.wait_ge(gated.sem, gated.at(b, k + 1))
                    dve.wait_ge(act_done.sem, act_done.emptied(b, AU("zz", k)))
                    tile = zz[k % 4].rearrange("p (e n) -> p e n", e=2)
                    tt(tile, tile, tile_rows(big1, k), ALU.mult).then_inc(weighed.sem, 1)
                assert steps[0] == DVE_STEPS, ("DVE_STEPS", steps[0])


def constants():
    n, k31, ky = np.arange(N), np.arange(1, 32), np.arange(KY)

    def cos(k):
        return np.cos(2 * np.pi * (np.outer(n, np.atleast_1d(k)) % N) / N)

    def sin(k):
        return np.sin(2 * np.pi * (np.outer(n, np.atleast_1d(k)) % N) / N)

    lx = np.where(KX_ORDER == 0, L0, L1)
    ly = np.where(ky == 0, L0, L1)
    t = {}
    t["fh"] = np.concatenate([L0 * cos(0), L1 * cos(k31), L1 * sin(k31), L0 * cos(32), L0 * sin(32), np.zeros((N, 63))],
                             1) / N
    t["fw"] = np.concatenate([L0 * cos(0), L1 * cos(k31), L0 * cos(32), L1 * sin(k31),
                              0 * cos(0), L1 * sin(k31), L0 * sin(32), -L1 * cos(k31)], 1) / N
    c, s = cos(KX_ORDER), sin(KX_ORDER)
    step = np.stack([np.stack([c.T, s.T], 1), np.stack([-s.T, c.T], 1)]) / lx[None, :, None, None]
    inv1 = np.zeros((2, 2, 2, KX, 2, 2, N))
    for y in range(2):
        inv1[:, y, :, :, y] = step
    inv1[0, 0, :, KX - 1, 0] *= 2
    t["inv1"] = inv1.reshape(2, N, 512).transpose(1, 0, 2).reshape(N, 1024)
    weight = (np.where(ky == 0, 1.0, 2.0) / ly)[:, None]
    inv2 = np.zeros((4, 2, KY, 4, N))
    for j in range(4):
        inv2[j, 0, :, j], inv2[j, 1, :, j] = cos(ky).T * weight, -sin(ky).T * weight
    t["inv2"] = inv2.reshape(N, 512)
    t["f2w"] = np.stack([cos(ky) * ly, -sin(ky) * ly], 2).reshape(N, 32) / N
    f2h = np.zeros((N, 2, 2, 2, 2, KX))
    for y in range(2):
        f2h[:, y, 0, y, 0], f2h[:, y, 0, y, 1] = c * lx, -s * lx
        f2h[:, y, 1, y, 0], f2h[:, y, 1, y, 1] = s * lx, c * lx
    t["f2h"] = f2h.reshape(N, 512) / N
    swap = np.zeros((2, 2, KX, 2, 2, KX))
    for y in range(2):
        swap[y, 1, :, y, 0], swap[y, 0, :, y, 1] = -np.eye(KX), np.eye(KX)
    t["swap"] = swap.reshape(N, N)
    varw = np.zeros((2, 2, 2, KX))
    varw[:] = 2 / (lx * L1) ** 2
    varw[0, 0] = 1 / (lx * L0) ** 2
    varw[0, 0, :, KX - 1] *= 2
    varw[0, 0, :, 0] = 0
    t["varw"] = np.repeat(varw.reshape(2, N).T, N, 1)
    t["ident"], t["ones"] = np.eye(N), np.ones((N, N))
    t["quad"] = np.kron(np.eye(N // 4), np.full((4, 4), 0.25))
    t["rho"] = np.tile(np.where(KX_ORDER == 0, 1.0, 0.5), 4)[:, None]
    t["pair"] = np.kron(np.tile(np.eye(2), (4, 1)), np.ones((C, 1))) / (4 * C)
    return np.concatenate([t[name].reshape(N, size) for name, size in CONST_PARTS], 1).astype(np.float32)


def on_modes(w):
    m1, m2 = w.shape[-2:]
    out = np.zeros((2,) + w.shape[:-2] + (KY, KX), w.dtype)
    for i, k in enumerate(KX_ORDER):
        for r, q in enumerate((k, -k)):
            if -(m1 // 2) <= q < m1 // 2:
                out[r][..., :m2, i] = w[..., q % m1, :]
    return out


def chunked(w):
    v = np.stack([w, w], -2)
    return np.moveaxis(v.reshape(w.shape[:-2] + (CH, N)), (-1, -2), (0, 1))


def lay_out(i):
    l0 = {k[8:]: np.asarray(v) for k, v in i.items() if k.startswith("L0_conv_")}
    l1 = {k[8:]: np.asarray(v) for k, v in i.items() if k.startswith("L1_conv_")}
    f = np.float32
    cols = np.zeros((N, COL_N), f)

    def put(name, a):
        cols[:, COL[name]] = a.reshape(N, -1)

    for name, a in (("n2w", "norm2_w"), ("n2b", "norm2_b"), ("monw", "mon_w"), ("monb", "mon_b")):
        put(name, np.tile(l0[a], N // 4))
    put("lng", np.tile(l1["ln2_g"], N // C))
    put("lnb", np.tile(l1["ln2_b"], N // C))
    kq = [chunked(on_modes(l0[a][0:2, 0])[r])[:, 0:4] for a in ("kqv_wr", "kqv_wi") for r in range(2)]
    put("kq", np.stack(kq, 1).transpose(0, 1, 3, 2, 4))
    mix = np.stack([on_modes(l0["mix_wr"]), on_modes(l0["mix_wi"])])
    mixed = chunked(mix)
    put("mix", mixed[:, :, :, 0].transpose(0, 3, 2, 1, 4, 5))
    put("mixrev", mixed[:, 0, :, 1].transpose(0, 2, 1, 3, 4))
    skip, wz = np.zeros((N, 2, N), f), np.zeros((N, 2, N), f)
    for g in range(N // 4):
        for layer in range(2):
            skip[4 * g:4 * g + 4, layer, 4 * g:4 * g + 4] = l0["mix_sw"][layer].T
    for j in range(8):
        wz[C * j:C * j + C, j % 2] = l1["Wz"]
    put("skip", skip)
    put("wz", wz)
    put("wg", l1["Wg"])
    put("wab", np.concatenate([l1[k] for k in 4 * ("Wa1", "Wb1") + 4 * ("Wa2", "Wb2")], 1))
    put("bab", np.stack([np.concatenate([l1[k] for k in 4 * pair]) for pair in (("ba1", "bb1"), ("ba2", "bb2"))], 1))
    vec = {"sw": l0["kqv_sw"], "sb": l0["kqv_sb"], "bias": l0["kqv_bias"], "psw": l0["p_sw"], "n1w": l0["norm1_w"],
           "n1b": l0["norm1_b"], "pbias": l0["p_bias"], "psb": l0["p_sb"], "anw": l0["attn_norm_w"],
           "anb": l0["attn_norm_b"], "pdc": l0["p_wr"][:, 0, 0, 0], "mixsb": np.tile(l0["mix_sb"], (1, N // 4)),
           "bg": l1["bg"], "bz": np.tile(l1["bz"], 2)}
    vec = np.concatenate([vec[name].reshape(1, n) for name, n in VEC_PARTS], 1)
    modes = [on_modes(a) for a in (l0["p_wr"][:, 0], l0["p_wi"][:, 0], l0["kqv_wr"][2, 0], l0["kqv_wi"][2, 0])]
    proj = np.concatenate([m[0].reshape(HEADS, 512) for m in modes] + [m[1][:, 0] for m in modes]
                          + [l0["kqv_sw"][2].reshape(HEADS, 1), l0["p_sw"].reshape(HEADS, 1)], 1)
    return cols, vec, proj


def kernel(**inputs):
    import concourse.bacc as bacc
    from concourse.bass_utils import run_bass_kernel_spmd as run

    nc = bacc.Bacc("TRN2", target_bir_lowering=False, num_devices=1)
    cols, vec, proj = lay_out(inputs)
    arrays = {"x": np.ascontiguousarray(inputs["x"]), "const": constants(), "cols": cols, "vec": vec, "proj": proj}
    aps = [nc.dram_tensor(k, a.shape, F32, kind="ExternalInput").ap() for k, a in arrays.items()]
    tables = nc.dram_tensor("head_tables", (HEADS, 1024), F32, kind="Internal").ap()
    out = nc.dram_tensor("out", (BATCH, N, N, N), F32, kind="ExternalOutput").ap()
    build(nc, *aps, tables, out)
    return run(nc, [arrays], core_ids=[0]).results[0]["out"]
```

```python
from contextlib import ExitStack

import numpy as np

import concourse.bass as bass
from concourse import mybir

F32 = mybir.dt.float32
ALU = mybir.AluOpType
ACT = mybir.ActivationFunctionType
AX = mybir.AxisListType

BATCH = 2
N = 128
HW = N * N
HEADS = 8
KX, KY = 32, 16
CH = 8
TILE = 512
TILES = HW // TILE
C = 16
EPS = 1e-5
L0, L1 = 8.0, float(np.sqrt(128.0))
DC = L0 * L0
KX_ORDER = np.concatenate([np.arange(0, 16), -np.arange(1, 17)])

CONST_PARTS = [("fh", 65), ("onecol", 63), ("fw", 128), ("ident", 128), ("ones", 128), ("quad", 128), ("rho", 1),
               ("pair", 2), ("swap", 128), ("varw", 256), ("inv1", 1024), ("inv2", 512), ("f2w", 32), ("f2h", 512)]
COL_PARTS = [("n2w", 1), ("n2b", 1), ("monw", 1), ("monb", 1), ("lng", 1),
             ("lnb", 1), ("kq", 256), ("mix", 512), ("mixrev", 64), ("skip", 256),
             ("wz", 256), ("wg", 128), ("wab", 256), ("bab", 2)]
VEC_PARTS = [("sw", 24), ("sb", 24), ("bias", 24), ("psw", 8), ("n1w", 1), ("n1b", 1), ("pbias", 1),
             ("psb", 1), ("anw", 1), ("anb", 1), ("pdc", 8), ("mixsb", 256), ("bg", 128), ("bz", 256)]


def spans(parts):
    at, out = 0, {}
    for name, n in parts:
        out[name] = slice(at, at + n)
        at += n
    return out, at


CONST, CONST_N = spans(CONST_PARTS)
CONST_EARLY = CONST["swap"].start
COL, COL_N = spans(COL_PARTS)
VEC, VEC_N = spans(VEC_PARTS)


def inverse_rows(za, c):
    return za[:, :].rearrange("p (h r k) -> p k r h", r=2, k=KY)[:, 2 * c:2 * c + 2]


LEAD = 16


def features(za, u):
    return za[:, TILE * u:TILE * u + TILE].rearrange("p (j s b) -> p s j b", j=2, s=4)


class Units:

    def __init__(self, parts):
        self.at, self.n = {}, 0
        for name, n in parts:
            self.at[name] = self.n
            self.n += n
        assert self.n % 4 == 0, self.n

    def __call__(self, name, k=0):
        return self.at[name] + k


AU = Units([("st1", 32), ("st2", 8), ("xft", 4), ("xct", 2), ("pt", 2), ("inv0", 8), ("y", 32),
            ("inv1", 8), ("p1", 48), ("zh", 4), ("inv2", 8), ("p2", 32),
            ("x2t", 32), ("abx", 8), ("af", 4), ("lead", LEAD), ("znt", 4), ("zz", 32)])
VU = Units([("s2", 1), ("s12t", 1), ("sum", 1), ("sbc", 1), ("xft", 4), ("gram", 1), ("sc", 2), ("u", 2), ("fy", 2), ("inv0", 8),
            ("rows", 2), ("o0", 2), ("var0", 1), ("inv1", 8), ("h1t", 32), ("zh", 4), ("hc", 2), ("o1", 2), ("var1", 1),
            ("inv2", 8), ("gn2", 1), ("bias", 2), ("ab", 16), ("z", 4), ("gate", TILES - LEAD)])


def first_pass():
    order = []
    for g in range(TILES + 4):
        if g < TILES:
            order.append(("tile", g))
        if g >= 5 and g % 4 == 1:
            order.append(("fw", (g - 5) // 4))
        if g >= 7 and g % 4 == 3:
            order.append(("zf", (g - 7) // 4))
    return order


FIRST_PASS = first_pass()


def p1_unit(kind, k):
    return AU("p1", FIRST_PASS.index((kind, k)))


def added_by_dve(g):
    return (g + 1) // 3


def aby_unit(k):
    return VU("ab", k + max(0, k - 2))


def abt_unit(k):
    return VU("ab", min(k + 2, 7) + k + 1)


def tile_rows(image, g):
    at = 2048 * (g // 4)
    return image[:, at:at + 2048].rearrange("p (e q n) -> p e q n", e=2, q=4)[:, :, g % 4, :]


class Signal:

    def __init__(self, nc, ctx, name, per):
        self.sem, self.per = ctx.enter_context(nc.semaphore(name)), per

    def at(self, b, n):
        return b * self.per + n

    def full(self, b, unit):
        return b * self.per + unit + 1

    def free(self, b, unit):
        return b * self.per + unit + 1

    def emptied(self, b, unit):
        return b * self.per + unit + 5


def bc(ap, axis, n):
    v = ap.unsqueeze(axis)
    shape = list(v.shape)
    shape[axis] = n
    return v.to_broadcast(shape)


DVE_STEPS = 87
POOL_STEPS = 8


def build(nc, x, const, places, cols, vec, proj, kernels_dram, out):
    ctx = ExitStack()
    with ctx:
        def sb(name, n, parts=N):
            return ctx.enter_context(nc.sbuf_tensor(name, [parts, n], F32))

        def sig(name, per):
            return Signal(nc, ctx, name, per)

        big1, big2 = sb("big1", HW), sb("big2", HW)
        za, zb = sb("za", 4096), sb("zb", 4096)
        cst, col, vc = sb("cst", CONST_N), sb("col", COL_N), sb("vc", VEC_N)

        def K(name):
            return cst[:, CONST[name]]

        def W(name):
            return col[:, COL[name]]

        def B(name):
            return vc[:, VEC[name]]

        ident, ones = K("ident"), K("ones")
        inv1, f2h = K("inv1"), K("f2h")

        yw = big2[:, 0:8320].rearrange("p (a t) -> p a t", t=N)
        xh = [z_[:, at:at + 1024].rearrange("p (t w) -> p t w", w=N) for z_ in (za, zb) for at in (2048, 3072)]
        s2s = zb[:, 0:TILE]

        def part(n, size=1024):
            return big2[:, 1024 * n:1024 * n + size]

        xcg, xc, xs = part(0), part(1), part(2)
        xct, xst = part(3, 512), part(4, 512)
        rh = [big2[:, 1024 * n + 512 * i:1024 * n + 512 * i + 512] for n in (5, 10) for i in range(2)]
        t2 = [part(6), part(7), part(13), part(15), part(14)]
        rt2 = [big2[:, 6144 + 512 * i:6656 + 512 * i] for i in range(4)]
        sc, prob, pt = part(8), part(9), part(10)
        wh = [part(11), part(12), part(4), part(5)]
        ul, fy = part(13), part(14)
        cri = [z_[:, 1024 * i:1024 * i + 1024] for z_ in (za, zb) for i in range(4)]
        hc = za[:, 0:1024]
        real = [za[:, 1024 * i:1024 * i + 1024] for i in range(1, 4)] + [zb[:, 0:1024]]
        oc, osq = (zb[:, 1024 * i:1024 * i + 1024] for i in range(2))
        abt = za[:, :].rearrange("p (n h) -> p n h", h=N)
        bf, af = za[:, 2048:4096], zb[:, 0:2048]
        firsts = [zb[:, 2048 + 512 * i:2560 + 512 * i] for i in range(2)]
        prods = [zb[:, 3072 + 512 * i:3584 + 512 * i] for i in range(2)]
        z = za[:, 0:2048].rearrange("p (c n) -> p c n", n=N)
        z2 = zb[:, 2048:4096]
        znt = za[:, 0:2048].rearrange("p (j i) -> p j i", i=N)
        zz = [zb[:, 512 * i:512 * i + 512] for i in range(4)]
        xr = [za[:, 0:2048], za[:, 2048:4096]]

        h1w = sb("h1w", 4 * TILE)
        fwr = sb("fwr", 2 * TILE)
        place = fwr[:, 0:TILE]
        sq = [h1w[:, 0:1024], h1w[:, 1024:2048], za[:, 0:1024], za[:, 1024:2048]]
        imag = [zb[:, 1024 * i:1024 * i + 1024] for i in range(1, 4)] + [h1w[:, 0:1024]]
        s12, mr_bc, root = sb("s12", 256), sb("mr_bc", 256), sb("root", 128)
        fws, gram, sbc, tq, tu = (sb(n, m) for n, m in (("fws", 128), ("gram", 128), ("sbc", 128), ("tq", 128), ("tu", 128)))
        at_, bt, dmat, m1s = (sb(n, 128) for n in ("at", "bt", "dmat", "m1s"))
        diag, crow = sb("diag", 384), sb("crow", 128)
        gs, sm = sb("gs", 128), sb("sm", 64)
        bn = sb("bn", TILES * 6)
        wabs, wgs, wzs, bgs = sb("wabs", 256), sb("wgs", 128), sb("wzs", 256), sb("bgs", 128)
        mrt, mit, ccol, wsum = sb("mrt", 32), sb("mit", 32), sb("ccol", 8), sb("wsum", 8)
        pj, crt = big2[0:HEADS, 8448:10626], big2[0:HEADS, 12288:13312]
        tmp8, vr8 = big2[0:HEADS, 10752:11264], big2[0:HEADS, 11264:11776]

        banks_a = [ctx.enter_context(nc.psum_tensor(f"bank_a{i}", [N, TILE], F32)) for i in range(4)]
        banks_v = [ctx.enter_context(nc.psum_tensor(f"bank_v{i}", [N, TILE], F32)) for i in range(4)]

        def A(n):
            return banks_a[n % 4]

        def V(n):
            return banks_v[n % 4]

        loaded, late_in = sig("loaded", 0), sig("late_in", 0)
        set_lnb, set_pe, set_crt, set_step = (sig(n, 0) for n in ("set_lnb", "set_pe", "set_crt", "set_step"))
        tables_stored, place_in = sig("tables_stored", 0), sig("place_in", 16)
        act_full, act_done = sig("act_full", AU.n), sig("act_done", AU.n)
        vec_full, vec_done = sig("vec_full", VU.n), sig("vec_done", VU.n)
        dve_step, pool_step = sig("dve_step", DVE_STEPS), sig("pool_step", POOL_STEPS)
        root_ask, root_got = sig("root_ask", 7), sig("root_got", 9)
        x_in = [sig(f"x_in{j}", 16) for j in range(8)]
        xh_in = [sig(f"xh_in{s}", 64) for s in range(4)]
        squared, square_used = sig("squared", 16), sig("square_used", 7)
        gn_ready, fw_ready, diag_ready = (sig(n, 1) for n in ("gn_ready", "fw_ready", "diag_ready"))
        gx_ready = sig("gx_ready", 8)
        xf_ready, xc_ready, low_ready = (sig(n, 1) for n in ("xf_ready", "xc_ready", "low_ready"))
        rh_t2, rh_ready, rh_used = sig("rh_t2", 8), sig("rh_ready", 8), sig("rh_used", 6)
        score_ready, exp_ready, prob_ready, bt_ready = sig("score_ready", 2), sig("exp_ready", 1), sig("prob_ready", 1), sig("bt_ready", 1)
        shares_ready, rh_act, gram_ready, gram_used = sig("shares_ready", 1), sig("rh_act", 4), sig("gram_ready", 1), sig("gram_used", 2)
        cri_in = [sig(f"cri_in{h}", 16) for h in range(HEADS)]
        wh_real, wh_t2, wh_ready, wh_used = sig("wh_real", 8), sig("wh_t2", 8), sig("wh_ready", 8), sig("wh_used", 7)
        rows_ready, mixed_dve, mixed_pool, osq_ready = sig("rows_ready", 2), sig("mixed_dve", 4), sig("mixed_pool", 6), sig("osq_ready", 4)
        coef2_ready, x2_half, scaled, x2_pool, x2_dve, stored, stored_high = sig("coef2_ready", 1), sig("x2_half", TILES), sig("scaled", TILES - added_by_dve(TILES - 1)), sig("x2_pool", TILES - added_by_dve(TILES - 1)), sig("x2_dve", added_by_dve(TILES - 1)), sig("stored", 80), sig("stored_high", 48)
        xr_in = [sig(f"xr_in{s}", 64) for s in range(2)]
        gn2_ready, w2_ready, ab_ready = sig("gn2_ready", 1), sig("w2_ready", 2), sig("ab_ready", 8)
        zn_ready, biased, gated, weighed, out_ready = sig("zn_ready", 1), sig("biased", LEAD), sig("gated", TILES), sig("weighed", TILES), sig("out_ready", TILES)

        block = ctx.enter_context(nc.Block())

        @block.sync
        def _(sync):
            def load_rows(b, k):
                sync.dma_start(big1[:, 2048 * k:2048 * k + 2048],
                               x[b, :, 16 * k:16 * k + 16].rearrange("t h w -> t (h w)")).then_inc(x_in[k].sem, 16)

            def load_tokens(b, j):
                sync.dma_start(xh[j % 4], x[b, 8 * j:8 * j + 8].rearrange("t h w -> h t w")).then_inc(xh_in[j % 4].sem, 16)

            sync.dma_start(cst[:, 0:CONST_EARLY], const[:, 0:CONST_EARLY]).then_inc(loaded.sem, 16)
            sync.dma_start(col[:, :], cols).then_inc(loaded.sem, 16)
            sync.dma_start(vc[:, :], vec.to_broadcast([N, VEC_N])).then_inc(loaded.sem, 16)
            sync.dma_start(pj, proj).then_inc(loaded.sem, 16)
            for b in range(BATCH):
                for j in range(16):
                    if j >= 4:
                        sync.wait_ge(act_done.sem, act_done.emptied(b, AU("st1", 2 * j - 7)))
                        sync.wait_ge(squared.sem, squared.at(b, j - 3))
                    if j >= 4 or b == 0:
                        load_tokens(b, j)
                    if b == 0 and j == 15:
                        sync.dma_start(place, places).then_inc(place_in.sem, 16)
                        sync.dma_start(cst[:, CONST_EARLY:], const[:, CONST_EARLY:]).then_inc(late_in.sem, 16)
                for k in range(8):
                    load_rows(b, k)
                if b == 0:
                    sync.wait_ge(set_crt.sem, 1)
                    sync.dma_start(kernels_dram, crt).then_inc(tables_stored.sem, 16)
                    sync.wait_ge(tables_stored.sem, 16)
                for h in range(HEADS):
                    if h == 0:
                        sync.wait_ge(xc_ready.sem, xc_ready.at(b, 1))
                    elif h == 4:
                        sync.wait_ge(vec_full.sem, vec_full.full(b, VU("gram")))
                    sync.dma_start(cri[h], kernels_dram[h:h + 1, :].to_broadcast([N, 1024]))\
                        .then_inc(cri_in[h].sem, 16)
                for j in range(8):
                    if j < 2:
                        sync.wait_ge(vec_full.sem, vec_full.full(b, VU("inv2", 7)))
                    else:
                        sync.wait_ge(x2_half.sem, x2_half.at(b, 4 * (j - 1)))
                    sync.dma_start(xr[j % 2], x[b, :, 16 * j:16 * j + 16].rearrange("t h w -> t (h w)"))\
                        .then_inc(xr_in[j % 2].sem, 16)
                if b + 1 < BATCH:
                    sync.dma_start(place, places).then_inc(place_in.sem, 16)
                    for k in range(4):
                        if k == 0:
                            sync.wait_ge(vec_done.sem, vec_done.emptied(b, VU("z", 3)))
                        elif k == 2:
                            sync.wait_ge(act_done.sem, act_done.emptied(b, AU("znt", 3)))
                        load_tokens(b + 1, k)
                for j in range(8):
                    sync.wait_ge(out_ready.sem, out_ready.at(b, 4 * (j + 1)))
                    sync.dma_start(out[b, :, 16 * j:16 * j + 16].rearrange("t h w -> t (h w)"),
                                   big2[:, 2048 * j:2048 * j + 2048]).then_inc(stored.sem if j < 5 else stored_high.sem, 16)
            sync.wait_ge(stored.sem, stored.at(BATCH, 16))
            sync.wait_ge(stored_high.sem, stored_high.at(BATCH, 16))

        @block.tensor
        def _(pe):
            mm, tr = nc.tensor.matmul, nc.tensor.transpose

            pe.wait_ge(loaded.sem, 64)
            pe.wait_ge(set_lnb.sem, 1)
            mm(banks_v[3][:, 0:256], m1s[:, :], W("wz"), start=True, stop=True).then_inc(set_pe.sem, 1)

            with pe.Fori(0, BATCH) as b:
                def inverse(k, coef):
                    for c in range(CH):
                        u = c // 2
                        bank = V(VU(f"inv{k}", u)) if c % 2 else A(AU(f"inv{k}", u))
                        if c % 2:
                            pe.wait_ge(vec_done.sem, vec_done.free(b, VU(f"inv{k}", u)))
                        else:
                            pe.wait_ge(act_done.sem, act_done.free(b, AU(f"inv{k}", u)))
                        mm(bank[:, :], coef[:, N * c:N * c + N], inv1[:, 512 * (c > 0):512 * (c > 0) + 512],
                           start=True, stop=True).then_inc(vec_full.sem if c % 2 else act_full.sem, 1)
                    pe.wait_ge(act_done.sem, act_done.emptied(b, AU(f"inv{k}", 3)))
                    pe.wait_ge(vec_done.sem, vec_done.emptied(b, VU(f"inv{k}", 3)))
                    for q in range(8):
                        u = 4 + q // 2
                        bank = V(VU(f"inv{k}", u)) if q % 2 else A(AU(f"inv{k}", u))
                        if q % 2:
                            pe.wait_ge(vec_done.sem, vec_done.free(b, VU(f"inv{k}", u)))
                        else:
                            pe.wait_ge(act_done.sem, act_done.free(b, AU(f"inv{k}", u)))
                        for j in range(4):
                            g = 4 * q + j
                            last = tr(bank[:, N * j:N * j + N], za[:, N * g:N * g + N], ident)
                        last.then_inc(vec_full.sem if q % 2 else act_full.sem, 1)
                    pe.wait_ge(act_done.sem, act_done.emptied(b, AU(f"inv{k}", 7)))
                    pe.wait_ge(vec_done.sem, vec_done.emptied(b, VU(f"inv{k}", 7)))

                def tile(unit, weights, image, g):
                    pe.wait_ge(act_done.sem, act_done.free(b, unit))
                    mm(A(unit)[:, :], weights, image[:, TILE * g:TILE * g + TILE], start=True, stop=False)
                    mm(A(unit)[:, :], zb[:, N * g:N * g + N], K("inv2"), start=False, stop=True)\
                        .then_inc(act_full.sem, 1)

                def square_sums(k):
                    pe.wait_ge(squared.sem, squared.at(b, 2 * k + 2))
                    for j in range(4):
                        src = sq[(2 * k + j // 2) % 4][:, TILE * (j % 2):TILE * (j % 2) + TILE]
                        last = mm(V(VU("s2"))[32 * j:32 * j + 32, :], K("onecol")[:, 31 - k:63 - k], src, start=k == 0,
                                  stop=k == 7, skip_group_check=True)
                    last.then_inc(square_used.sem if k < 7 else vec_full.sem, 1)

                pe.wait_ge(vec_done.sem, vec_done.free(b, VU("s2")))
                for q in range(16):
                    pe.wait_ge(xh_in[q % 4].sem, xh_in[q % 4].at(b, 16 * (q // 4 + 1)))
                    for r in range(2):
                        n = AU("st1", 2 * q + r)
                        pe.wait_ge(act_done.sem, act_done.free(b, n))
                        for j in range(4):
                            last = mm(A(n)[:, N * j:N * j + N], xh[q % 4][:, 4 * r + j, :], cst[:, 0:N],
                                      start=True, stop=True)
                        last.then_inc(act_full.sem, 1)
                    if q % 2 == 0 and q >= 2:
                        square_sums(q // 2 - 1)
                square_sums(7)

                n = VU("s12t")
                pe.wait_ge(act_done.sem, act_done.emptied(b, AU("st1", 31)))
                pe.wait_ge(vec_done.sem, vec_done.free(b, n))
                tr(V(n)[:, 0:N], yw[:, 0, :], ident)
                pe.wait_ge(vec_done.sem, vec_done.emptied(b, VU("s2")))
                pe.wait_ge(place_in.sem, place_in.at(b, 16))
                for i in range(4):
                    last = mm(V(n)[:, N:2 * N], place[:, N * i:N * i + N], s2s[:, N * i:N * i + N], start=i == 0, stop=i == 3)
                last.then_inc(vec_full.sem, 1)
                n = VU("sum")
                pe.wait_ge(vec_done.sem, vec_done.emptied(b, VU("s12t")))
                mm(V(n)[:, 0:2 * N], ones, s12[:, :], start=True, stop=True).then_inc(vec_full.sem, 1)

                pe.wait_ge(fw_ready.sem, fw_ready.at(b, 1))
                for u in range(8):
                    n = AU("st2", u)
                    pe.wait_ge(act_done.sem, act_done.free(b, n))
                    for j in range(2):
                        a = 8 * u + 4 * j
                        o = A(n)[64 * j:64 * j + 64, :]
                        if a < 60:
                            last = mm(o, fws[:, 0:64], yw[:, a:a + 4, :], start=True, stop=True)
                        else:
                            mm(o[:, 0:3 * N], fws[:, 0:64], yw[:, 60:63, :], start=True, stop=True)
                            mm(o[:, 3 * N:4 * N], fws[:, 0:64], yw[:, 63, :], start=True, stop=False)
                            last = mm(o[:, 3 * N:4 * N], fws[:, 64:128], yw[:, 64, :], start=False, stop=True)
                    last.then_inc(act_full.sem, 1)

                n = VU("sbc")
                pe.wait_ge(diag_ready.sem, diag_ready.at(b, 1))
                pe.wait_ge(vec_done.sem, vec_done.free(b, n))
                mm(V(n)[:, 0:N], ones, diag[:, 0:N], start=True, stop=True).then_inc(vec_full.sem, 1)

                for u in range(8):
                    pe.wait_ge(act_done.sem, act_done.emptied(b, AU("st2", u)))
                    n = VU("xft", u // 2) if u % 2 else AU("xft", u // 2)
                    if u % 2:
                        pe.wait_ge(vec_done.sem, vec_done.free(b, n))
                    else:
                        pe.wait_ge(act_done.sem, act_done.free(b, n))
                    bank = V(n) if u % 2 else A(n)
                    for k in range(4):
                        c = 4 * u + k
                        last = tr(bank[:, N * k:N * k + N], zb[:, N * c:N * c + N], ident)
                    last.then_inc(vec_full.sem if u % 2 else act_full.sem, 1)

                def gram_of(chunks):
                    for c in chunks:
                        last = mm(V(VU("gram"))[:, 0:N], zb[:, N * c:N * c + N], zb[:, N * c:N * c + N], start=c == 0, stop=c == 31)
                    if c == 31:
                        last.then_inc(vec_full.sem, 1)

                pe.wait_ge(xf_ready.sem, xf_ready.at(b, 1))
                pe.wait_ge(vec_done.sem, vec_done.free(b, VU("gram")))
                gram_of(range(16))

                pe.wait_ge(xc_ready.sem, xc_ready.at(b, 1))
                for u, src in enumerate((xc, xs)):
                    n = AU("xct", u)
                    pe.wait_ge(act_done.sem, act_done.free(b, n))
                    for c in range(4):
                        last = tr(A(n)[:, N * c:N * c + N], src[:, N * c:N * c + N], ident)
                    last.then_inc(act_full.sem, 1)

                gram_of(range(16, 32))

                pe.wait_ge(low_ready.sem, low_ready.at(b, 1))
                for h in range(HEADS):
                    n = VU("sc", h // 4)
                    if h % 4 == 0:
                        pe.wait_ge(vec_done.sem, vec_done.free(b, n))
                    pe.wait_ge(rh_ready.sem, rh_ready.at(b, h + 1))
                    for c in range(4):
                        last = mm(V(n)[:, N * (h % 4):N * (h % 4) + N], xct[:, N * c:N * c + N],
                                  rh[h % 4][:, N * c:N * c + N], start=c == 0, stop=c == 3)
                    last.then_inc(vec_full.sem if h % 4 == 3 else rh_used.sem, 1)

                pe.wait_ge(prob_ready.sem, prob_ready.at(b, 1))
                for u in range(2):
                    n = AU("pt", u)
                    pe.wait_ge(act_done.sem, act_done.free(b, n))
                    for j in range(4):
                        h = 4 * u + j
                        last = tr(A(n)[:, N * j:N * j + N], prob[:, N * h:N * h + N], ident)
                    last.then_inc(act_full.sem, 1)

                pe.wait_ge(vec_done.sem, vec_done.free(b, VU("u", 0)))
                pe.wait_ge(vec_done.sem, vec_done.free(b, VU("u", 1)))
                for h in range(HEADS):
                    if h % 4 == 0:
                        pe.wait_ge(act_done.sem, act_done.emptied(b, AU("pt", h // 4)))
                    pe.wait_ge(wh_ready.sem, wh_ready.at(b, h + 1))
                    for c in range(CH):
                        last = mm(V(VU("u", 1 - c // 4))[:, N * (c % 4):N * (c % 4) + N], wh[h % 4][:, N * c:N * c + N],
                                  pt[:, N * h:N * h + N], start=h == 0 and c % 4 == 0,
                                  stop=h == HEADS - 1 and c > 0, skip_group_check=True)
                    last.then_inc(wh_used.sem if h < HEADS - 1 else vec_full.sem, 1)
                pe.wait_ge(bt_ready.sem, bt_ready.at(b, 1))
                mm(V(VU("u", 1))[:, 0:N], dmat[:, :], at_[:, :], start=False, stop=True,
                   skip_group_check=True).then_inc(vec_full.sem, 1)
                for u in range(2):
                    n = VU("fy", u)
                    pe.wait_ge(vec_done.sem, vec_done.free(b, n))
                    for j in range(4):
                        c = 4 * u + j
                        last = mm(V(n)[:, N * j:N * j + N], xcg[:, N * c:N * c + N], bt[:, :], start=True, stop=True)
                    last.then_inc(vec_full.sem, 1)

                pe.wait_ge(vec_done.sem, vec_done.emptied(b, VU("u", 1)))
                pe.wait_ge(late_in.sem, 16)
                inverse(0, ul)

                for g in range(TILES):
                    if g % 4 == 0:
                        pe.wait_ge(gx_ready.sem, gx_ready.at(b, g // 4 + 1))
                    tile(AU("y", g), bt[:, :], big1, g)

                for k, at in enumerate((slice(0, N), slice(N, 3 * N))):
                    n = VU("rows", k)
                    pe.wait_ge(rows_ready.sem, rows_ready.at(b, k + 1))
                    pe.wait_ge(vec_done.sem, vec_done.free(b, n))
                    mm(V(n)[:, at], ones, diag[:, at], start=True, stop=True).then_inc(vec_full.sem, 1)

                def mix(layer):
                    n = VU(f"o{layer}")
                    pe.wait_ge(vec_done.sem, vec_done.free(b, n + 1))
                    terms = ((imag[0], mixed_dve, 1), (imag[1], mixed_pool, 1), (imag[2], mixed_pool, 2),
                             (imag[3], mixed_pool, 3), (real[0], mixed_dve, 2))
                    for k, (term, mixed, count) in enumerate(terms):
                        pe.wait_ge(mixed.sem, mixed.at(b, (2 if mixed is mixed_dve else 3) * layer + count))
                        for u in range(2):
                            last = mm(V(n + u)[:, :], ident if mixed is mixed_dve and count > 1 else K("swap"),
                                      term[:, 512 * u:512 * u + 512], start=k == 0, stop=k == 4)
                            if k == 4:
                                last.then_inc(vec_full.sem, 1)
                    n = VU(f"var{layer}")
                    pe.wait_ge(vec_done.sem, vec_done.free(b, n))
                    for c in range(CH):
                        if c % 4 == 0:
                            pe.wait_ge(osq_ready.sem, osq_ready.at(b, 2 * layer + c // 4 + 1))
                        last = mm(V(n)[:, 0:N], varw[:, N * (c > 0):N * (c > 0) + N], osq[:, N * c:N * c + N],
                                  start=c == 0, stop=c == CH - 1)
                    last.then_inc(vec_full.sem, 1)
                    pe.wait_ge(vec_done.sem, vec_done.emptied(b, n))
                    inverse(layer + 1, oc)

                varw = K("varw")
                mix(0)

                def turn(g):
                    n = VU("h1t", g)
                    pe.wait_ge(act_done.sem, act_done.emptied(b, p1_unit("tile", g)))
                    pe.wait_ge(vec_done.sem, vec_done.free(b, n))
                    for j in range(4):
                        at = TILE * g + N * j
                        last = tr(V(n)[:, N * j:N * j + N], big2[:, at:at + N], ident)
                    last.then_inc(vec_full.sem, 1)

                for g in range(TILES + 4):
                    if g < TILES:
                        tile(p1_unit("tile", g), m1s[:, :], big1, g)
                    if g >= 5 and g % 4 == 1:
                        k = (g - 5) // 4
                        n = p1_unit("fw", k)
                        pe.wait_ge(vec_done.sem, vec_done.emptied(b, VU("h1t", 4 * k + 3)))
                        pe.wait_ge(act_done.sem, act_done.free(b, n))
                        for j in range(4):
                            last = mm(A(n)[32 * j:32 * j + 32, :], K("f2w"), h1w[:, TILE * j:TILE * j + TILE],
                                      start=True, stop=True)
                        last.then_inc(act_full.sem, 1)
                    if 1 <= g <= TILES:
                        turn(g - 1)
                    if g >= 7 and g % 4 == 3:
                        k = (g - 7) // 4
                        n = p1_unit("zf", k)
                        pe.wait_ge(act_done.sem, act_done.emptied(b, p1_unit("fw", k)))
                        pe.wait_ge(act_done.sem, act_done.free(b, n))
                        for j in range(4):
                            at = TILE * (k % 2) + N * j
                            last = tr(A(n)[:, N * j:N * j + N], fwr[:, at:at + N], ident)
                        last.then_inc(act_full.sem, 1)

                for q in range(8):
                    u = q // 2
                    n = VU("zh", u) if q % 2 else AU("zh", u)
                    if q == 0:
                        pe.wait_ge(act_done.sem, act_done.emptied(b, p1_unit("zf", 7)))
                    if q % 2:
                        pe.wait_ge(vec_done.sem, vec_done.free(b, n))
                    else:
                        pe.wait_ge(act_done.sem, act_done.free(b, n))
                    bank = V(n) if q % 2 else A(n)
                    for j in range(4):
                        c = 4 * q + j
                        last = tr(bank[:, N * j:N * j + N], za[:, N * c:N * c + N], ident)
                    last.then_inc(vec_full.sem if q % 2 else act_full.sem, 1)
                pe.wait_ge(act_done.sem, act_done.emptied(b, AU("zh", 3)))
                pe.wait_ge(vec_done.sem, vec_done.emptied(b, VU("zh", 3)))
                for u in range(2):
                    n = VU("hc", u)
                    pe.wait_ge(vec_done.sem, vec_done.free(b, n))
                    for j in range(4):
                        c = 4 * u + j
                        for v in range(4):
                            r = 4 * c + v
                            last = mm(V(n)[:, N * j:N * j + N], f2h[:, N * v:N * v + N], zb[:, N * r:N * r + N],
                                      start=v == 0, stop=v == 3)
                    last.then_inc(vec_full.sem, 1)
                mix(1)

                for g in range(TILES):
                    tile(AU("p2", g), W("skip")[:, N:2 * N], big2, g)

                for g in range(TILES):
                    n = AU("x2t", g)
                    if g % 3 == 2:
                        pe.wait_ge(x2_dve.sem, x2_dve.at(b, added_by_dve(g)))
                    else:
                        pe.wait_ge(x2_pool.sem, x2_pool.at(b, g + 1 - added_by_dve(g)))
                    pe.wait_ge(act_done.sem, act_done.free(b, n))
                    for j in range(4):
                        at = TILE * g + N * j
                        last = tr(A(n)[:, N * j:N * j + N], big2[:, at:at + N], ident)
                    last.then_inc(act_full.sem, 1)

                n = VU("gn2")
                pe.wait_ge(gn2_ready.sem, gn2_ready.at(b, 1))
                pe.wait_ge(vec_done.sem, vec_done.free(b, n))
                mm(V(n)[:, 0:2], K("quad"), sm[:, 40:42], start=True, stop=True).then_inc(vec_full.sem, 1)
                n = VU("bias")
                pe.wait_ge(w2_ready.sem, w2_ready.at(b, 1))
                pe.wait_ge(vec_done.sem, vec_done.free(b, n))
                mm(V(n)[:, 0:1], wabs[:, 0:N], sm[:, 48:49], start=True, stop=True)
                mm(V(n)[:, 1:2], wabs[:, N:2 * N], sm[:, 48:49], start=True, stop=True).then_inc(vec_full.sem, 1)
                for k in range(8 + 2):
                    if k < 8:
                        n, m = AU("abx", k), aby_unit(k)
                        pe.wait_ge(act_done.sem, act_done.free(b, n))
                        for j in range(4):
                            at = TILE * (4 * k + j)
                            last = mm(A(n)[32 * j:32 * j + 32, :], wabs[:, 0:32], big1[:, at:at + TILE], start=True,
                                      stop=True)
                        last.then_inc(act_full.sem, 1)
                        if k == 0:
                            n = VU("bias", 1)
                            pe.wait_ge(w2_ready.sem, w2_ready.at(b, 2))
                            pe.wait_ge(vec_done.sem, vec_done.free(b, n))
                            mm(V(n)[:, 0:N], tq[:, :], wgs[:, :], start=True, stop=True).then_inc(vec_full.sem, 1)
                        pe.wait_ge(vec_done.sem, vec_done.free(b, m))
                        for j in range(4):
                            at = TILE * (4 * k + j)
                            last = mm(V(m)[32 * j:32 * j + 32, :], wabs[:, N:N + 32], big1[:, at:at + TILE], start=True,
                                      stop=True)
                        last.then_inc(vec_full.sem, 1)
                    if k >= 2:
                        m = abt_unit(k - 2)
                        pe.wait_ge(ab_ready.sem, ab_ready.at(b, k - 1))
                        pe.wait_ge(vec_done.sem, vec_done.free(b, m))
                        for j in range(4):
                            last = tr(V(m)[:, N * j:N * j + N], prods[k % 2][:, N * j:N * j + N], ident)
                        last.then_inc(vec_full.sem, 1)
                pe.wait_ge(vec_done.sem, vec_done.emptied(b, abt_unit(7)))
                for u in range(4):
                    n = AU("af", u)
                    pe.wait_ge(act_done.sem, act_done.free(b, n))
                    for j in range(4):
                        c = 4 * u + j
                        last = tr(A(n)[:, N * j:N * j + N], abt[:, c, :], ident)
                    last.then_inc(act_full.sem, 1)
                for u in range(4):
                    n = VU("z", u)
                    if u == 0:
                        pe.wait_ge(act_done.sem, act_done.emptied(b, AU("af", 3)))
                    pe.wait_ge(vec_done.sem, vec_done.free(b, n))
                    for j in range(4):
                        c = 4 * u + j
                        last = mm(V(n)[:, N * j:N * j + N], af[:, N * c:N * c + N], bf[:, N * c:N * c + N], start=True,
                                  stop=True)
                    last.then_inc(vec_full.sem, 1)

                def gate(bank, g):
                    for j in range(4):
                        at = 2048 * (g // 4) + 1024 * (j // 2) + 256 * (g % 4) + N * (j % 2)
                        last = mm(bank[:, N * j:N * j + N], big1[:, at:at + N], wgs[:, :], start=True, stop=True)
                    return last

                for g in range(LEAD):
                    n = AU("lead", g)
                    pe.wait_ge(act_done.sem, act_done.free(b, n))
                    gate(A(n), g).then_inc(act_full.sem, 1)
                pe.wait_ge(zn_ready.sem, zn_ready.at(b, 1))
                for u in range(4):
                    n = AU("znt", u)
                    pe.wait_ge(act_done.sem, act_done.free(b, n))
                    for j in range(4):
                        c = 4 * u + j
                        last = tr(A(n)[:, N * j:N * j + N], z2[:, N * c:N * c + N], ident)
                    last.then_inc(act_full.sem, 1)
                pe.wait_ge(act_done.sem, act_done.emptied(b, AU("znt", 3)))

                for k in range(TILES // 2):
                    if k < TILES - LEAD:
                        n = VU("gate", k)
                        pe.wait_ge(vec_done.sem, vec_done.free(b, n))
                        gate(V(n), LEAD + k).then_inc(vec_full.sem, 1)
                    n = AU("zz", 2 * k)
                    pe.wait_ge(act_done.sem, act_done.free(b, n + 1))
                    for e in range(2):
                        for g in range(2 * k, 2 * k + 2):
                            quarter = 32 * (g % 4)
                            last = mm(A(AU("zz", g))[:, 256 * e:256 * e + 256], znt[quarter:quarter + 32, 2 * (g // 4) + e, :],
                                      wzs[quarter:quarter + 32, :], start=True, stop=True)
                            if e:
                                last.then_inc(act_full.sem, 1)

        @block.scalar
        def _(act):
            act.wait_ge(loaded.sem, 64)
            with act.Fori(0, BATCH) as b:
                roots = [0]

                def square_root(n):
                    roots[0] += 1
                    act.wait_ge(root_ask.sem, root_ask.at(b, roots[0]))
                    nc.scalar.activation(root[:, 0:n], root[:, 0:n], ACT.Sqrt, bias=sm[:, 63:64])\
                        .then_inc(root_got.sem, 1)

                def inverse(k):
                    for u in range(4):
                        act.wait_ge(act_full.sem, act_full.full(b, AU(f"inv{k}", u)))
                        nc.scalar.activation(inverse_rows(za, 2 * u), A(AU(f"inv{k}", u))[:, :].rearrange("p (y r h) -> p y r h", y=2, r=2), ACT.Copy).then_inc(act_done.sem, 1)
                    for u in range(4, 8):
                        act.wait_ge(act_full.sem, act_full.full(b, AU(f"inv{k}", u)))
                        q = 2 * (u - 4)
                        nc.scalar.activation(zb[:, TILE * q:TILE * q + TILE], A(AU(f"inv{k}", u))[:, :], ACT.Copy).then_inc(act_done.sem, 1)

                for j in range(16):
                    act.wait_ge(xh_in[j % 4].sem, xh_in[j % 4].at(b, 16 * (j // 4 + 1)))
                    if j >= 4:
                        act.wait_ge(square_used.sem, square_used.at(b, j // 2 - 1))
                    nc.scalar.activation(sq[j % 4].rearrange("p (t w) -> p t w", w=N), xh[j % 4], ACT.Square)\
                        .then_inc(squared.sem, 1)
                    for u in range(2 * j, 2 * j + 2):
                        n = AU("st1", u)
                        act.wait_ge(act_full.sem, act_full.full(b, n))
                        if u == 0:
                            act.wait_ge(stored.sem, stored.at(b, 16))
                        nc.scalar.activation(yw[:, :, 4 * u:4 * u + 4].rearrange("p a t -> p t a"),
                             A(n)[:, :].rearrange("p (t a) -> p t a", t=4)[:, :, 0:65], ACT.Copy).then_inc(act_done.sem, 1)
                square_root(32)
                square_root(1)
                for u in range(8):
                    act.wait_ge(act_full.sem, act_full.full(b, AU("st2", u)))
                    nc.scalar.activation(zb[:, TILE * u:TILE * u + TILE], A(AU("st2", u))[:, :], ACT.Copy).then_inc(act_done.sem, 1)
                for u in range(4):
                    n = AU("xft", u)
                    act.wait_ge(act_full.sem, act_full.full(b, n))
                    nc.scalar.activation(features(za, 2 * u), A(n)[:, :].rearrange("p (s j b) -> p s j b", s=4, j=2),
                         ACT.Copy).then_inc(act_done.sem, 1)
                for u, dst in enumerate((xct, xst)):
                    act.wait_ge(act_full.sem, act_full.full(b, AU("xct", u)))
                    nc.scalar.activation(dst, A(AU("xct", u))[:, :], ACT.Copy).then_inc(act_done.sem, 1)
                def real_part(h):
                    if h == 5:
                        act.wait_ge(rh_used.sem, rh_used.at(b, 2))
                    elif h == 7:
                        act.wait_ge(vec_full.sem, vec_full.full(b, VU("sc", 0)))
                    for c in range(4):
                        at = slice(N * c, N * c + N)
                        ins = nc.scalar.activation(rh[h % 4][:, at], xct[:, at], ACT.Copy, scale=mrt[:, 8 * c + h:8 * c + h + 1])
                    ins.then_inc(rh_act.sem, 1)

                def gram_part(u):
                    for h in range(4 * u, 4 * u + 4):
                        ins = nc.scalar.activation(sc[:, N * h:N * h + N], gram[:, :], ACT.Copy, scale=wsum[:, h:h + 1])
                    ins.then_inc(gram_used.sem, 1)

                act.wait_ge(low_ready.sem, low_ready.at(b, 1))
                real_part(1)
                real_part(3)
                real_part(5)
                act.wait_ge(gram_ready.sem, gram_ready.at(b, 1))
                gram_part(0)
                real_part(7)
                gram_part(1)
                for h in range(HEADS):
                    if h % 4 == 0:
                        act.wait_ge(score_ready.sem, score_ready.at(b, h // 4 + 1))
                    ins = nc.scalar.activation(sc[:, N * h:N * h + N], sc[:, N * h:N * h + N], ACT.Exp, scale=1.0 / 64,
                                               bias=sm[:, 53 + h:54 + h], accum_out=sm[:, 20 + h:21 + h])
                ins.then_inc(exp_ready.sem, 1)
                for u in range(2):
                    act.wait_ge(act_full.sem, act_full.full(b, AU("pt", u)))
                    nc.scalar.activation(pt[:, TILE * u:TILE * u + TILE], A(AU("pt", u))[:, :], ACT.Copy).then_inc(act_done.sem, 1)
                act.wait_ge(act_done.sem, act_done.emptied(b, AU("pt", 1)))
                for h in range(HEADS):
                    ins = nc.scalar.activation(sc[:, N * h:N * h + N], pt[:, N * h:N * h + N], ACT.Copy, scale=sm[:, h:h + 1])
                ins.then_inc(shares_ready.sem, 1)
                inverse(0)
                for g in range(TILES):
                    act.wait_ge(act_full.sem, act_full.full(b, AU("y", g)))
                    nc.scalar.activation(big1[:, TILE * g:TILE * g + TILE], A(AU("y", g))[:, :], ACT.Copy).then_inc(act_done.sem, 1)
                square_root(1)
                square_root(1)

                def mix(layer):
                    for u in range(2):
                        n = VU(f"o{layer}", u)
                        act.wait_ge(vec_full.sem, vec_full.full(b, n))
                        nc.scalar.activation(osq[:, 512 * u:512 * u + 512], V(n)[:, :], ACT.Square).then_inc(osq_ready.sem, 1)
                    n = VU(f"var{layer}")
                    act.wait_ge(vec_full.sem, vec_full.full(b, n))
                    nc.scalar.activation(root[:, :], V(n)[:, 0:N], ACT.Sqrt, bias=sm[:, 63:64]).then_inc(root_got.sem, 1)
                    inverse(layer + 1)

                mix(0)

                for kind, k in FIRST_PASS:
                    n = p1_unit(kind, k)
                    act.wait_ge(act_full.sem, act_full.full(b, n))
                    if kind == "tile":
                        dst, src, func = big2[:, TILE * k:TILE * k + TILE], A(n)[:, :], ACT.Gelu
                    elif kind == "fw":
                        dst, src, func = fwr[:, TILE * (k % 2):TILE * (k % 2) + TILE], A(n)[:, :], ACT.Copy
                    else:
                        dst = za[:, :].rearrange("p (k h) -> p h k", h=N)[:, 16 * k:16 * k + 16, :]
                        dst = dst.rearrange("p (j l) k -> p l j k", l=4)
                        src, func = A(n)[:, :].rearrange("p (l j k) -> p l j k", l=4, j=4), ACT.Copy
                    nc.scalar.activation(dst, src, func).then_inc(act_done.sem, 1)
                for u in range(4):
                    act.wait_ge(act_full.sem, act_full.full(b, AU("zh", u)))
                    nc.scalar.activation(zb[:, 2 * TILE * u:2 * TILE * u + TILE], A(AU("zh", u))[:, :], ACT.Copy).then_inc(act_done.sem, 1)
                mix(1)
                for g in range(TILES):
                    act.wait_ge(act_full.sem, act_full.full(b, AU("p2", g)))
                    nc.scalar.activation(big2[:, TILE * g:TILE * g + TILE], A(AU("p2", g))[:, :], ACT.Copy).then_inc(act_done.sem, 1)
                square_root(1)

                act.wait_ge(coef2_ready.sem, coef2_ready.at(b, 1))
                for g in range(TILES + 4):
                    if g < TILES and g % 3 < 2:
                        at = slice(TILE * g, TILE * g + TILE)
                        nc.scalar.activation(big2[:, at], big2[:, at], ACT.Identity, bias=sm[:, 31:32],
                                             scale=sm[:, 30:31]).then_inc(scaled.sem, 1)
                    if g >= 4:
                        n = AU("x2t", g - 4)
                        act.wait_ge(act_full.sem, act_full.full(b, n))
                        nc.scalar.activation(big1[:, TILE * (g - 4):TILE * (g - 4) + TILE], A(n)[:, :], ACT.Copy).then_inc(act_done.sem, 1)
                square_root(1)
                for k in range(8 + 1):
                    if k < 8:
                        n = AU("abx", k)
                        act.wait_ge(act_full.sem, act_full.full(b, n))
                        if k == 0:
                            act.wait_ge(vec_done.sem, vec_done.emptied(b, VU("bias")))
                        elif k >= 2:
                            act.wait_ge(vec_done.sem, vec_done.emptied(b, aby_unit(k - 2)))
                        nc.scalar.activation(firsts[k % 2], A(n)[:, :], ACT.Identity, bias=sm[:, 51:52])\
                            .then_inc(act_done.sem, 1)
                    if k >= 1:
                        act.wait_ge(vec_done.sem, vec_done.emptied(b, aby_unit(k - 1)))
                        nc.scalar.activation(prods[(k - 1) % 2], prods[(k - 1) % 2], ACT.Sigmoid).then_inc(ab_ready.sem, 1)
                for u in range(4):
                    act.wait_ge(act_full.sem, act_full.full(b, AU("af", u)))
                    nc.scalar.activation(af[:, TILE * u:TILE * u + TILE], A(AU("af", u))[:, :], ACT.Copy).then_inc(act_done.sem, 1)
                for g in range(LEAD):
                    if g == 8:
                        square_root(N)
                    act.wait_ge(act_full.sem, act_full.full(b, AU("lead", g)))
                    nc.scalar.activation(tile_rows(big1, g), A(AU("lead", g))[:, :].rearrange("p (e n) -> p e n", e=2), ACT.Copy)\
                        .then_inc(act_done.sem, 1)
                for u in range(4):
                    act.wait_ge(act_full.sem, act_full.full(b, AU("znt", u)))
                    nc.scalar.activation(znt[:, 4 * u:4 * u + 4, :], A(AU("znt", u))[:, :].rearrange("p (j i) -> p j i", i=N),
                         ACT.Identity, bias=ones[:, 0:1]).then_inc(act_done.sem, 1)
                for g in range(TILES):
                    if g < LEAD:
                        act.wait_ge(biased.sem, biased.at(b, g + 1))
                    else:
                        act.wait_ge(vec_done.sem, vec_done.emptied(b, VU("gate", g - LEAD)))
                    nc.scalar.activation(tile_rows(big1, g), tile_rows(big1, g), ACT.Sigmoid).then_inc(gated.sem, 1)
                    act.wait_ge(act_full.sem, act_full.full(b, AU("zz", g)))
                    if g >= 4:
                        act.wait_ge(out_ready.sem, out_ready.at(b, g - 3))
                    nc.scalar.activation(zz[g % 4], A(AU("zz", g))[:, :], ACT.Copy).then_inc(act_done.sem, 1)

        @block.gpsimd
        def _(pool):
            pool.wait_ge(loaded.sem, 64)
            tt = nc.gpsimd.tensor_tensor
            with pool.Fori(0, BATCH) as b:
                steps = [0]

                def link(ins):
                    steps[0] += 1
                    ins.then_inc(pool_step.sem, 1)
                    pool.wait_ge(pool_step.sem, pool_step.at(b, steps[0]))

                def gx(j):
                    pool.wait_ge(x_in[j].sem, x_in[j].at(b, 16))
                    v = big1[:, 2048 * j:2048 * j + 2048].rearrange("p (h w) -> p h w", w=N)
                    link(tt(v, v, bc(mr_bc[:, 0:N], 1, 16), ALU.subtract))
                    tt(v, v, bc(mr_bc[:, N:2 * N], 1, 16), ALU.mult).then_inc(gx_ready.sem, 1)

                pool.wait_ge(gn_ready.sem, gn_ready.at(b, 1))
                for j in range(2):
                    gx(j)
                pool.wait_ge(low_ready.sem, low_ready.at(b, 1))
                for h in range(HEADS):
                    if h >= 4:
                        pool.wait_ge(rh_ready.sem, rh_ready.at(b, h - 3))
                    tt(rt2[h % 4].rearrange("p (c t) -> p c t", t=N), xst.rearrange("p (c t) -> p c t", t=N),
                       bc(mit[:, :].rearrange("p (c h) -> p c h", h=HEADS)[:, :, h], 2, N), ALU.mult)\
                        .then_inc(rh_t2.sem, 1)
                for h in range(HEADS):
                    pool.wait_ge(cri_in[h].sem, cri_in[h].at(b, 16))
                    if h >= 5:
                        pool.wait_ge(wh_ready.sem, wh_ready.at(b, h - 4))
                    elif h == 0:
                        pool.wait_ge(rh_ready.sem, rh_ready.at(b, HEADS))
                    tt(t2[h % 5].rearrange("p (y r k) -> p y r k", r=2, k=KX), xs.rearrange("p (y r k) -> p y r k", r=2, k=KX),
                       bc(cri[h][:, 512:1024].rearrange("p (y k) -> p y k", k=KX), 2, 2), ALU.mult)\
                        .then_inc(wh_t2.sem, 1)
                for j in range(2, 8):
                    gx(j)

                def mix(layer):
                    w = W("mix")[:, 256 * layer + 128:256 * layer + 256].rearrange("p (c i o) -> p c i o", c=CH, i=4)
                    src = hc.rearrange("p (c g i) -> p c g i", c=CH, i=4)
                    pool.wait_ge(vec_done.sem, vec_done.emptied(b, VU("hc", 1) if layer else VU("rows", 1)))
                    for i in range(1, 4):
                        tt(imag[i].rearrange("p (c g o) -> p c g o", c=CH, o=4), bc(src[:, :, :, i], 3, 4), bc(w[:, :, i, :], 2, 32),
                           ALU.mult).then_inc(mixed_pool.sem, 1)

                mix(0)
                mix(1)
                for g in range(TILES):
                    if g % 3 < 2:
                        at = slice(TILE * g, TILE * g + TILE)
                        pool.wait_ge(x2_half.sem, x2_half.at(b, g + 1))
                        pool.wait_ge(scaled.sem, scaled.at(b, g + 1 - added_by_dve(g)))
                        tt(big2[:, at], big2[:, at], big1[:, at], ALU.add).then_inc(x2_pool.sem, 1)
                for g in range(LEAD):
                    pool.wait_ge(act_done.sem, act_done.emptied(b, AU("lead", g)))
                    rows4 = tile_rows(big1, g).rearrange("p e (r w) -> p e r w", w=N)
                    tt(rows4, rows4, bc(bc(bgs[:, :], 1, 2), 1, 2), ALU.add).then_inc(biased.sem, 1)
                for g in range(TILES):
                    pool.wait_ge(weighed.sem, weighed.at(b, g + 1))
                    dst = tile_rows(big2, g)
                    tt(dst, dst, zz[g % 4].rearrange("p (e n) -> p e n", e=2), ALU.add).then_inc(out_ready.sem, 1)
                assert steps[0] == POOL_STEPS, ("POOL_STEPS", steps[0])

        @block.vector
        def _(dve):
            v = nc.vector
            tt, ts, stt, red = v.tensor_tensor, v.tensor_scalar, v.scalar_tensor_tensor, v.tensor_reduce
            count = [0]

            def step(ins):
                count[0] += 1
                ins.then_inc(set_step.sem, 1)
                dve.wait_ge(set_step.sem, count[0])

            for i in range(4):
                v.memset(gs[:, 112 + i:113 + i], 0.0).then_inc(act_done.sem, 1)
                v.memset(gs[:, 116 + i:117 + i], 0.0).then_inc(vec_done.sem, 1)
            v.memset(gs[:, 110:111], 0.0).then_inc(stored.sem, 16)
            v.memset(gs[:, 111:112], 0.0).then_inc(stored_high.sem, 16)
            v.memset(sm[:, 63:64], EPS)
            v.memset(dmat[:, :], 0.0)
            dve.wait_ge(loaded.sem, 64)
            step(tt(sm[:, 9:10], W("lnb"), W("lng"), ALU.subtract))
            ts(m1s[:, :], ones, sm[:, 9:10], None, ALU.mult).then_inc(set_lnb.sem, 1)
            kq = W("kq").rearrange("p (f g n) -> p f g n", f=4, g=2)
            for f, op in ((0, ALU.add), (2, ALU.subtract)):
                for g in range(2):
                    step(tt(kq[0:64, f, g, 0:8], kq[0:64, f, g, 0:8], kq[0:64, f + 1, g, 0:8], op))
                    step(ts(kq[0:64, f, g, 0:8], kq[0:64, f, g, 0:8], 0.5, None, ALU.mult))
            for layer in range(2):
                for f, op in ((0, ALU.add), (1, ALU.subtract)):
                    at = COL["mix"].start + 256 * layer + 128 * f
                    rv = COL["mixrev"].start + 32 * layer + 16 * f
                    step(tt(col[0:64, at:at + 16], col[0:64, at:at + 16], col[0:64, rv:rv + 16], op))
                    step(ts(col[0:64, at:at + 16], col[0:64, at:at + 16], 0.5, None, ALU.mult))
            swk, swq, swv = (B("sw")[:, 8 * i:8 * i + 8] for i in range(3))
            step(tt(B("sb"), B("sb"), B("bias"), ALU.add))
            cbk, cbq, cbv = (B("sb")[:, 8 * i:8 * i + 8] for i in range(3))
            kr, qr, ki, qi = kq[:, 0, 0, :], kq[:, 0, 1, :], kq[:, 2, 0, :], kq[:, 2, 1, :]
            chunks = lambda ap: ap.rearrange("p (c h) -> p c h", h=HEADS)
            step(tt(chunks(kr), chunks(kr), bc(swk, 1, 4), ALU.add))
            step(tt(chunks(qr), chunks(qr), bc(swq, 1, 4), ALU.add))
            step(tt(mrt[:, :], qr, kr, ALU.mult))
            step(tt(mit[:, :], qi, ki, ALU.mult))
            step(tt(mrt[:, :], mrt[:, :], mit[:, :], ALU.add))
            step(tt(wsum[:, :], swq, swk, ALU.mult))
            step(tt(chunks(mrt[:, :]), chunks(mrt[:, :]), bc(wsum[:, :], 1, 4), ALU.subtract))
            step(tt(mit[:, :], qr, ki, ALU.mult))
            step(tt(gs[:, 0:32], qi, kr, ALU.mult))
            step(tt(mit[:, :], mit[:, :], gs[:, 0:32], ALU.subtract))
            step(ts(mrt[:, :], mrt[:, :], K("rho"), None, ALU.mult))
            step(ts(mit[:, :], mit[:, :], K("rho"), None, ALU.mult))
            step(tt(mrt[0:1, 0:8], mrt[0:1, 0:8], wsum[0:1, :], ALU.add))
            step(tt(gs[0:1, 32:40], cbk[0:1, :], qr[0:1, 0:8], ALU.mult))
            step(ts(mit[0:1, 0:8], gs[0:1, 32:40], -1.0, None, ALU.mult))
            step(tt(mrt[32:33, 0:8], cbk[32:33, :], cbq[32:33, :], ALU.mult))
            step(tt(mit[32:33, 0:8], cbq[32:33, :], kr[32:33, 0:8], ALU.mult))
            csum = sm[:, 61:62]
            step(tt(ccol[:, :], B("pdc"), B("psw"), ALU.add))
            step(tt(ccol[:, :], ccol[:, :], cbv, ALU.mult))
            step(tt(gs[:, 40:41], B("pbias"), B("psb"), ALU.add))
            step(tt(ccol[:, 0:1], ccol[:, 0:1], gs[:, 40:41], ALU.add))
            step(red(csum, ccol[:, :], AX.X, ALU.add))
            step(stt(csum, csum, DC, ident[:, 0:1], ALU.mult, ALU.mult))
            vsum = sm[:, 0:8]
            step(tt(vsum, B("psw"), swv, ALU.mult))
            step(ts(sm[:, 8:9], B("n1b"), DC, None, ALU.mult))
            step(ts(B("mixsb"), B("mixsb"), DC, None, ALU.mult))
            step(ts(wzs[:, :], W("wz"), W("lng"), None, ALU.mult))
            dve.wait_ge(set_pe.sem, 1)
            step(stt(B("bz"), B("bz"), 4.0, banks_v[3][:, 0:256], ALU.mult, ALU.add))
            for k in range(2):
                at = slice(N * k, N * k + N)
                step(stt(wzs[:, at], B("bz")[:, at], K("pair")[:, k:k + 1], wzs[:, at], ALU.mult, ALU.add))
            f4 = [pj[:, 512 * i:512 * i + 512] for i in range(4)]
            for i, op in enumerate((ALU.add, ALU.subtract, ALU.add, ALU.subtract)):
                step(tt(f4[i][:, 0:KX], f4[i][:, 0:KX], pj[:, 2048 + 32 * i:2080 + 32 * i], op))
                step(ts(f4[i][:, 0:KX], f4[i][:, 0:KX], 0.5, None, ALU.mult))
            swv8, psw8 = pj[:, 2176:2177], pj[:, 2177:2178]
            cr, ci = crt[:, 0:512], crt[:, 512:1024]
            step(ts(vr8, f4[2], swv8, None, ALU.add))
            step(tt(cr, f4[0], vr8, ALU.mult))
            step(tt(tmp8, f4[1], f4[3], ALU.mult))
            step(tt(cr, cr, tmp8, ALU.subtract))
            step(stt(cr, f4[2], psw8, cr, ALU.mult, ALU.add))
            step(tt(ci, f4[0], f4[3], ALU.mult))
            step(tt(tmp8, f4[1], vr8, ALU.mult))
            step(tt(ci, ci, tmp8, ALU.add))
            stt(ci, f4[3], psw8, ci, ALU.mult, ALU.add).then_inc(set_crt.sem, 1)

            with dve.Fori(0, BATCH) as b:
                steps, roots = [0], [0]

                def link(ins):
                    steps[0] += 1
                    ins.then_inc(dve_step.sem, 1)
                    dve.wait_ge(dve_step.sem, dve_step.at(b, steps[0]))

                def link_done(ins, n):
                    ins.then_inc(vec_done.sem, 1)
                    dve.wait_ge(vec_done.sem, vec_done.emptied(b, n))

                def inverse_root(dst, n):
                    roots[0] += 1
                    dve.wait_ge(root_got.sem, root_got.at(b, roots[0]))
                    link(v.reciprocal(dst, root[:, 0:n]))

                def inverse(k):
                    for u in range(4):
                        dve.wait_ge(vec_full.sem, vec_full.full(b, VU(f"inv{k}", u)))
                        v.tensor_copy(inverse_rows(za, 2 * u + 1),
                                           V(VU(f"inv{k}", u))[:, :].rearrange("p (y r h) -> p y r h", y=2, r=2)).then_inc(vec_done.sem, 1)
                    for u in range(4, 8):
                        dve.wait_ge(vec_full.sem, vec_full.full(b, VU(f"inv{k}", u)))
                        q = 2 * (u - 4) + 1
                        v.tensor_copy(zb[:, TILE * q:TILE * q + TILE], V(VU(f"inv{k}", u))[:, :]).then_inc(vec_done.sem, 1)

                dve.wait_ge(stored_high.sem, stored_high.at(b, 16))
                dve.wait_ge(vec_full.sem, vec_full.full(b, VU("s2")))
                v.tensor_copy(s2s, V(VU("s2"))[:, :]).then_inc(vec_done.sem, 1)
                s1, s2 = s12[:, 0:N], s12[:, N:2 * N]
                n = VU("s12t")
                dve.wait_ge(vec_full.sem, vec_full.full(b, n))
                ts(s1, V(n)[:, 0:N], N / L0, None, ALU.mult)
                link_done(v.tensor_copy(s2, V(n)[:, N:2 * N]), n)
                n = VU("sum")
                dve.wait_ge(vec_full.sem, vec_full.full(b, n))
                link_done(red(gs[:, 0:64], V(n)[:, 0:256].rearrange("p (g q) -> p g q", q=4), AX.X, ALU.add), n)
                link(ts(gs[:, 0:64], gs[:, 0:64], 1.0 / (4 * HW), None, ALU.mult))
                link(tt(gs[:, 64:96], gs[:, 0:32], gs[:, 0:32], ALU.mult))
                tt(root[:, 0:32], gs[:, 32:64], gs[:, 64:96], ALU.subtract).then_inc(root_ask.sem, 1)
                mean, rstd = mr_bc[:, 0:N], mr_bc[:, N:2 * N]
                link(v.tensor_copy(mean.rearrange("p (g q) -> p g q", q=4), bc(gs[:, 0:32], 2, 4)))
                inverse_root(gs[:, 64:96], 32)
                v.tensor_copy(rstd.rearrange("p (g q) -> p g q", q=4), bc(gs[:, 64:96], 2, 4)).then_inc(gn_ready.sem, 1)
                dve.wait_ge(gn_ready.sem, gn_ready.at(b, 1))
                link(tt(tq[:, :], mean, ident, ALU.mult))
                link(red(sm[:, 10:11], tq[:, :], AX.X, ALU.add))
                link(tt(tu[:, :], rstd, ident, ALU.mult))
                link(red(sm[:, 11:12], tu[:, :], AX.X, ALU.add))
                link(ts(sm[:, 10:11], sm[:, 10:11], 128.0 / 16, None, ALU.mult))
                link(ts(fws[:, :], K("fw"), sm[:, 11:12], None, ALU.mult))
                dve.wait_ge(act_done.sem, act_done.emptied(b, AU("st1", 31)))
                ts(yw[:, 0, :], yw[:, 0, :], sm[:, 10:11], None, ALU.subtract).then_inc(fw_ready.sem, 1)
                link(stt(tq[:, :], mean, -128.0, s1, ALU.mult, ALU.add))
                link(tt(tu[:, :], s1, tq[:, :], ALU.add))
                link(tt(tu[:, :], tu[:, :], mean, ALU.mult))
                link(tt(tu[:, :], s2, tu[:, :], ALU.subtract))
                link(tt(tu[:, :], tu[:, :], rstd, ALU.mult))
                link(tt(tu[:, :], tu[:, :], rstd, ALU.mult))
                link(tt(tq[:, :], tq[:, :], rstd, ALU.mult))
                link(red(sm[:, 12:13], tq[:, :], AX.X, ALU.add))
                link(red(sm[:, 13:14], tu[:, :], AX.X, ALU.add))
                link(ts(sm[:, 12:14], sm[:, 12:14], 1.0 / HW, None, ALU.mult))
                link(tt(sm[:, 14:15], sm[:, 12:13], sm[:, 12:13], ALU.mult))
                tt(root[:, 0:1], sm[:, 13:14], sm[:, 14:15], ALU.subtract).then_inc(root_ask.sem, 1)
                inverse_root(sm[:, 15:16], 1)
                scol = sm[:, 16:17]
                link(tt(scol, sm[:, 15:16], B("n1w"), ALU.mult))
                ts(diag[:, 0:N], ident, scol, None, ALU.mult).then_inc(diag_ready.sem, 1)
                link(tt(sm[:, 17:18], scol, sm[:, 12:13], ALU.mult))
                link(tt(sm[:, 17:18], B("n1b"), sm[:, 17:18], ALU.subtract))
                link(ts(dmat[:, 0:1], sm[:, 17:18], DC, None, ALU.mult))
                dve.wait_ge(vec_full.sem, vec_full.full(b, VU("sbc")))
                link_done(v.tensor_copy(sbc[:, :], V(VU("sbc"))[:, 0:N]), VU("sbc"))

                for u in range(4):
                    n = VU("xft", u)
                    dve.wait_ge(vec_full.sem, vec_full.full(b, n))
                    if u == 0:
                        v.memset(zb[0:1, 0:N], 0.0).then_inc(xf_ready.sem, 1)
                    v.tensor_copy(features(za, 2 * u + 1), V(n)[:, :].rearrange("p (s j b) -> p s j b", s=4, j=2))\
                        .then_inc(vec_done.sem, 1)
                dve.wait_ge(vec_done.sem, vec_done.emptied(b, VU("xft", 3)))
                dve.wait_ge(act_done.sem, act_done.emptied(b, AU("xft", 3)))
                xf = za[:, :].rearrange("p (a b) -> p a b", b=64)

                def f(a0, a1, b0, b1):
                    return xf[:, a0:a1, b0:b1].rearrange("p a b -> p b a")

                plane = lambda ap: ap.rearrange("p (y r k) -> p y r k", r=2, k=KX)
                m = plane(xcg)
                tt(m[:, 1:16, 0, 1:16], f(1, 16, 1, 16), f(32, 47, 33, 48), ALU.subtract)
                stt(m[:, 1:16, 1, 1:16], f(32, 47, 1, 16), -1.0, f(1, 16, 33, 48), ALU.mult, ALU.subtract)
                tt(m[:, 1:16, 0, 16:32], f(1, 17, 1, 16), f(32, 48, 33, 48), ALU.add)
                tt(m[:, 1:16, 1, 16:32], f(32, 48, 1, 16), f(1, 17, 33, 48), ALU.subtract)
                v.tensor_copy(m[:, 1:16, 0, 0], xf[:, 0, 1:16])
                ts(m[:, 1:16, 1, 0], xf[:, 0, 33:48], -1.0, None, ALU.mult)
                v.tensor_copy(m[:, 0, 0, 0:16], xf[:, 0:16, 0])
                v.tensor_copy(m[:, 0, 0, 16:32], xf[:, 1:17, 0])
                ts(m[:, 0, 1, 1:16], xf[:, 32:47, 0], -1.0, None, ALU.mult)
                v.tensor_copy(m[:, 0, 1, 16:32], xf[:, 32:48, 0])
                link(v.memset(m[:, 0, 1, 0:1], 0.0))
                link(ts(xc, xcg, scol, None, ALU.mult))
                link(v.tensor_copy(xc[:, 0:1], sm[:, 8:9]))
                link(ts(plane(xs)[:, :, 0, :], plane(xc)[:, :, 1, :], -1.0, None, ALU.mult))
                v.tensor_copy(plane(xs)[:, :, 1, :], plane(xc)[:, :, 0, :]).then_inc(xc_ready.sem, 1)
                dve.wait_ge(act_done.sem, act_done.emptied(b, AU("xct", 1)))
                link(v.memset(xct[32:33, 0:N], DC))
                v.memset(xst[0:1, 0:N], -DC).then_inc(low_ready.sem, 1)
                dve.wait_ge(low_ready.sem, low_ready.at(b, 1))
                tiles4 = lambda ap: ap.rearrange("p (c t) -> p c t", t=N)
                for h in range(HEADS):
                    if h % 2:
                        dve.wait_ge(rh_act.sem, rh_act.at(b, h // 2 + 1))
                    else:
                        if h >= 4:
                            dve.wait_ge(rh_used.sem, rh_used.at(b, h - 3))
                        link(tt(tiles4(rh[h % 4]), tiles4(xct), bc(chunks(mrt[:, :])[:, :, h], 2, N), ALU.mult))
                    dve.wait_ge(rh_t2.sem, rh_t2.at(b, h + 1))
                    tt(rh[h % 4], rh[h % 4], rt2[h % 4], ALU.add).then_inc(rh_ready.sem, 1)
                    if h == 2:
                        dve.wait_ge(vec_full.sem, vec_full.full(b, VU("gram")))
                        link_done(ts(gram[:, :], V(VU("gram"))[:, 0:N], scol, None, ALU.mult), VU("gram"))
                        tt(gram[:, :], gram[:, :], sbc[:, :], ALU.mult).then_inc(gram_ready.sem, 1)
                sc8 = tiles4(sc)
                for u in range(2):
                    dve.wait_ge(vec_full.sem, vec_full.full(b, VU("sc", u)))
                    dve.wait_ge(gram_used.sem, gram_used.at(b, u + 1))
                    at = slice(512 * u, 512 * u + 512)
                    link_done(tt(sc[:, at], sc[:, at], V(VU("sc", u))[:, :], ALU.add), VU("sc", u))
                    top = slice(53 + 4 * u, 57 + 4 * u)
                    link(red(sm[:, top], tiles4(sc[:, at]), AX.X, ALU.max))
                    ts(sm[:, top], sm[:, top], -1.0 / 64, None, ALU.mult).then_inc(score_ready.sem, 1)

                def weigh(h):
                    dve.wait_ge(cri_in[h].sem, cri_in[h].at(b, 16))
                    if h >= 4:
                        dve.wait_ge(wh_used.sem, wh_used.at(b, h - 3))
                    tt(plane(wh[h % 4]), plane(xc), bc(cri[h][:, 0:512].rearrange("p (y k) -> p y k", k=KX), 2, 2), ALU.mult)\
                        .then_inc(wh_real.sem, 1)

                def value(h):
                    dve.wait_ge(wh_real.sem, wh_real.at(b, h + 1))
                    dve.wait_ge(wh_t2.sem, wh_t2.at(b, h + 1))
                    tt(wh[h % 4], wh[h % 4], t2[h % 5], ALU.add).then_inc(wh_ready.sem, 1)

                for h in range(2):
                    weigh(h)
                dve.wait_ge(exp_ready.sem, exp_ready.at(b, 1))
                link(v.reciprocal(sm[:, 20:28], sm[:, 20:28]))
                tt(tiles4(prob), sc8, bc(sm[:, 20:28], 2, N), ALU.mult).then_inc(prob_ready.sem, 1)
                for h in range(HEADS):
                    value(h)
                    if h + 2 < HEADS:
                        weigh(h + 2)
                    if h == 3:
                        dve.wait_ge(shares_ready.sem, shares_ready.at(b, 1))
                        link(red(at_[:, :], sc8.rearrange("p h t -> p t h"), AX.X, ALU.add))
                        stt(bt[:, :], at_[:, :], scol, ident, ALU.mult, ALU.add).then_inc(bt_ready.sem, 1)
                for u in range(2):
                    dve.wait_ge(vec_full.sem, vec_full.full(b, VU("u", u)))
                    at = slice(512 - 512 * u + N * u, 1024 - 512 * u)
                    if u:
                        ts(ul[:, 0:N], V(VU("u", u))[:, 0:N], csum, None, ALU.add)
                    link_done(v.tensor_copy(ul[:, at], V(VU("u", u))[:, N * u:]), VU("u", u))
                for u in range(2):
                    dve.wait_ge(vec_full.sem, vec_full.full(b, VU("fy", u)))
                    at = slice(512 * u, 512 * u + 512)
                    tt(fy[:, at], V(VU("fy", u))[:, :], ul[:, at], ALU.add).then_inc(vec_done.sem, 1)
                inverse(0)

                def statistics(src, unit, beside=None):
                    for g in range(TILES):
                        if beside:
                            beside(g)
                        dve.wait_ge(act_done.sem, act_done.emptied(b, unit(g)))
                        ins = v.bn_stats(bn[:, 6 * g:6 * g + 6], src[:, TILE * g:TILE * g + TILE])
                    link(ins)
                    v.memset(gs[:, 100:101], 0.0)
                    link(v.bn_aggr(sm[:, 18:20], bn[:, :]))

                statistics(big1, lambda g: AU("y", g))
                v.tensor_copy(root[:, 0:1], sm[:, 19:20]).then_inc(root_ask.sem, 1)
                inverse_root(sm[:, 28:29], 1)
                ay, by, a0, b0 = sm[:, 28:29], sm[:, 29:30], sm[:, 32:33], sm[:, 33:34]
                link(tt(ay, ay, B("anw"), ALU.mult))
                link(tt(by, ay, sm[:, 18:19], ALU.mult))
                link(tt(by, B("anb"), by, ALU.subtract))
                link(tt(sm[:, 34:35], ay, ay, ALU.mult))
                tt(root[:, 0:1], sm[:, 34:35], sm[:, 19:20], ALU.mult).then_inc(root_ask.sem, 1)
                inverse_root(a0, 1)
                link(tt(a0, a0, ay, ALU.mult))
                link(tt(a0, a0, W("n2w"), ALU.mult))
                ts(diag[:, 0:N], ident, a0, None, ALU.mult).then_inc(rows_ready.sem, 1)
                link(tt(b0, a0, sm[:, 18:19], ALU.mult))
                link(tt(b0, W("n2b"), b0, ALU.subtract))
                link(ts(sm[:, 35:36], b0, DC, None, ALU.mult))
                ts(diag[:, N:2 * N], ident, sm[:, 35:36], None, ALU.mult)
                ts(diag[:, 2 * N:3 * N], W("skip")[:, 0:N], sm[:, 35:36], None, ALU.mult).then_inc(rows_ready.sem, 1)
                ts(m1s[:, :], W("skip")[:, 0:N], a0, None, ALU.mult)
                n = VU("rows")
                dve.wait_ge(vec_full.sem, vec_full.full(b, n))
                link_done(tt(tiles4(hc), tiles4(fy), bc(V(n)[:, 0:N], 1, CH), ALU.mult), n)
                n = VU("rows", 1)
                dve.wait_ge(vec_full.sem, vec_full.full(b, n))
                link(tt(crow[0:1, 0:N], V(n)[0:1, 2 * N:3 * N], vc[0:1, VEC["mixsb"].start:VEC["mixsb"].start + N], ALU.add))
                link_done(tt(hc[0:1, 0:N], hc[0:1, 0:N], V(n)[0:1, N:2 * N], ALU.add), n)

                def mix(layer):
                    src = hc.rearrange("p (c g i) -> p c g i", c=CH, i=4)

                    def product(dst, i, part):
                        at = COL["mix"].start + 256 * layer + 128 * part
                        w = col[:, at:at + 128].rearrange("p (c i o) -> p c i o", c=CH, i=4)
                        return tt(dst.rearrange("p (c g o) -> p c g o", c=CH, o=4), bc(src[:, :, :, i], 3, 4),
                                  bc(w[:, :, i, :], 2, 32), ALU.mult)

                    product(imag[0], 0, 1).then_inc(mixed_dve.sem, 1)
                    for i in range(4):
                        ins = product(real[i], i, 0)
                    link(ins)
                    tt(real[0], real[0], real[1], ALU.add)
                    link(tt(real[2], real[2], real[3], ALU.add))
                    tt(real[0], real[0], real[2], ALU.add).then_inc(mixed_dve.sem, 1)
                    inverse_root(tq[:, :], N)
                    row = crow[0:1, 0:N] if layer == 0 else vc[0:1, VEC["mixsb"].start + N:VEC["mixsb"].stop]
                    for u in range(2):
                        n = VU(f"o{layer}", u)
                        at = slice(512 * u, 512 * u + 512)
                        ins = tt(tiles4(oc[:, at]), tiles4(V(n)[:, :]), bc(tq[:, :], 1, 4), ALU.mult)
                        if u:
                            ins.then_inc(vec_done.sem, 1)
                        else:
                            link_done(ins, n)
                    v.tensor_copy(oc[0:1, 0:N], row).then_inc(vec_done.sem, 1)
                    inverse(layer + 1)

                mix(0)
                for g in range(TILES):
                    dve.wait_ge(vec_full.sem, vec_full.full(b, VU("h1t", g)))
                    v.tensor_copy(h1w[:, TILE * (g % 4):TILE * (g % 4) + TILE], V(VU("h1t", g))[:, :]).then_inc(vec_done.sem, 1)
                for u in range(4):
                    dve.wait_ge(vec_full.sem, vec_full.full(b, VU("zh", u)))
                    v.tensor_copy(zb[:, TILE * (2 * u + 1):TILE * (2 * u + 2)], V(VU("zh", u))[:, :]).then_inc(vec_done.sem, 1)
                for u in range(2):
                    dve.wait_ge(vec_full.sem, vec_full.full(b, VU("hc", u)))
                    link_done(v.tensor_copy(hc[:, 512 * u:512 * u + 512], V(VU("hc", u))[:, :]), VU("hc", u))
                mix(1)

                def skip(g):
                    j, at = g // 4, slice(TILE * g, TILE * g + TILE)
                    if g % 4 == 0:
                        dve.wait_ge(xr_in[j % 2].sem, xr_in[j % 2].at(b, 16 * (j // 2 + 1)))
                    stt(big1[:, at], big1[:, at], ay, xr[j % 2][:, TILE * (g % 4):TILE * (g % 4) + TILE],
                        ALU.mult, ALU.add).then_inc(x2_half.sem, 1)

                statistics(big2, lambda g: AU("p2", g), skip)
                v.tensor_copy(root[:, 0:1], sm[:, 19:20]).then_inc(root_ask.sem, 1)
                a2, b2 = sm[:, 30:31], sm[:, 31:32]
                inverse_root(a2, 1)
                link(tt(a2, a2, W("monw"), ALU.mult))
                link(tt(b2, a2, sm[:, 18:19], ALU.mult))
                link(tt(b2, W("monb"), b2, ALU.subtract))
                tt(b2, b2, by, ALU.add).then_inc(coef2_ready.sem, 1)

                dve.wait_ge(x2_half.sem, x2_half.at(b, TILES))
                dve.wait_ge(coef2_ready.sem, coef2_ready.at(b, 1))
                for g in range(TILES + 5):
                    if g < TILES and g % 3 == 2:
                        at = slice(TILE * g, TILE * g + TILE)
                        link(ts(big2[:, at], big2[:, at], a2, b2, ALU.mult, ALU.add))
                        tt(big2[:, at], big2[:, at], big1[:, at], ALU.add).then_inc(x2_dve.sem, 1)
                    if g >= 5:
                        k = g - 5
                        dve.wait_ge(act_done.sem, act_done.emptied(b, AU("x2t", k)))
                        ins = v.bn_stats(bn[:, 6 * k:6 * k + 6], big1[:, TILE * k:TILE * k + TILE])
                link(ins)
                v.memset(gs[:, 100:101], 0.0)
                link(v.bn_aggr(sm[:, 40:42], bn[:, :]))
                link(tt(sm[:, 42:43], sm[:, 40:41], sm[:, 40:41], ALU.mult))
                tt(sm[:, 41:42], sm[:, 41:42], sm[:, 42:43], ALU.add).then_inc(gn2_ready.sem, 1)
                n = VU("gn2")
                dve.wait_ge(vec_full.sem, vec_full.full(b, n))
                link_done(v.tensor_copy(sm[:, 44:46], V(n)[:, 0:2]), n)
                link(tt(sm[:, 46:47], sm[:, 44:45], sm[:, 44:45], ALU.mult))
                tt(root[:, 0:1], sm[:, 45:46], sm[:, 46:47], ALU.subtract).then_inc(root_ask.sem, 1)
                inverse_root(sm[:, 47:48], 1)
                link(ts(wabs[:, :], W("wab"), sm[:, 47:48], None, ALU.mult))
                ts(sm[:, 48:49], sm[:, 44:45], -1.0, None, ALU.mult).then_inc(w2_ready.sem, 1)
                dve.wait_ge(w2_ready.sem, w2_ready.at(b, 1))
                ts(wgs[:, :], W("wg"), sm[:, 47:48], None, ALU.mult)
                ts(tq[:, :], ones, sm[:, 48:49], None, ALU.mult).then_inc(w2_ready.sem, 1)
                n = VU("bias")
                dve.wait_ge(vec_full.sem, vec_full.full(b, n))
                link_done(tt(sm[:, 51:53], V(n)[:, 0:2], W("bab"), ALU.add), n)
                n = VU("bias", 1)
                dve.wait_ge(vec_full.sem, vec_full.full(b, n))
                link_done(tt(bgs[:, :], V(n)[:, 0:N], B("bg"), ALU.add), n)
                for k in range(8 + 2):
                    if k < 8:
                        n = aby_unit(k)
                        dve.wait_ge(vec_full.sem, vec_full.full(b, n))
                        dve.wait_ge(act_done.sem, act_done.emptied(b, AU("abx", k)))
                        if k >= 2:
                            dve.wait_ge(vec_full.sem, vec_full.full(b, abt_unit(k - 2)))
                        stt(prods[k % 2], V(n)[:, :], sm[:, 52:53], firsts[k % 2], ALU.add, ALU.mult)\
                            .then_inc(vec_done.sem, 1)
                    if k >= 2:
                        n = abt_unit(k - 2)
                        dve.wait_ge(vec_full.sem, vec_full.full(b, n))
                        dst = abt[:, :, 16 * (k - 2):16 * (k - 2) + 16].rearrange("p n (j l) -> p l j n", l=4)
                        v.tensor_copy(dst, V(n)[:, :].rearrange("p (l j n) -> p l j n", l=4, j=4)).then_inc(vec_done.sem, 1)
                for u in range(4):
                    n = VU("z", u)
                    dve.wait_ge(vec_full.sem, vec_full.full(b, n))
                    link_done(v.tensor_copy(z[:, 4 * u:4 * u + 4, :], V(n)[:, :].rearrange("p (c j) -> p c j", j=N)), n)
                link(red(tq[:, :], z.rearrange("p c j -> p j c"), AX.X, ALU.add))
                link(ts(tq[:, :], tq[:, :], 1.0 / C, None, ALU.mult))
                link(tt(z, z, bc(tq[:, :], 1, C), ALU.subtract))
                zsq = z2.rearrange("p (c j) -> p c j", j=N)
                link(tt(zsq, z, z, ALU.mult))
                link(red(tu[:, :], zsq.rearrange("p c j -> p j c"), AX.X, ALU.add))
                ts(root[:, :], tu[:, :], 1.0 / C, None, ALU.mult).then_inc(root_ask.sem, 1)
                inverse_root(tq[:, :], N)
                tt(z2.rearrange("p (j c) -> p c j", c=C), z, bc(tq[:, :], 1, C), ALU.mult).then_inc(zn_ready.sem, 1)
                for k in range(TILES):
                    if k % 2 == 0 and k // 2 < TILES - LEAD:
                        n = VU("gate", k // 2)
                        dve.wait_ge(vec_full.sem, vec_full.full(b, n))
                        tt(tile_rows(big1, k // 2 + LEAD).rearrange("p e (r w) -> p e r w", w=N),
                           V(n)[:, :].rearrange("p (e r w) -> p e r w", e=2, w=N), bc(bc(bgs[:, :], 1, 2), 1, 2), ALU.add)\
                            .then_inc(vec_done.sem, 1)
                    dve.wait_ge(gated.sem, gated.at(b, k + 1))
                    dve.wait_ge(act_done.sem, act_done.emptied(b, AU("zz", k)))
                    tile = zz[k % 4].rearrange("p (e n) -> p e n", e=2)
                    tt(tile, tile, tile_rows(big1, k), ALU.mult).then_inc(weighed.sem, 1)
                assert steps[0] == DVE_STEPS, ("DVE_STEPS", steps[0])


def constants():
    n, k31, ky = np.arange(N), np.arange(1, 32), np.arange(KY)

    def cos(k):
        return np.cos(2 * np.pi * (np.outer(n, np.atleast_1d(k)) % N) / N)

    def sin(k):
        return np.sin(2 * np.pi * (np.outer(n, np.atleast_1d(k)) % N) / N)

    lx = np.where(KX_ORDER == 0, L0, L1)
    ly = np.where(ky == 0, L0, L1)
    t = {}
    t["fh"] = np.concatenate([L0 * cos(0), L1 * cos(k31), L1 * sin(k31), L0 * cos(32), L0 * sin(32)], 1) / N
    t["fw"] = np.concatenate([L0 * cos(0), L1 * cos(k31), L0 * cos(32), L1 * sin(k31),
                              0 * cos(0), L1 * sin(k31), L0 * sin(32), -L1 * cos(k31)], 1) / N
    c, s = cos(KX_ORDER), sin(KX_ORDER)
    step = np.stack([np.stack([c.T, s.T], 1), np.stack([-s.T, c.T], 1)]) / lx[None, :, None, None]
    inv1 = np.zeros((2, 2, 2, KX, 2, 2, N))
    for y in range(2):
        inv1[:, y, :, :, y] = step
    inv1[0, 0, :, KX - 1, 0] *= 2
    t["inv1"] = inv1.reshape(2, N, 512).transpose(1, 0, 2).reshape(N, 1024)
    weight = (np.where(ky == 0, 1.0, 2.0) / ly)[:, None]
    inv2 = np.zeros((4, 2, KY, 4, N))
    for j in range(4):
        inv2[j, 0, :, j], inv2[j, 1, :, j] = cos(ky).T * weight, -sin(ky).T * weight
    t["inv2"] = inv2.reshape(N, 512)
    t["f2w"] = np.stack([cos(ky) * ly, -sin(ky) * ly], 2).reshape(N, 32) / N
    f2h = np.zeros((N, 2, 2, 2, 2, KX))
    for y in range(2):
        f2h[:, y, 0, y, 0], f2h[:, y, 0, y, 1] = c * lx, -s * lx
        f2h[:, y, 1, y, 0], f2h[:, y, 1, y, 1] = s * lx, c * lx
    t["f2h"] = f2h.reshape(N, 512) / N
    swap = np.zeros((2, 2, KX, 2, 2, KX))
    for y in range(2):
        swap[y, 1, :, y, 0], swap[y, 0, :, y, 1] = -np.eye(KX), np.eye(KX)
    t["swap"] = swap.reshape(N, N)
    varw = np.zeros((2, 2, 2, KX))
    varw[:] = 2 / (lx * L1) ** 2
    varw[0, 0] = 1 / (lx * L0) ** 2
    varw[0, 0, :, KX - 1] *= 2
    varw[0, 0, :, 0] = 0
    t["varw"] = np.repeat(varw.reshape(2, N).T, N, 1)
    t["ident"], t["ones"] = np.eye(N), np.ones((N, N))
    t["quad"] = np.kron(np.eye(N // 4), np.full((4, 4), 0.25))
    t["rho"] = np.tile(np.where(KX_ORDER == 0, 1.0, 0.5), 4)[:, None]
    t["pair"] = np.kron(np.tile(np.eye(2), (4, 1)), np.ones((C, 1))) / (4 * C)
    t["onecol"] = np.zeros((N, 63))
    t["onecol"][:, 31] = 1
    return np.concatenate([t[name].reshape(N, size) for name, size in CONST_PARTS], 1).astype(np.float32)


def token_places():
    place = np.zeros((N, 4, N), np.float32)
    for token in range(N):
        place[32 * (token % 16 // 4) + token // 16, token % 4, token] = 1
    return place.reshape(N, 4 * N)


def on_modes(w):
    m1, m2 = w.shape[-2:]
    out = np.zeros((2,) + w.shape[:-2] + (KY, KX), w.dtype)
    for i, k in enumerate(KX_ORDER):
        for r, q in enumerate((k, -k)):
            if -(m1 // 2) <= q < m1 // 2:
                out[r][..., :m2, i] = w[..., q % m1, :]
    return out


def chunked(w):
    v = np.stack([w, w], -2)
    return np.moveaxis(v.reshape(w.shape[:-2] + (CH, N)), (-1, -2), (0, 1))


def lay_out(i):
    l0 = {k[8:]: np.asarray(v) for k, v in i.items() if k.startswith("L0_conv_")}
    l1 = {k[8:]: np.asarray(v) for k, v in i.items() if k.startswith("L1_conv_")}
    f = np.float32
    cols = np.zeros((N, COL_N), f)

    def put(name, a):
        cols[:, COL[name]] = a.reshape(N, -1)

    for name, a in (("n2w", "norm2_w"), ("n2b", "norm2_b"), ("monw", "mon_w"), ("monb", "mon_b")):
        put(name, np.tile(l0[a], N // 4))
    put("lng", np.tile(l1["ln2_g"], N // C))
    put("lnb", np.tile(l1["ln2_b"], N // C))
    kq = [chunked(on_modes(l0[a][0:2, 0])[r])[:, 0:4] for a in ("kqv_wr", "kqv_wi") for r in range(2)]
    put("kq", np.stack(kq, 1).transpose(0, 1, 3, 2, 4))
    mix = np.stack([on_modes(l0["mix_wr"]), on_modes(l0["mix_wi"])])
    mixed = chunked(mix)
    put("mix", mixed[:, :, :, 0].transpose(0, 3, 2, 1, 4, 5))
    put("mixrev", mixed[:, 0, :, 1].transpose(0, 2, 1, 3, 4))
    skip, wz = np.zeros((N, 2, N), f), np.zeros((N, 2, N), f)
    for g in range(N // 4):
        for layer in range(2):
            skip[4 * g:4 * g + 4, layer, 4 * g:4 * g + 4] = l0["mix_sw"][layer].T
    for j in range(8):
        wz[C * j:C * j + C, j % 2] = l1["Wz"]
    put("skip", skip)
    put("wz", wz)
    put("wg", l1["Wg"])
    put("wab", np.concatenate([l1[k] for k in 4 * ("Wa1", "Wb1") + 4 * ("Wa2", "Wb2")], 1))
    put("bab", np.stack([np.concatenate([l1[k] for k in 4 * pair]) for pair in (("ba1", "bb1"), ("ba2", "bb2"))], 1))
    vec = {"sw": l0["kqv_sw"], "sb": l0["kqv_sb"], "bias": l0["kqv_bias"], "psw": l0["p_sw"], "n1w": l0["norm1_w"],
           "n1b": l0["norm1_b"], "pbias": l0["p_bias"], "psb": l0["p_sb"], "anw": l0["attn_norm_w"],
           "anb": l0["attn_norm_b"], "pdc": l0["p_wr"][:, 0, 0, 0], "mixsb": np.tile(l0["mix_sb"], (1, N // 4)),
           "bg": l1["bg"], "bz": np.tile(l1["bz"], 2)}
    vec = np.concatenate([vec[name].reshape(1, n) for name, n in VEC_PARTS], 1)
    modes = [on_modes(a) for a in (l0["p_wr"][:, 0], l0["p_wi"][:, 0], l0["kqv_wr"][2, 0], l0["kqv_wi"][2, 0])]
    proj = np.concatenate([m[0].reshape(HEADS, 512) for m in modes] + [m[1][:, 0] for m in modes]
                          + [l0["kqv_sw"][2].reshape(HEADS, 1), l0["p_sw"].reshape(HEADS, 1)], 1)
    return cols, vec, proj


def kernel(**inputs):
    import concourse.bacc as bacc
    from concourse.bass_utils import run_bass_kernel_spmd as run

    nc = bacc.Bacc("TRN2", target_bir_lowering=False, num_devices=1)
    cols, vec, proj = lay_out(inputs)
    arrays = {"x": np.ascontiguousarray(inputs["x"]), "const": constants(), "places": token_places(), "cols": cols, "vec": vec, "proj": proj}
    aps = [nc.dram_tensor(k, a.shape, F32, kind="ExternalInput").ap() for k, a in arrays.items()]
    tables = nc.dram_tensor("head_tables", (HEADS, 1024), F32, kind="Internal").ap()
    out = nc.dram_tensor("out", (BATCH, N, N, N), F32, kind="ExternalOutput").ap()
    build(nc, *aps, tables, out)
    return run(nc, [arrays], core_ids=[0]).results[0]["out"]
```
